# Optimizing a Trainium2 kernel written in Bass

```python
import numpy as np
import jax
import jax.numpy as jnp

def _softmax(x, axis=-1):
    return jax.nn.softmax(x, axis=axis)

def _gelu(x):
    return jax.nn.gelu(x, approximate=True)

def _silu(x):
    return jax.nn.silu(x)

def _sigmoid(x):
    return jax.nn.sigmoid(x)

def _layernorm(x, axis=-1, eps=1e-05):
    m = jnp.mean(x, axis=axis, keepdims=True)
    v = jnp.var(x, axis=axis, keepdims=True)
    return (x - m) / jnp.sqrt(v + eps)

def _scatter_add(tgt, idx, src, axis=0):
    return tgt.at[idx].add(src)

def _segment_sum(src, seg, n):
    return jax.ops.segment_sum(src, seg, n)
kernel_name = 'mk_audio_tower_d2_tok_audfeat256_r4_43ecfc'

def setup_inputs(seed: int=0):
    np.random.seed(seed)
    _w = jnp.asarray

    def _rec_inputs():
        import jax
        import jax.numpy as jnp
        _rk = jax.random.key(seed)
        x = -0.000154596 + 0.999967 * jax.random.normal(jax.random.fold_in(_rk, 1), (32, 750, 64), jnp.float32)
        return x
    x = _rec_inputs()

    def _L0_tok_setup():
        import jax, jax.numpy as jnp
        import numpy as np
        RATIO = 0.5
        key = jax.random.key(seed)
        k1, k2 = jax.random.split(key)
        B, N, F = (32, 4096, 64)
        inputs = jax.random.normal(k1, (B, N, F), dtype=jnp.float32)
        score_proj = jax.random.normal(k2, (F, 1), dtype=jnp.float32) * (1.0 / np.sqrt(F))
        return {'inputs': inputs, 'score_proj': score_proj}
    _L0_tok_all = _L0_tok_setup()
    _L0_tok_in = {k: v for k, v in _L0_tok_all.items() if k in ('score_proj',)}
    del _L0_tok_all

    def _L0_attn_setup():
        import jax, jax.numpy as jnp
        import numpy as np
        NUM_HEADS = 4
        LN_EPS = 1e-05

        def positional_encoding(length, d_model):
            pos = jnp.arange(length, dtype=jnp.float32)[:, None]
            div = jnp.exp(jnp.arange(0, d_model, 2, dtype=jnp.float32) * (-np.log(10000.0) / d_model))
            pe = jnp.zeros((length, d_model), dtype=jnp.float32)
            pe = pe.at[:, 0::2].set(jnp.sin(pos * div))
            pe = pe.at[:, 1::2].set(jnp.cos(pos * div))
            return pe

        def rel_shift(pos_score):
            B, H, S, _ = pos_score.shape
            padded = jnp.pad(pos_score, ((0, 0), (0, 0), (0, 0), (1, 0)))
            padded = padded.reshape(B, H, S + 1, S)
            return padded[:, :, 1:].reshape(B, H, S, S)
        key = jax.random.key(seed)
        ks = jax.random.split(key, 8)
        B, S, D, H = (8, 512, 64, NUM_HEADS)
        dh = D // H
        s = 0.02
        return {'inputs': jax.random.normal(ks[0], (B, S, D), dtype=jnp.float32), 'ln_gamma': jnp.ones((D,), jnp.float32), 'ln_beta': jnp.zeros((D,), jnp.float32), 'Wq': jax.random.normal(ks[1], (D, D), jnp.float32) * s, 'bq': jnp.zeros((D,), jnp.float32), 'Wk': jax.random.normal(ks[2], (D, D), jnp.float32) * s, 'bk': jnp.zeros((D,), jnp.float32), 'Wv': jax.random.normal(ks[3], (D, D), jnp.float32) * s, 'bv': jnp.zeros((D,), jnp.float32), 'Wpos': jax.random.normal(ks[4], (D, D), jnp.float32) * s, 'u_bias': jax.random.normal(ks[5], (H, dh), jnp.float32) * s, 'v_bias': jax.random.normal(ks[6], (H, dh), jnp.float32) * s, 'Wout': jax.random.normal(ks[7], (D, D), jnp.float32) * s, 'bout': jnp.zeros((D,), jnp.float32)}
    _L0_attn_all = _L0_attn_setup()
    _L0_attn_in = {k: v for k, v in _L0_attn_all.items() if k in ('ln_gamma', 'ln_beta', 'Wq', 'bq', 'Wk', 'bk', 'Wv', 'bv', 'Wpos', 'u_bias', 'v_bias', 'Wout', 'bout')}
    del _L0_attn_all

    def _L0_ffn_setup():
        import jax, jax.numpy as jnp
        import numpy as np
        B, T, D, H, E = (16, 1024, 64, 128, 8)
        key = jax.random.key(seed)
        ks = jax.random.split(key, 5)
        x = jax.random.normal(ks[0], (B, T, D), dtype=jnp.float32)
        gate_w = jax.random.normal(ks[1], (D, E), dtype=jnp.float32) * 0.02
        gate_b = jnp.zeros((E,), dtype=jnp.float32)
        W1 = jax.random.normal(ks[2], (E, D, H), dtype=jnp.float32) * 0.02
        b1 = jnp.zeros((E, H), dtype=jnp.float32)
        W2 = jax.random.normal(ks[3], (E, H, D), dtype=jnp.float32) * 0.02
        b2 = jnp.zeros((E, D), dtype=jnp.float32)
        return {'x': x, 'gate_w': gate_w, 'gate_b': gate_b, 'W1': W1, 'b1': b1, 'W2': W2, 'b2': b2}
    _L0_ffn_all = _L0_ffn_setup()
    _L0_ffn_in = {k: v for k, v in _L0_ffn_all.items() if k in ('gate_w', 'gate_b', 'W1', 'b1', 'W2', 'b2')}
    del _L0_ffn_all

    def _L1_attn_setup():
        import jax, jax.numpy as jnp
        import numpy as np
        B, T, C, H, G = (8, 2048, 64, 8, 64)
        D = C // H
        key = jax.random.key(seed)
        ks = jax.random.split(key, 16)
        s = 0.02
        return {'x_q': jax.random.normal(ks[0], (B, T, C), jnp.float32), 'x_r': jax.random.normal(ks[1], (B, T, C), jnp.float32), 'y': jax.random.normal(ks[2], (B, T, C), jnp.float32), 'W_in': jax.random.normal(ks[3], (C, C), jnp.float32) * s, 'b_in': jnp.zeros((C,), jnp.float32), 'W_slice': jax.random.normal(ks[4], (D, G), jnp.float32) * s, 'b_slice': jnp.zeros((G,), jnp.float32), 'temperature': jnp.ones((1, H, 1, 1), jnp.float32) / np.float32(np.sqrt(D)), 'W_q': jax.random.normal(ks[5], (D, D), jnp.float32) * s, 'b_q': jnp.zeros((D,), jnp.float32), 'W_k': jax.random.normal(ks[6], (D, D), jnp.float32) * s, 'b_k': jnp.zeros((D,), jnp.float32), 'W_v': jax.random.normal(ks[7], (D, D), jnp.float32) * s, 'b_v': jnp.zeros((D,), jnp.float32), 'W_out': jax.random.normal(ks[8], (C, C), jnp.float32) * s, 'b_out': jnp.zeros((C,), jnp.float32)}
    _L1_attn_all = _L1_attn_setup()
    _L1_attn_in = {k: v for k, v in _L1_attn_all.items() if k in ('x_r', 'y', 'W_in', 'b_in', 'W_slice', 'b_slice', 'temperature', 'W_q', 'b_q', 'W_k', 'b_k', 'W_v', 'b_v', 'W_out', 'b_out')}
    del _L1_attn_all

    def _L1_ffn_setup():
        import jax, jax.numpy as jnp
        import numpy as np
        B, S, H, NH, NE = (4, 256, 64, 4, 4)
        D = H // NH
        EPS = 1e-08

        def layernorm(x, g, b):
            m = jnp.mean(x, axis=-1, keepdims=True)
            v = jnp.mean((x - m) ** 2, axis=-1, keepdims=True)
            return (x - m) / jnp.sqrt(v + EPS) * g + b
        key = jax.random.key(seed)
        ks = jax.random.split(key, 18)
        sc = 0.05
        return {'x': jax.random.normal(ks[0], (B, S, H), jnp.float32), 'hl_w': jax.random.normal(ks[1], (NH, D, H), jnp.float32) * sc, 'hl_b': jax.random.normal(ks[2], (NH, D), jnp.float32) * sc, 'wq': jax.random.normal(ks[3], (NH, NE, D, D), jnp.float32) * sc, 'wk': jax.random.normal(ks[4], (NH, D, D), jnp.float32) * sc, 'wv': jax.random.normal(ks[5], (NH, D, D), jnp.float32) * sc, 'gate_w': jax.random.normal(ks[6], (NH, NE, NE * D), jnp.float32) * sc, 'gate_b': jax.random.normal(ks[7], (NH, NE), jnp.float32) * sc, 'ln_g': jnp.ones((D,), jnp.float32), 'ln_b': jnp.zeros((D,), jnp.float32), 'fc1_w': jax.random.normal(ks[8], (D, D), jnp.float32) * sc, 'fc1_b': jax.random.normal(ks[9], (D,), jnp.float32) * sc, 'fc2_w': jax.random.normal(ks[10], (D, D), jnp.float32) * sc, 'fc2_b': jax.random.normal(ks[11], (D,), jnp.float32) * sc, 'fnorm_g': jnp.ones((D,), jnp.float32), 'fnorm_b': jnp.zeros((D,), jnp.float32), 'fgate_w': jax.random.normal(ks[12], (NH, H), jnp.float32) * sc}
    _L1_ffn_all = _L1_ffn_setup()
    _L1_ffn_in = {k: v for k, v in _L1_ffn_all.items() if k in ('hl_w', 'hl_b', 'wq', 'wk', 'wv', 'gate_w', 'gate_b', 'ln_g', 'ln_b', 'fc1_w', 'fc1_b', 'fc2_w', 'fc2_b', 'fnorm_g', 'fnorm_b', 'fgate_w')}
    del _L1_ffn_all
    return {'x': x, 'L0_tok_score_proj': _L0_tok_in['score_proj'], 'L0_attn_ln_gamma': _L0_attn_in['ln_gamma'], 'L0_attn_ln_beta': _L0_attn_in['ln_beta'], 'L0_attn_Wq': _L0_attn_in['Wq'], 'L0_attn_bq': _L0_attn_in['bq'], 'L0_attn_Wk': _L0_attn_in['Wk'], 'L0_attn_bk': _L0_attn_in['bk'], 'L0_attn_Wv': _L0_attn_in['Wv'], 'L0_attn_bv': _L0_attn_in['bv'], 'L0_attn_Wpos': _L0_attn_in['Wpos'], 'L0_attn_u_bias': _L0_attn_in['u_bias'], 'L0_attn_v_bias': _L0_attn_in['v_bias'], 'L0_attn_Wout': _L0_attn_in['Wout'], 'L0_attn_bout': _L0_attn_in['bout'], 'L0_ffn_gate_w': _L0_ffn_in['gate_w'], 'L0_ffn_gate_b': _L0_ffn_in['gate_b'], 'L0_ffn_W1': _L0_ffn_in['W1'], 'L0_ffn_b1': _L0_ffn_in['b1'], 'L0_ffn_W2': _L0_ffn_in['W2'], 'L0_ffn_b2': _L0_ffn_in['b2'], 'L1_attn_x_r': _L1_attn_in['x_r'], 'L1_attn_y': _L1_attn_in['y'], 'L1_attn_W_in': _L1_attn_in['W_in'], 'L1_attn_b_in': _L1_attn_in['b_in'], 'L1_attn_W_slice': _L1_attn_in['W_slice'], 'L1_attn_b_slice': _L1_attn_in['b_slice'], 'L1_attn_temperature': _L1_attn_in['temperature'], 'L1_attn_W_q': _L1_attn_in['W_q'], 'L1_attn_b_q': _L1_attn_in['b_q'], 'L1_attn_W_k': _L1_attn_in['W_k'], 'L1_attn_b_k': _L1_attn_in['b_k'], 'L1_attn_W_v': _L1_attn_in['W_v'], 'L1_attn_b_v': _L1_attn_in['b_v'], 'L1_attn_W_out': _L1_attn_in['W_out'], 'L1_attn_b_out': _L1_attn_in['b_out'], 'L1_ffn_hl_w': _L1_ffn_in['hl_w'], 'L1_ffn_hl_b': _L1_ffn_in['hl_b'], 'L1_ffn_wq': _L1_ffn_in['wq'], 'L1_ffn_wk': _L1_ffn_in['wk'], 'L1_ffn_wv': _L1_ffn_in['wv'], 'L1_ffn_gate_w': _L1_ffn_in['gate_w'], 'L1_ffn_gate_b': _L1_ffn_in['gate_b'], 'L1_ffn_ln_g': _L1_ffn_in['ln_g'], 'L1_ffn_ln_b': _L1_ffn_in['ln_b'], 'L1_ffn_fc1_w': _L1_ffn_in['fc1_w'], 'L1_ffn_fc1_b': _L1_ffn_in['fc1_b'], 'L1_ffn_fc2_w': _L1_ffn_in['fc2_w'], 'L1_ffn_fc2_b': _L1_ffn_in['fc2_b'], 'L1_ffn_fnorm_g': _L1_ffn_in['fnorm_g'], 'L1_ffn_fnorm_b': _L1_ffn_in['fnorm_b'], 'L1_ffn_fgate_w': _L1_ffn_in['fgate_w']}

def reference(x, L0_tok_score_proj, L0_attn_ln_gamma, L0_attn_ln_beta, L0_attn_Wq, L0_attn_bq, L0_attn_Wk, L0_attn_bk, L0_attn_Wv, L0_attn_bv, L0_attn_Wpos, L0_attn_u_bias, L0_attn_v_bias, L0_attn_Wout, L0_attn_bout, L0_ffn_gate_w, L0_ffn_gate_b, L0_ffn_W1, L0_ffn_b1, L0_ffn_W2, L0_ffn_b2, L1_attn_x_r, L1_attn_y, L1_attn_W_in, L1_attn_b_in, L1_attn_W_slice, L1_attn_b_slice, L1_attn_temperature, L1_attn_W_q, L1_attn_b_q, L1_attn_W_k, L1_attn_b_k, L1_attn_W_v, L1_attn_b_v, L1_attn_W_out, L1_attn_b_out, L1_ffn_hl_w, L1_ffn_hl_b, L1_ffn_wq, L1_ffn_wk, L1_ffn_wv, L1_ffn_gate_w, L1_ffn_gate_b, L1_ffn_ln_g, L1_ffn_ln_b, L1_ffn_fc1_w, L1_ffn_fc1_b, L1_ffn_fc2_w, L1_ffn_fc2_b, L1_ffn_fnorm_g, L1_ffn_fnorm_b, L1_ffn_fgate_w):
    import jax
    import jax.numpy as jnp

    def _L0_tok_ref(inputs, score_proj):
        import jax, jax.numpy as jnp
        import numpy as np
        RATIO = 0.5
        N = inputs.shape[1]
        k = max(int(N * RATIO), 1)
        scores = jnp.einsum('bnf,fo->bn', inputs, score_proj)
        _, top_idx = jax.lax.top_k(scores, k)
        sel_feat = jnp.take_along_axis(inputs, top_idx[:, :, None], axis=1)
        sel_scores = jnp.take_along_axis(scores, top_idx, axis=1)
        gate = jax.nn.sigmoid(sel_scores)[:, :, None]
        return sel_feat * gate

    def _L0_attn_ref(inputs, ln_gamma, ln_beta, Wq, bq, Wk, bk, Wv, bv, Wpos, u_bias, v_bias, Wout, bout):
        import jax, jax.numpy as jnp
        import numpy as np
        NUM_HEADS = 4
        LN_EPS = 1e-05

        def positional_encoding(length, d_model):
            pos = jnp.arange(length, dtype=jnp.float32)[:, None]
            div = jnp.exp(jnp.arange(0, d_model, 2, dtype=jnp.float32) * (-np.log(10000.0) / d_model))
            pe = jnp.zeros((length, d_model), dtype=jnp.float32)
            pe = pe.at[:, 0::2].set(jnp.sin(pos * div))
            pe = pe.at[:, 1::2].set(jnp.cos(pos * div))
            return pe

        def rel_shift(pos_score):
            B, H, S, _ = pos_score.shape
            padded = jnp.pad(pos_score, ((0, 0), (0, 0), (0, 0), (1, 0)))
            padded = padded.reshape(B, H, S + 1, S)
            return padded[:, :, 1:].reshape(B, H, S, S)
        B, S, D = inputs.shape
        H = NUM_HEADS
        dh = D // H
        mu = jnp.mean(inputs, axis=-1, keepdims=True)
        var = jnp.mean(jnp.square(inputs - mu), axis=-1, keepdims=True)
        x = (inputs - mu) / jnp.sqrt(var + LN_EPS) * ln_gamma + ln_beta
        pe = positional_encoding(S, D)
        q = (x @ Wq + bq).reshape(B, S, H, dh)
        k = (x @ Wk + bk).reshape(B, S, H, dh)
        v = (x @ Wv + bv).reshape(B, S, H, dh)
        p = (pe @ Wpos).reshape(S, H, dh)
        content_score = jnp.einsum('bshd,bthd->bhst', q + u_bias, k)
        pos_score = jnp.einsum('bshd,thd->bhst', q + v_bias, p)
        pos_score = rel_shift(pos_score)
        score = (content_score + pos_score) / np.sqrt(D).astype(np.float32)
        attn = jax.nn.softmax(score, axis=-1)
        ctx = jnp.einsum('bhst,bthd->bshd', attn, v).reshape(B, S, D)
        return ctx @ Wout + bout

    def _L0_ffn_ref(x, gate_w, gate_b, W1, b1, W2, b2):
        import jax, jax.numpy as jnp
        import numpy as np
        B, T, D, H, E = (16, 1024, 64, 128, 8)
        Bb, Tt, Dd = x.shape
        Ee = gate_w.shape[1]
        xf = x.reshape(-1, Dd)
        N = xf.shape[0]
        logits = xf @ gate_w + gate_b
        probs = jax.nn.softmax(logits, axis=-1)
        top2_vals, top2_idx = jax.lax.top_k(probs, 2)
        cw = jnp.zeros((N, Ee), dtype=xf.dtype).at[jnp.arange(N)[:, None], top2_idx].add(top2_vals)

        def step(acc, params):
            w1, bb1, w2, bb2, we = params
            h = jax.nn.gelu(xf @ w1 + bb1, approximate=False)
            y = h @ w2 + bb2
            return (acc + we[:, None] * y, None)
        out, _ = jax.lax.scan(step, jnp.zeros_like(xf), (W1, b1, W2, b2, cw.T))
        return out.reshape(Bb, Tt, Dd)

    def _L1_attn_ref(x_q, x_r, y, W_in, b_in, W_slice, b_slice, temperature, W_q, b_q, W_k, b_k, W_v, b_v, W_out, b_out):
        import jax, jax.numpy as jnp
        import numpy as np
        B, T, C, H, G = (8, 2048, 64, 8, 64)
        D = C // H
        Bs, Ts, Cs = x_q.shape
        Hh = temperature.shape[1]
        Dd = Cs // Hh
        tmp_x = (x_q @ W_in + b_in).reshape(Bs, Ts, Hh, Dd).transpose(0, 2, 1, 3)
        slice_weights = jax.nn.softmax((tmp_x @ W_slice + b_slice) / temperature, axis=-1)
        slice_norm = slice_weights.sum(axis=2)
        slice_ = jnp.einsum('bhnc,bhng->bhgc', tmp_x, slice_weights)
        token = slice_ / (slice_norm[:, :, :, None] + 1e-05)
        q = token @ W_q + b_q
        k = token @ W_k + b_k
        v = token @ W_v + b_v
        attn = jax.nn.softmax(q @ k.swapaxes(-2, -1) / float(np.sqrt(Dd)), axis=-1)
        out = attn @ v
        out = jnp.einsum('bhgc,bhng->bhnc', out, slice_weights)
        out = out.transpose(0, 2, 1, 3).reshape(Bs, Ts, Cs)
        return out @ W_out + b_out

    def _L1_ffn_ref(x, hl_w, hl_b, wq, wk, wv, gate_w, gate_b, ln_g, ln_b, fc1_w, fc1_b, fc2_w, fc2_b, fnorm_g, fnorm_b, fgate_w):
        import jax, jax.numpy as jnp
        import numpy as np
        B, S, H, NH, NE = (4, 256, 64, 4, 4)
        D = H // NH
        EPS = 1e-08

        def layernorm(x, g, b):
            m = jnp.mean(x, axis=-1, keepdims=True)
            v = jnp.mean((x - m) ** 2, axis=-1, keepdims=True)
            return (x - m) / jnp.sqrt(v + EPS) * g + b
        b, s, h = x.shape
        nh, d, _ = wk.shape
        ne = wq.shape[1]
        sx = jnp.einsum('bsh,ndh->bnsd', x, hl_w) + hl_b[None, :, None, :]
        pad = sx == 0
        q = jnp.einsum('bnsd,neod->bneso', sx, wq)
        k = jnp.einsum('bnsd,nod->bnso', sx, wk)
        v = jnp.einsum('bnsd,nod->bnso', sx, wv)
        causal = jnp.where(jnp.tril(jnp.ones((s, s), bool)), 0.0, -jnp.inf).astype(x.dtype)
        scores = jnp.einsum('bnesd,bntd->bnest', q, k) * d ** 0.5 + causal
        att = jax.nn.softmax(scores, axis=-1)
        qkv = jnp.einsum('bnest,bntd->bnesd', att, v)
        qkv = jnp.where(pad[:, :, None], 0.0, qkv)
        out = jnp.transpose(qkv, (0, 1, 3, 2, 4)).reshape(b, nh, s, ne * d)
        gs = jax.nn.softmax(jnp.einsum('bnsf,nef->bnse', out, gate_w) + gate_b[None, :, None, :], axis=-1)
        mixed = jnp.einsum('bnsed,bnse->bnsd', out.reshape(b, nh, s, ne, d), gs)
        resid = sx[jnp.arange(nh), jnp.arange(nh)]
        hn = layernorm(mixed + resid, ln_g, ln_b)
        f_n = jnp.transpose(hn, (0, 2, 1, 3)).reshape(b, s, h)
        fx = f_n.reshape(b, s, nh, d)
        pm = fx == 0
        hx = jnp.where(pm, 0.0, fx @ fc1_w.T + fc1_b)
        hx = jax.nn.relu(hx)
        hx = jnp.where(pm, 0.0, hx @ fc2_w.T + fc2_b)
        hx = layernorm(hx + fx, fnorm_g, fnorm_b)
        fout = hx.reshape(b, s, h)
        fg = jax.nn.softmax(fout @ fgate_w.T, axis=-1)
        return (fout.reshape(b, s, nh, d) * fg[..., None]).reshape(b, s, h)
    h = _L0_tok_ref(x, L0_tok_score_proj)
    h = h + _L0_attn_ref(_layernorm(h, axis=-1), L0_attn_ln_gamma, L0_attn_ln_beta, L0_attn_Wq, L0_attn_bq, L0_attn_Wk, L0_attn_bk, L0_attn_Wv, L0_attn_bv, L0_attn_Wpos, L0_attn_u_bias, L0_attn_v_bias, L0_attn_Wout, L0_attn_bout)
    h = h + _L0_ffn_ref(_layernorm(h, axis=-1), L0_ffn_gate_w, L0_ffn_gate_b, L0_ffn_W1, L0_ffn_b1, L0_ffn_W2, L0_ffn_b2)
    h = h + _L1_attn_ref(_layernorm(h, axis=-1), L1_attn_x_r, L1_attn_y, L1_attn_W_in, L1_attn_b_in, L1_attn_W_slice, L1_attn_b_slice, L1_attn_temperature, L1_attn_W_q, L1_attn_b_q, L1_attn_W_k, L1_attn_b_k, L1_attn_W_v, L1_attn_b_v, L1_attn_W_out, L1_attn_b_out)
    h = h + _L1_ffn_ref(_layernorm(h, axis=-1), L1_ffn_hl_w, L1_ffn_hl_b, L1_ffn_wq, L1_ffn_wk, L1_ffn_wv, L1_ffn_gate_w, L1_ffn_gate_b, L1_ffn_ln_g, L1_ffn_ln_b, L1_ffn_fc1_w, L1_ffn_fc1_b, L1_ffn_fc2_w, L1_ffn_fc2_b, L1_ffn_fnorm_g, L1_ffn_fnorm_b, L1_ffn_fgate_w)
    return h

_drawn_inputs = setup_inputs


def setup_inputs(seed=0):
    import zlib

    import numpy as np

    out = dict(_drawn_inputs(seed))
    spreads = {'L0_attn_ln_gamma': (1.0, 0.6),
     'L0_attn_ln_beta': (0.0, 0.8),
     'L0_attn_bq': (0.0, 0.8),
     'L0_attn_bk': (0.0, 2.0),
     'L0_attn_bv': (0.0, 0.332),
     'L0_attn_bout': (0.0, 0.1),
     'L0_ffn_gate_b': (0.0, 0.302),
     'L0_ffn_b1': (0.0, 0.8),
     'L0_ffn_b2': (0.0, 0.282),
     'L1_attn_b_in': (0.0, 0.8),
     'L1_attn_b_slice': (0.0, 2.0),
     'L1_attn_temperature': (0.3535533845424652, 0.6),
     'L1_attn_b_q': (0.0, 2.0),
     'L1_attn_b_k': (0.0, 2.0),
     'L1_attn_b_v': (0.0, 0.397),
     'L1_attn_b_out': (0.0, 0.1),
     'L1_ffn_ln_g': (1.0, 0.2),
     'L1_ffn_ln_b': (0.0, 0.35),
     'L1_ffn_fnorm_g': (1.0, 0.2),
     'L1_ffn_fnorm_b': (0.0, 0.283)}
    factors = {'L0_attn_Wq': 8.0,
     'L0_attn_Wk': 8.0,
     'L0_attn_Wv': 8.0,
     'L0_attn_Wpos': 8.0,
     'L0_attn_u_bias': 8.0,
     'L0_attn_v_bias': 24.191,
     'L0_ffn_W1': 8.0,
     'L0_ffn_W2': 8.0,
     'L1_attn_W_in': 8.0,
     'L1_attn_W_slice': 8.0,
     'L1_attn_W_q': 64.0,
     'L1_attn_W_k': 63.04,
     'L1_attn_W_v': 8.0,
     'L1_attn_W_out': 2.879,
     'L1_ffn_wq': 8.0,
     'L1_ffn_wk': 8.0,
     'L1_ffn_gate_w': 64.0,
     'L1_ffn_gate_b': 57.923,
     'L1_ffn_fc1_w': 6.486,
     'L1_ffn_fc1_b': 8.0,
     'L1_ffn_fc2_w': 4.38,
     'L1_ffn_fc2_b': 3.482}
    for name, (base, spread) in spreads.items():
        noise = np.random.default_rng([zlib.crc32(name.encode()), seed]).standard_normal(out[name].shape)
        drawn = base * np.exp(spread * noise) if base else spread * noise
        out[name] = jnp.asarray(drawn.astype(out[name].dtype))
    for name, factor in factors.items():
        out[name] = (out[name] * factor).astype(out[name].dtype)
    return out
```

```python
from contextlib import ExitStack

import numpy as np

import concourse.bass as bass
from concourse import mybir

F32 = mybir.dt.float32
BF16 = mybir.dt.bfloat16
ALU = mybir.AluOpType
ACT = mybir.ActivationFunctionType
AX = mybir.AxisListType.X

NB = 32
N_IN = 750
S = N_IN // 2
D = 64
TP = 125
CI = N_IN // TP
NT = S // TP
H0, DH = 4, 16
NE, DE = 8, 128
HS, DS, G = 8, 8, 64
PS = HS // 2
DS1 = DS + 1
HE, EE, DH2 = 4, 4, 16
QE = HE * EE
VS = DH2 + 1
EPS = 1e-5
EPS2 = 1e-8
BIG = -1e30
TINY = 2.0 ** -126




class Pack:

    def __init__(self):
        self.parts, self.at, self.width = [], {}, 0

    def add(self, name, array):
        array = np.asarray(array)
        rows, shape = array.shape[0], array.shape[1:]
        cols = int(np.prod(shape))
        self.at[name] = (rows, self.width, shape)
        self.parts.append(array.reshape(rows, cols))
        self.width += cols

    def build(self, dtype):
        out = np.zeros((128, self.width), dtype)
        at = 0
        for part in self.parts:
            out[:part.shape[0], at:at + part.shape[1]] = part
            at += part.shape[1]
        return out

    def view(self, tile, name):
        rows, at, shape = self.at[name]
        v = tile[0:rows, at:at + int(np.prod(shape))]
        if len(shape) == 2:
            v = v.rearrange("p (a b) -> p a b", a=shape[0])
        if len(shape) == 3:
            v = v.rearrange("p (a b c) -> p a b c", a=shape[0], b=shape[1])
        return v


def shape_constants():
    f, b = Pack(), Pack()
    f.add("ident", np.eye(128))
    w = np.exp(np.arange(0, D, 2, dtype=np.float32) * np.float32(-np.log(10000.0) / D)).astype(np.float64)
    wf = np.repeat(w, 2)[:, None]
    is_cos = (np.arange(D) % 2 == 1)[:, None]
    sign = np.where(is_cos, 1.0, -1.0)
    j = np.arange(S)[None, :]
    pe = np.where(is_cos, np.cos(j * wf), np.sin(j * wf))
    f.add("pe", np.concatenate([pe, pe]))
    c = (S - 1 - j)
    f.add("cos_low", np.tile(np.cos(c * wf), (2, 1)))
    f.add("sin_low", np.tile(sign * np.sin(c * wf), (2, 1)))
    c = -(np.arange(1, S)[None, :] + 1)
    f.add("cos_up", np.tile(np.cos(c * wf), (2, 1)))
    f.add("sin_up", np.tile(sign * np.sin(c * wf), (2, 1)))
    for name, value in (("eps", EPS), ("one_eps", 1.0 + EPS), ("eps_eps", EPS * EPS)):
        f.add(name, np.full((TP, 4 * NT), value))
    f.add("iota", np.tile(np.arange(S)[None, :], (TP, 1)))
    last = np.zeros((TP, NT, H0))
    last[TP - 1, NT - 1] = BIG
    f.add("no_next", last)
    p = np.arange(TP)[:, None]
    b.add("ident_b", np.eye(128))
    tie = np.zeros((TP, CI, N_IN))
    for t in range(CI):
        tie[:, t] = np.where(np.arange(N_IN)[None, :] < t * TP + p, 0.0, TINY)
    b.add("tie", tie)
    q = np.arange(TP)[None, :]
    q2 = np.arange(2 * TP)[None, :]
    b.add("m_low_q", np.where(q > p, BIG, 0.0))
    b.add("m_up_q", np.where(q2 < p + 2, BIG, 0.0))
    b.add("m_low_k", np.where(q < p, BIG, 0.0))
    b.add("m_up_k", np.where(q2 - TP > p - 2, BIG, 0.0))
    pick = np.zeros((96, H0, TP))
    for h in range(H0):
        pick[h, h] = 1.0
    b.add("pick_head", pick)
    expert = np.zeros((96, NE, 128))
    for e in range(NE):
        expert[e:3 * NE:NE, e] = 1.0
    b.add("pick_expert", expert)
    b.add("earlier", np.tile(np.tril(np.ones((NE, NE)), -1).reshape(1, NE * NE), (TP, 1)))
    f.add("slice_block", np.kron(np.eye(HS), np.full((DS1, DS1), 1 / np.sqrt(np.float64(DS)))))
    own_pair = np.zeros((HS * DS1, PS, G))
    for h in range(HS):
        own_pair[h * DS1:(h + 1) * DS1, h // 2] = 1.0
    f.add("own_pair", own_pair)
    slices = np.zeros((96, HS * G))
    for h in range(HS):
        slices[h, h * G:(h + 1) * G] = 1.0
    b.add("pick_slices", slices)
    sel = np.zeros((128, HE * VS))
    for n in range(HE):
        sel[32 * n:32 * n + VS, n * VS:(n + 1) * VS] = np.eye(VS)
    f.add("sel", sel)
    f.add("eps2", np.full((TP, NT * HE), EPS2))
    f.add("per_width", np.full((TP, NT * HE), 1.0 / DH2))
    expert_row = np.zeros((96, QE, TP))
    for n in range(QE):
        expert_row[n, n] = 1.0
    b.add("pick_query", expert_row)
    f.add("two_halves", np.concatenate([np.eye(D), np.eye(D)]))
    f.add("euler", np.full((TP, NT * NE), np.e))
    return f, b


def weight_layout(w):
    k = Pack()
    z = lambda *s: np.zeros(s, np.float32)

    def over(matrix, *rows):
        out = z(96, matrix.shape[1])
        out[:matrix.shape[0]] = matrix
        for n, r in enumerate(rows):
            out[matrix.shape[0] + n] = r
        return out

    g = {n[len("L0_attn_"):]: v for n, v in w.items() if n.startswith("L0_attn_")}
    k.add("score_w", np.broadcast_to(w["L0_tok_score_proj"].reshape(1, D), (TP, D)))
    k.add("gamma", g["ln_gamma"].reshape(D, 1))
    k.add("beta", g["ln_beta"].reshape(D, 1))
    wq = over(g["Wq"], g["bq"], g["u_bias"].reshape(D))
    wk = over(g["Wk"], g["bk"])
    wv = over(g["Wv"], g["bv"])
    cq, ck = z(96, 2, 128), z(96, 2, 128)
    for h in range(H0):
        at = 64 if h % 2 == 0 else 0
        cq[:, h // 2, at:at + DH] = wq[:, h * DH:(h + 1) * DH]
        ck[:, h // 2, at:at + DH] = wk[:, h * DH:(h + 1) * DH]
    k.add("wcq", cq)
    k.add("wck", ck)
    va = z(96, H0, 32)
    va[:, :, :DH] = wv.reshape(96, H0, DH)
    va[D, :, DH] = 1.0
    k.add("wq_tok", wq)
    k.add("wv_aug", va.reshape(96, 128))
    k.add("wkv_next", np.concatenate([wk, wv], 1))
    k.add("wout", over(g["Wout"], g["bout"]))
    qT = z(DH, H0, 66)
    qT[:, :, :D] = g["Wq"].reshape(D, H0, DH).transpose(2, 1, 0)
    qT[:, :, D] = g["bq"].reshape(H0, DH).T
    qT[:, :, D + 1] = g["v_bias"].T
    posT = g["Wpos"].reshape(D, H0, DH).transpose(2, 1, 0)
    k.add("wqT", qT)
    k.add("wposT", np.ascontiguousarray(posT))
    m = {n[len("L0_ffn_"):]: v for n, v in w.items() if n.startswith("L0_ffn_")}
    k.add("gate_w", over(m["gate_w"], m["gate_b"]))
    w1 = z(96, NE, DE)
    w1[:D] = m["W1"].transpose(1, 0, 2)
    w1[D] = m["b1"]
    k.add("w1", w1)
    k.add("w2", m["W2"].transpose(1, 0, 2))
    k.add("b2", np.tile(m["b2"], (3, 1)))
    a = {n[len("L1_attn_"):]: v for n, v in w.items() if n.startswith("L1_attn_")}
    k.add("w_in", over(a["W_in"], a["b_in"]))
    inT = z(DS1, HS, D + 1)
    inT[:DS, :, :D] = a["W_in"].reshape(D, HS, DS).transpose(2, 1, 0)
    inT[:DS, :, D] = a["b_in"].reshape(HS, DS).T
    inT[DS, :, D] = 1.0
    k.add("w_inT", inT)
    k.add("w_slice", np.concatenate([a["W_slice"], a["b_slice"][None, :]]))
    k.add("temperature", np.broadcast_to(a["temperature"].reshape(1, HS), (96, HS)))
    k.add("wq_sT", np.tile(np.concatenate([a["W_q"], a["b_q"][None, :]]).T, (1, HS)))
    k.add("wk_sT", np.tile(np.concatenate([a["W_k"], a["b_k"][None, :]]).T, (1, HS)))
    wv9 = np.concatenate([a["W_v"], a["b_v"][None, :]])
    bdv = z(HS * DS1, PS, DS)
    for h in range(HS):
        bdv[h * DS1:(h + 1) * DS1, h // 2] = wv9
    k.add("wv_s", bdv.reshape(HS * DS1, PS * DS))
    k.add("w_out_s", over(a["W_out"], a["b_out"]))
    l = {n[len("L1_ffn_"):]: v for n, v in w.items() if n.startswith("L1_ffn_")}
    sx = over(l["hl_w"].reshape(D, D).T, l["hl_b"].reshape(D))
    k.add("w_sx", sx)
    wide = z(96, HE, 32)
    wide[:, :, :DH2] = sx.reshape(96, HE, DH2)
    wide[D, :, DH2] = 1.0
    k.add("w_sx_wide", wide.reshape(96, 128))
    k.add("w_sxT", np.concatenate([l["hl_w"].reshape(D, D), l["hl_b"].reshape(D, 1)], 1))
    heads = z(D, 4, HE, 2, DH2)
    for n in range(HE):
        rows = slice(n * DH2, (n + 1) * DH2)
        for e in range(EE):
            heads[rows, e % 2, n, e // 2] = l["wq"][n, e].T
        heads[rows, 2, n, 0] = l["wk"][n].T
        heads[rows, 3, n, 0] = l["wv"][n].T
    k.add("w_heads", heads.reshape(D, 4, 128))
    gw = z(128, EE, HE * EE)
    for n in range(HE):
        for e in range(EE):
            gw[32 * n:32 * n + DH2, e, n * EE:(n + 1) * EE] = l["gate_w"][n, :, e * DH2:(e + 1) * DH2].T
    k.add("gate_w2", gw)
    k.add("gate_b2", np.broadcast_to(l["gate_b"].reshape(1, QE), (TP, QE)))
    for name in ("ln_g", "ln_b", "fnorm_g", "fnorm_b"):
        k.add(name, np.broadcast_to(l[name].reshape(1, DH2), (TP, DH2)))
    for name in ("fc1", "fc2"):
        block = z(D, D)
        for n in range(HE):
            block[n * DH2:(n + 1) * DH2, n * DH2:(n + 1) * DH2] = l[name + "_w"].T
        k.add(name, over(block, np.tile(l[name + "_b"], HE)))
    k.add("fgate", l["fgate_w"].T)
    k.add("wposT_swap", posT.reshape(DH, H0, D // 2, 2)[..., ::-1].reshape(DH, H0, D))
    return k




class Tally:

    def __init__(self, sem):
        self.sem, self.base, self.n = sem, 0, 0

    def up(self, instruction):
        instruction.then_inc(self.sem, 1)
        self.n += 1

    def wait(self, eng):
        eng.wait_ge(self.sem, self.base + self.n)

    def link(self, eng, instruction):
        self.up(instruction)
        self.wait(eng)


def wait(eng, sem, value):
    if not isinstance(value, int) or value > 0:
        eng.wait_ge(sem, value)


def rounds(eng, step, lags, tally, n, period=2):
    peel = lags + period
    peel += (n - peel) % period
    for t in range(peel):
        if t == peel - period:
            before = tally.n
        step(t, t % period)
    per = tally.n - before
    entry = tally.base + tally.n
    count = (n - peel) // period
    if count:
        with eng.Fori(0, count) as g:
            tally.base, tally.n = g * per + entry, 0
            for i in range(period):
                step(g * period + (peel + i), (peel + i) % period)
            assert tally.n == per
    tally.base, tally.n = entry + count * per, 0
    for t in range(n, n + lags):
        step(t, t % period)


def alive(b, n):
    return not isinstance(b, int) or 0 <= b < n


class Core:

    def __init__(self, nc, ctx, packs, nb):
        self.nc, self.nb = nc, nb
        fpack, bpack, wpack = packs
        self.sb = lambda name, shape, dt=F32: ctx.enter_context(nc.sbuf_tensor(name, shape, dt))
        self.sem = lambda name: nc.alloc_semaphore(name=name)
        self.fc = self.sb("fconst", [128, fpack.width])
        self.bc = self.sb("bconst", [128, bpack.width], BF16)
        self.wc = self.sb("weights", [128, wpack.width])
        self.F = lambda name: fpack.view(self.fc, name)
        self.B = lambda name: bpack.view(self.bc, name)
        self.W = lambda name: wpack.view(self.wc, name)
        self.bank = ctx.enter_context(nc.psum_tensor("psum", [128, 8, 512], F32))
        self.h = self.sb("h_all", [TP, nb, NT * D])
        self.half = self.sb("minus_half", [TP, 4 * NT])





def score_tokens(k, x_dram, fpack_dram, bpack_dram, wpack_dram, s_dram, t):
    nc, nb = k.nc, k.nb
    tiles = nb * CI
    chunk = 4 * CI if nb % 4 == 0 else CI
    n_chunks = tiles // chunk
    loaded, multiplied = (k.sem("x_even_loaded"), k.sem("x_odd_loaded")), k.sem("x_multiplied")
    half_set = k.sem("half_set")
    const_loaded, w_loaded = k.sem("const_loaded"), k.sem("weights_loaded")
    dve_own, scored = k.sem("score_dve_own"), k.sem("scored")
    s_turned, s_copied, s_stored = k.sem("scores_turned"), k.sem("scores_copied"), k.sem("scores_stored")
    gate_exp, folded, folded_copied = k.sem("gate_exp"), k.sem("folded"), k.sem("folded_copied")
    W, F = k.W, k.F
    with ExitStack() as ctx:
        xs = ctx.enter_context(nc.sbuf_tensor("x_chunks", [TP, 2, chunk, D], F32))
        prod = ctx.enter_context(nc.sbuf_tensor("prod", [TP, chunk, D], F32))
        s_rows = ctx.enter_context(nc.sbuf_tensor("s_rows", [128, 2, TP], F32))
        block = ctx.enter_context(nc.Block())
        groups = [(a, min(a + 128, tiles)) for a in range(0, tiles, 128)]

        @block.sync
        def _(sp):
            sp.dma_start(k.wc[:], wpack_dram).then_inc(w_loaded, 16)
            for i in range(n_chunks):
                src = x_dram.rearrange("b (c p) f -> p (b c) f", p=TP)[:, i * chunk:(i + 1) * chunk, :]
                wait(sp, multiplied, i - 1)
                sp.dma_start(xs[:, i % 2], src).then_inc(loaded[i % 2], 16)
                if i == 0:
                    sp.dma_start(k.fc[:], fpack_dram).then_inc(const_loaded, 16)
                    sp.dma_start(k.bc[:], bpack_dram).then_inc(const_loaded, 16)
            sp.wait_ge(s_copied, len(groups))
            for n, (a, e) in enumerate(groups):
                sp.dma_start(s_dram[a:e, :], s_rows[0:e - a, n, :]).then_inc(s_stored, 16)
            sp.wait_ge(s_stored, 16 * len(groups))

        @block.vector
        def _(dve):
            own = Tally(dve_own)
            nc.vector.memset(k.half[:], -0.5).then_inc(half_set, 1)
            own.link(dve, nc.vector.memset(t.xT[:], 0.0))
            own.up(nc.vector.memset(t.xT[D:D + 2], 1.0))
            own.up(nc.vector.memset(t.xn[:, :, D:], 0.0))
            own.up(nc.vector.memset(t.ctx[:, :, D:], 0.0))
            own.up(nc.vector.memset(t.RW[:], 0.0))
            own.up(nc.vector.memset(t.maxT[:], 0.0))
            own.up(nc.vector.memset(t.neg_max[:], 0.0))
            own.up(nc.vector.memset(t.Q[:], 0.0))
            own.link(dve, nc.vector.memset(t.K[:], 0.0))
            own.up(nc.vector.memset(t.ctxT[:], 0.0))
            own.wait(dve)
            own.up(nc.vector.memset(t.ctxT[D:D + 1], 1.0))
            dve.wait_ge(w_loaded, 16)
            w = W("score_w").rearrange("p (o f) -> p o f", o=1).to_broadcast((TP, chunk, D))
            for i in range(n_chunks):
                dve.wait_ge(loaded[i % 2], 16 * (i // 2 + 1))
                nc.vector.tensor_tensor(prod[:], xs[:, i % 2], w, ALU.mult).then_inc(multiplied, 1)
                dve.wait_ge(multiplied, i + 1)
                width = D
                while width > 2:
                    width //= 2
                    own.link(dve, nc.vector.tensor_tensor(prod[:, :, 0:width], prod[:, :, 0:width],
                                                          prod[:, :, width:2 * width], ALU.add))
                own.link(dve, nc.vector.tensor_tensor(t.score[:, i * chunk:(i + 1) * chunk],
                                                      prod[:, :, 0], prod[:, :, 1], ALU.add))
            own.up(nc.vector.memset(prod[:, 0, 0:1], 0.0))
            nc.vector.tensor_scalar(t.score[:], t.score[:], 1.0, None, ALU.mult).then_inc(scored, 1)
            for n, (a, e) in enumerate(groups):
                dve.wait_ge(s_turned, n + 1)
                nc.vector.tensor_copy(s_rows[0:e - a, n, :], k.bank[0:e - a, n, 0:TP]).then_inc(s_copied, 1)
            dve.wait_ge(gate_exp, 1)
            own.link(dve, nc.vector.tensor_scalar(t.gate[:], t.gate[:], 1.0, None, ALU.add))
            own.link(dve, nc.vector.reciprocal(t.gate[:], t.gate[:]))
            dve.wait_ge(const_loaded, 32)
            for par in range(2):
                for h in range(H0):
                    at = 0 if h % 2 == 0 else D
                    own.up(nc.vector.tensor_copy(t.K[at:at + D, par, h, :], F("pe")[at:at + D, :]))
            dve.wait_ge(folded, 1)
            for n in range(2):
                own.up(nc.vector.tensor_copy(t.RW[0:D + 2, n, :], k.bank[0:D + 2, 2 + n, 0:H0 * D]))

        @block.scalar
        def _(act):
            act.wait_ge(scored, 1)
            nc.scalar.activation(t.gate[:], t.score[:], ACT.Exp, scale=-1.0).then_inc(gate_exp, 1)

        @block.tensor
        def _(pe):
            pe.wait_ge(w_loaded, 16)
            for n, name in enumerate(("wposT", "wposT_swap")):
                for h in range(H0):
                    last = nc.tensor.matmul(k.bank[0:D + 2, 2 + n, h * D:(h + 1) * D], W("wqT")[:, h, :],
                                            W(name)[:, h, :], start=True, stop=True)
            last.then_inc(folded, 1)
            pe.wait_ge(const_loaded, 32)
            pe.wait_ge(scored, 1)
            for n, (a, e) in enumerate(groups):
                nc.tensor.transpose(k.bank[0:e - a, n, 0:TP], t.score[:, a:e],
                                    F("ident")[0:TP, 0:TP]).then_inc(s_turned, 1)




class SelectAttend:

    def __init__(self, k, ctx):
        nb = k.nb
        sb = lambda name, shape, dt=F32: ctx.enter_context(k.nc.sbuf_tensor(name, shape, dt))
        self.x = sb("x_tokens", [TP, 2, CI, D])
        self.score = sb("score", [TP, nb * CI])
        self.gate = sb("gate", [TP, nb * CI])
        self.s_row = sb("s_row", [TP, 2, N_IN])
        self.s_loc = sb("s_loc", [TP, CI])
        self.xg = sb("x_gated", [TP, CI, D])
        self.counted = sb("counted", [TP, N_IN], BF16)
        self.rank = sb("rank", [TP, CI])
        self.hot = sb("one_hot", [TP, CI, S])
        self.h_new = sb("h_new", [TP, NT * D])
        self.stats = sb("stats", [TP, NT, 6])
        self.mv = sb("mean_var", [TP, NT, 2])
        self.rstd = sb("rstd", [TP, NT])
        self.xn = sb("xn", [TP, NT, 128])
        self.xT = sb("xT", [96, 2, S + 1])
        self.RW = sb("RW", [96, 2, H0 * D])
        self.rot = sb("rot", [128, 4, S])
        self.Q = sb("Q", [128, 2 * H0, 2, S])
        self.K = sb("K", [128, 2, H0, S])
        self.q_tok = sb("q_tok", [TP, NT, D])
        self.v_aug = sb("v_aug", [TP, 2, NT, 128])
        self.v_next = sb("v_next", [TP, 2, NT, D])
        self.qk = sb("qk_next", [TP, NT, D])
        self.s_next = sb("s_next", [TP, NT, H0])
        self.mx = sb("mx", [TP, NT, H0])
        self.neg_max = sb("neg_max", [TP, NT, 96], BF16)
        self.maxT = sb("maxT", [96, 2, S], BF16)
        self.e_next = sb("e_next", [TP, 2, NT * H0])
        self.E = sb("E", [TP, 3, 2, 500])
        self.cT = sb("cT", [128, S])
        self.e_v = sb("e_v", [TP, NT * H0, DH])
        self.den = sb("den", [TP, NT, H0])
        self.ctx = sb("ctx", [TP, NT, 128])
        self.ctxT = sb("ctxT", [96, S])

    def Qb(self, par):
        return self.Q[:, par * H0:(par + 1) * H0]


def select_attend(k, t, x_dram, s_dram):
    nc, nb, F, B, W, bank = k.nc, k.nb, k.F, k.B, k.W, k.bank
    sem = lambda n: k.sem("a_" + n)
    row_loaded, x_loaded, ranked, hot_ready, gathered, h_copied = map(sem, ("row_loaded", "x_loaded", "ranked", "hot", "gathered", "h_copied"))
    var_ready, rstd_ready, xn_ready, x_turned, xT_ready = map(sem, ("var", "rstd", "xn", "x_turned", "xT"))
    pv_ready, pa_ready = sem("proj_for_dve"), sem("proj_for_act")
    pv_free, pa_free = sem("proj_by_dve"), sem("proj_by_act")
    Q_rows = sem("Q_rows")
    m_ready, m_free, e_ready, e_done, pv_done = map(sem, ("m_ready", "m_free", "e_ready", "e_done", "pv_done"))
    neg_ready, neg_turned, maxT_ready, snext_ready, enext_ready = map(sem, ("neg", "neg_turned", "maxT", "snext", "enext"))
    cT_ready, ctx_turned, tok_ready, ctx_ready, ctxT_turned, ctxT_ready, out_ready, out_added = map(
        sem, ("cT", "c_turned", "tok", "ctx", "ctx_turned", "ctxT", "out", "out_added"))
    own_dve, own_act, own_pool, own_pe, own_sp = map(sem, ("own_dve", "own_act", "own_pool", "own_pe", "own_sp"))

    def q_unit(it):
        return ((0, 0, 0, TP * (it + 1)), (1, TP * it, TP * (it + 1), TP * (NT - it)))

    def k_unit(jt):
        return ((0, TP * jt, 0, TP * (NT - jt)), (1, 0, TP * (NT - jt), TP * (jt + 1)))

    def rows(h):
        return 96 if h % 2 == 0 else 128

    pairs = [(tile, hp) for tile in range(NT) for hp in range(2)]

    with nc.Block() as block:

        @block.sync
        def _(sp):
            def step(b, par):
                if alive(b, nb):
                    wait(sp, ranked, (b - 1) * CI)
                    wait(sp, x_loaded, b * 16)
                    wait(sp, row_loaded, b * 16)
                    sp.dma_start(t.s_row[:, par, :], s_row_of(b)).then_inc(row_loaded, 16)
                    sp.dma_start(t.x[:, par], x_dram[bass.ds(b, 1)].rearrange("o (c p) f -> p (o c) f", p=TP)
                                 ).then_inc(x_loaded, 16)

            def s_row_of(b):
                flat = s_dram.rearrange("(b c) p -> b (c p)", c=CI)
                return flat[bass.ds(b, 1), :].to_broadcast((TP, N_IN))

            rounds(sp, step, 2, Tally(own_sp), nb)

        @block.tensor
        def _(pe):
            def project(b, par):
                xT = t.xT[:, par, :]
                wait(pe, xT_ready, b + 1)
                n = [b * 6, b * 5]

                def fill(which, parts):
                    wait(pe, (pv_free, pa_free)[which], n[which])
                    for out, lhsT, rhs in parts:
                        last = nc.tensor.matmul(out, lhsT, rhs, start=True, stop=True)
                    last.then_inc((pv_ready, pa_ready)[which], 1)
                    n[which] = n[which] + 1

                x = xT[:, 0:S]
                full = lambda bk: bank[:, bk, 0:S]
                tile = lambda it: xT[:, it * TP:(it + 1) * TP]
                after = lambda it: xT[:, it * TP + 1:(it + 1) * TP + 1]
                for p in range(2):
                    fill(0, [(full(1), t.RW[:, 0, p * 128:(p + 1) * 128], x)])
                    fill(1, [(full(2), W("wck")[:, p, :], x)])
                    fill(0, [(full(1), t.RW[:, 1, p * 128:(p + 1) * 128], x)])
                    fill(1, [(full(2), W("wcq")[:, p, :], x)])
                fill(0, [(bank[0:TP, 1, it * D:(it + 1) * D], tile(it), W("wq_tok")) for it in range(NT)])
                fill(1, [(bank[0:TP, 2, it * 128:(it + 1) * 128], tile(it), W("wv_aug")) for it in range(NT)])
                fill(0, [(bank[0:TP, 1, it * 128:(it + 1) * 128], after(it), W("wkv_next")) for it in range(NT)])

            def scores_for_exp(b, par, n):
                jt, hp = pairs[n]
                if n == 0:
                    pe.wait_ge(maxT_ready, b + 1)
                wait(pe, e_done, b * 6 + n)
                for i in range(2):
                    h = 2 * hp + i
                    out = bank[0:TP, 4 + i, :]
                    key = t.K[0:rows(h), par, h, jt * TP:(jt + 1) * TP]
                    for part, q0, c0, cols in k_unit(jt):
                        nc.tensor.matmul(out[:, c0:c0 + cols], key, t.Qb(par)[0:rows(h), h, part, q0:q0 + cols],
                                         start=part == 0, stop=False, skip_group_check=True)
                        nc.tensor.matmul(out[:, c0:c0 + cols], B("pick_head")[:, h, :], t.maxT[:, par, q0:q0 + cols],
                                         start=False, stop=False, skip_group_check=True)
                    nc.tensor.matmul(out[:, 0:TP], B("ident_b")[0:TP, 0:TP], B("m_low_k"),
                                     start=False, stop=False, skip_group_check=True)
                    w = TP if jt == 0 else 2 * TP
                    last = nc.tensor.matmul(out[:, 4 * TP - w:4 * TP], B("ident_b")[0:TP, 0:TP],
                                            B("m_up_k")[:, 2 * TP - w:], start=False, stop=True, skip_group_check=True)
                last.then_inc(e_ready, 1)

            def scores_for_max(b, par, n):
                it, hp = pairs[n]
                if n == 0:
                    pe.wait_ge(Q_rows, (b + 1) * 2)
                    pe.wait_ge(pa_free, b * 5 + 5)
                wait(pe, m_free, b * 6 + n)
                for i in range(2):
                    h = 2 * hp + i
                    out = bank[0:TP, 6 + i, :]
                    for part, j0, c0, cols in q_unit(it):
                        nc.tensor.matmul(out[:, c0:c0 + cols], t.Qb(par)[0:rows(h), h, part, it * TP:(it + 1) * TP],
                                         t.K[0:rows(h), par, h, j0:j0 + cols],
                                         start=part == 0, stop=False, skip_group_check=True)
                    nc.tensor.matmul(out[:, it * TP:(it + 1) * TP], B("ident_b")[0:TP, 0:TP], B("m_low_q"),
                                     start=False, stop=False, skip_group_check=True)
                    w = TP if it == NT - 1 else 2 * TP
                    c0 = TP * (it + 1)
                    last = nc.tensor.matmul(out[:, c0:c0 + w], B("ident_b")[0:TP, 0:TP], B("m_up_q")[:, 0:w],
                                            start=False, stop=True, skip_group_check=True)
                last.then_inc(m_ready, 1)

            def weigh_values(b, par, n):
                jt, hp = pairs[n]
                pe.wait_ge(e_done, b * 6 + n + 1)
                if n == 0:
                    wait(pe, out_added, b)
                for part, q0, c0, cols in k_unit(jt):
                    for i in range(2):
                        h = 2 * hp + i
                        last = nc.tensor.matmul(bank[32 * h:32 * h + 32, 3, q0:q0 + cols],
                                                t.v_aug[:, par, jt, 32 * h:32 * h + 32],
                                                t.E[:, n % 3, i, c0:c0 + cols],
                                                start=(jt == 0 and part == 0), stop=(jt == NT - 1 and part == 1),
                                                skip_group_check=True)
                last.then_inc(pv_done, 1)

            def finish(b):
                pe.wait_ge(cT_ready, b + 1)
                for it in range(NT):
                    last = nc.tensor.transpose(bank[0:TP, 3, it * 128:(it + 1) * 128],
                                               t.cT[:, it * TP:(it + 1) * TP], F("ident"))
                last.then_inc(ctx_turned, 1)
                pe.wait_ge(ctx_ready, b + 1)
                for it in range(NT):
                    last = nc.tensor.transpose(bank[:, 3, it * TP:(it + 1) * TP], t.ctx[:, it, :],
                                               F("ident")[0:TP, 0:TP])
                last.then_inc(ctxT_turned, 1)
                pe.wait_ge(ctxT_ready, b + 1)
                for it in range(NT):
                    last = nc.tensor.matmul(bank[0:TP, 3, it * D:(it + 1) * D], t.ctxT[:, it * TP:(it + 1) * TP],
                                            W("wout"), start=True, stop=True)
                last.then_inc(out_ready, 1)

            def turn_max(b):
                pe.wait_ge(neg_ready, b + 1)
                wait(pe, pa_free, b * 5 + 5)
                for it in range(NT):
                    last = nc.tensor.matmul(bank[0:96, 2, it * TP:(it + 1) * TP], t.neg_max[:, it, :],
                                            B("ident_b")[0:TP, 0:TP], start=True, stop=True)
                last.then_inc(neg_turned, 1)

            def gather(b, par):
                pe.wait_ge(hot_ready, b + 1)
                wait(pe, xT_ready, b)
                for it in range(NT):
                    for c in range(CI):
                        last = nc.tensor.matmul(bank[0:TP, 0, it * D:(it + 1) * D],
                                                t.hot[:, c, it * TP:(it + 1) * TP], t.xg[:, c, :],
                                                start=c == 0, stop=c == CI - 1)
                last.then_inc(gathered, 1)
                pe.wait_ge(xn_ready, b + 1)
                for it in range(NT):
                    last = nc.tensor.transpose(bank[:, 0, it * TP:(it + 1) * TP], t.xn[:, it, :],
                                               F("ident")[0:TP, 0:TP])
                last.then_inc(x_turned, 1)

            def step(r, par):
                b1, b2 = r - 1, r - 2
                if alive(b1, nb):
                    if not isinstance(b1, int) or b1 > 0:
                        pe.wait_ge(maxT_ready, b1)
                    project(b1, 1 - par)
                for n in range(6):
                    if alive(b2, nb):
                        scores_for_exp(b2, par, n)
                    if alive(b1, nb):
                        scores_for_max(b1, 1 - par, n)
                    if alive(b2, nb) and n:
                        weigh_values(b2, par, n - 1)
                if alive(b2, nb):
                    weigh_values(b2, par, 5)
                    finish(b2)
                if alive(b1, nb):
                    turn_max(b1)
                if alive(r, nb):
                    gather(r, par)

            rounds(pe, step, 2, Tally(own_pe), nb)

        @block.vector
        def _(dve):
            own = Tally(own_dve)

            def projections(b, par):
                n = b * 6
                for p in range(2):
                    wait(dve, Q_rows, b * 2 + p)
                    for i, (low, up) in enumerate((("cos_low", "cos_up"), ("sin_low", "sin_up"))):
                        dve.wait_ge(pv_ready, n + 2 * p + i + 1)
                        nc.vector.tensor_tensor(t.rot[:, i, :], bank[:, 1, 0:S], F(low), ALU.mult)
                        nc.vector.tensor_tensor(t.rot[:, 2 + i, 0:S - 1], bank[:, 1, 1:S], F(up),
                                                ALU.mult).then_inc(pv_free, 1)
                dve.wait_ge(pv_ready, n + 5)
                nc.vector.tensor_copy(flat3(t.q_tok[:]), bank[0:TP, 1, 0:NT * D]).then_inc(pv_free, 1)
                dve.wait_ge(pv_free, n + 5)
                dve.wait_ge(pv_ready, n + 6)
                kv = bank[0:TP, 1, 0:NT * 128].rearrange("p (a b) -> p a b", a=NT)
                nc.vector.tensor_tensor(t.qk[:], t.q_tok[:], kv[:, :, 0:D], ALU.mult)
                wait(dve, out_added, b - 1)
                nc.vector.tensor_copy(t.v_next[:, par], kv[:, :, D:2 * D]).then_inc(pv_free, 1)
                dve.wait_ge(pv_free, n + 6)
                wait(dve, enext_ready, b)
                own.link(dve, nc.vector.tensor_reduce(flat3(t.s_next[:]), t.qk[:].rearrange("p a (h d) -> p (a h) d", h=H0),
                                                      AX, ALU.add))
                own.up(nc.vector.tensor_tensor(t.s_next[:], t.s_next[:], F("no_next"), ALU.add))

            def maxima(b, n):
                it, hp = pairs[n]
                dve.wait_ge(m_ready, b * 6 + n + 1)
                nc.vector.tensor_reduce(t.mx[:, it, 2 * hp:2 * hp + 2], bank[0:TP, 6:8, 0:4 * TP], AX,
                                        ALU.max).then_inc(m_free, 1)

            def negate_max(b):
                dve.wait_ge(m_free, b * 6 + 6)
                own.link(dve, nc.vector.tensor_tensor(t.mx[:], t.mx[:], t.s_next[:], ALU.max))
                wait(dve, neg_turned, b)
                nc.vector.tensor_scalar(t.neg_max[:, :, 0:H0], t.mx[:], -1.0, None, ALU.mult).then_inc(neg_ready, 1)
                dve.wait_ge(neg_ready, b + 1)
                nc.vector.tensor_tensor(t.s_next[:], t.s_next[:], t.neg_max[:, :, 0:H0], ALU.add).then_inc(snext_ready, 1)

            def take(b, par):
                own.up(nc.vector.tensor_scalar(t.s_loc[:], t.score[:, bass.ds(b * CI, CI)], 1.0, None, ALU.mult))
                wait(dve, gathered, b)
                dve.wait_ge(x_loaded, (b + 1) * 16)
                own.up(nc.vector.tensor_tensor(t.xg[:], t.x[:, par],
                                               t.gate[:, bass.ds(b * CI, CI)].rearrange("p (c o) -> p c o", o=1)
                                               .to_broadcast((TP, CI, D)), ALU.mult))
                own.wait(dve)
                dve.wait_ge(row_loaded, (b + 1) * 16)

            def count(b, par, c):
                wait(dve, ranked, b * CI + c)
                nc.vector.scalar_tensor_tensor(t.counted[:], t.s_row[:, par, :], t.s_loc[:, c:c + 1], B("tie")[:, c, :],
                                               ALU.subtract, ALU.is_ge,
                                               accum_out=t.rank[:, c:c + 1]).then_inc(ranked, 1)

            def one_hot(b):
                wait(dve, gathered, b)
                dve.wait_ge(ranked, (b + 1) * CI)
                for c in range(CI):
                    last = nc.vector.tensor_scalar(t.hot[:, c, :], F("iota"), t.rank[:, c:c + 1], None, ALU.is_equal)
                last.then_inc(hot_ready, 1)

            def finish(b, par):
                dve.wait_ge(enext_ready, b + 1)
                e = t.e_next[:, par, :]
                wide = lambda v: v.rearrange("p (a o) -> p a o", o=1).to_broadcast((TP, NT * H0, DH))
                own.up(nc.vector.tensor_tensor(t.e_v[:], t.v_next[:, par].rearrange("p a (h d) -> p (a h) d", h=H0),
                                               wide(e), ALU.mult))
                own.wait(dve)
                dve.wait_ge(ctx_turned, b + 1)
                c = bank[0:TP, 3, 0:NT * 128].rearrange("p (a d) -> p a d", d=32)
                den = flat3(t.den[:])
                own.link(dve, nc.vector.tensor_tensor(den, c[:, :, DH], e, ALU.add))
                own.up(nc.vector.reciprocal(den, den))
                wait(dve, ctxT_turned, b)
                own.link(dve, nc.vector.tensor_tensor(t.e_v[:], c[:, :, 0:DH], t.e_v[:], ALU.add))
                for it in range(NT):
                    heads = slice(it * H0, (it + 1) * H0)
                    last = nc.vector.tensor_tensor(t.ctx[:, it, 0:D].rearrange("p (h d) -> p h d", h=H0), t.e_v[:, heads, :],
                                                   den[:, heads].rearrange("p (h o) -> p h o", o=1)
                                                   .to_broadcast((TP, H0, DH)), ALU.mult)
                last.then_inc(ctx_ready, 1)
                dve.wait_ge(out_ready, b + 1)
                h = one(k.h, b)
                nc.vector.tensor_tensor(h, h, bank[0:TP, 3, 0:NT * D], ALU.add).then_inc(out_added, 1)

            def receive(b):
                dve.wait_ge(gathered, b + 1)
                nc.vector.tensor_copy(t.h_new[:], bank[0:TP, 0, 0:NT * D]).then_inc(h_copied, 1)
                dve.wait_ge(h_copied, b + 1)
                for it in range(NT):
                    own.up(nc.vector.bn_stats(t.stats[:, it, :], t.h_new[:, it * D:(it + 1) * D]))
                own.wait(dve)
                own.up(nc.vector.tensor_scalar(one(k.h, b), t.h_new[:], 1.0, None, ALU.mult))
                for it in range(NT):
                    last = nc.vector.bn_aggr(t.mv[:, it, :], t.stats[:, it, :])
                last.then_inc(var_ready, 1)
                dve.wait_ge(var_ready, b + 1)
                dve.wait_ge(rstd_ready, b + 1)
                wait(dve, x_turned, b)
                for it in range(NT):
                    last = nc.vector.tensor_scalar(t.xn[:, it, 0:D], t.h_new[:, it * D:(it + 1) * D],
                                                   t.mv[:, it, 0:1], t.rstd[:, it:it + 1], ALU.subtract, ALU.mult)
                last.then_inc(xn_ready, 1)

            def step(r, par):
                b1, b2 = r - 1, r - 2
                if alive(b1, nb):
                    projections(b1, 1 - par)
                if alive(r, nb):
                    take(r, par)
                for n in range(6):
                    if alive(b1, nb):
                        maxima(b1, n)
                    if alive(r, nb):
                        count(r, par, n)
                if alive(b1, nb):
                    negate_max(b1)
                if alive(r, nb):
                    one_hot(r)
                if alive(b2, nb):
                    finish(b2, par)
                if alive(r, nb):
                    receive(r)

            rounds(dve, step, 2, own, nb)

        @block.scalar
        def _(act):
            def projections(b, par):
                n = b * 5
                wait(act, e_ready, (b - 1) * 6)
                for p in range(2):
                    dst = (t.K[:, par], t.Qb(par))
                    for i in range(2):
                        act.wait_ge(pa_ready, n + 2 * p + i + 1)
                        for h in (2 * p, 2 * p + 1):
                            at = D if h % 2 == 0 else 0
                            src = bank[at:at + 32, 2, 0:S]
                            if i == 0:
                                last = nc.scalar.copy(t.K[at:at + 32, par, h, :], src)
                            else:
                                last = nc.scalar.copy(t.Qb(par)[at:at + 32, h, :, :],
                                                      src.rearrange("p (o q) -> p o q", o=1).to_broadcast((32, 2, S)))
                        last.then_inc(pa_free, 1)
                act.wait_ge(pa_ready, n + 5)
                wait(act, pv_done, (b - 1) * 6)
                nc.scalar.copy(flat3(t.v_aug[:, par]), bank[0:TP, 2, 0:NT * 128]).then_inc(pa_free, 1)

            def exponentials(b, n):
                act.wait_ge(e_ready, b * 6 + n + 1)
                wait(act, pv_done, b * 6 + n - 2)
                nc.scalar.activation(t.E[:, n % 3], bank[0:TP, 4:6, 0:4 * TP], ACT.Exp,
                                     scale=float(D) ** -0.5).then_inc(e_done, 1)

            def finish(b):
                act.wait_ge(pv_done, b * 6 + 6)
                wait(act, ctx_turned, b)
                nc.scalar.copy(t.cT[:], bank[:, 3, 0:S]).then_inc(cT_ready, 1)
                act.wait_ge(ctxT_turned, b + 1)
                wait(act, out_ready, b)
                nc.scalar.copy(t.ctxT[0:D, :], bank[0:D, 3, 0:S]).then_inc(ctxT_ready, 1)

            def keep_max(b, par):
                act.wait_ge(neg_turned, b + 1)
                wait(act, e_ready, (b - 1) * 6)
                nc.scalar.copy(t.maxT[:, par, :], bank[0:96, 2, 0:S]).then_inc(maxT_ready, 1)
                act.wait_ge(snext_ready, b + 1)
                wait(act, out_added, b - 1)
                nc.scalar.activation(t.e_next[:, par, :], flat3(t.s_next[:]), ACT.Exp,
                                     scale=float(D) ** -0.5).then_inc(enext_ready, 1)

            def receive(b, par):
                act.wait_ge(x_turned, b + 1)
                wait(act, pv_ready, (b - 1) * 6)
                nc.scalar.activation(t.xT[0:D, par, 0:S], bank[0:D, 0, 0:S], ACT.Identity, bias=W("beta"),
                                     scale=W("gamma")).then_inc(xT_ready, 1)

            def step(r, par):
                b1, b2 = r - 1, r - 2
                if alive(b1, nb):
                    projections(b1, 1 - par)
                if alive(b2, nb):
                    for n in range(6):
                        exponentials(b2, n)
                    finish(b2)
                if alive(b1, nb):
                    keep_max(b1, 1 - par)
                if alive(r, nb):
                    receive(r, par)

            rounds(act, step, 2, Tally(own_act), nb)

        @block.gpsimd
        def _(pool):
            own = Tally(own_pool)

            def rotations(b, par):
                wait(pool, e_ready, (b - 1) * 6)
                for p in range(2):
                    pool.wait_ge(pv_free, b * 6 + 2 * p + 2)
                    for h in (2 * p, 2 * p + 1):
                        at = 0 if h % 2 == 0 else D
                        for part, cols in ((0, S), (1, S - 1)):
                            a = t.rot[at:at + D, 2 * part, 0:cols]
                            c = t.rot[at:at + D, 2 * part + 1, 0:cols]
                            last = nc.gpsimd.tensor_tensor(t.Qb(par)[at:at + D, h, part, 0:cols], a, c, ALU.add)
                    last.then_inc(Q_rows, 1)

            def normalise(b):
                pool.wait_ge(var_ready, b + 1)
                own.link(pool, nc.gpsimd.tensor_tensor(t.rstd[:], t.mv[:, :, 1], F("one_eps")[:, 0:NT], ALU.mult))
                own.link(pool, nc.gpsimd.tensor_tensor(t.rstd[:], t.rstd[:], F("eps_eps")[:, 0:NT], ALU.add))
                nc.gpsimd.tensor_tensor(t.rstd[:], t.rstd[:], k.half[:, 0:NT], ALU.pow).then_inc(rstd_ready, 1)

            def step(r, par):
                if alive(r - 1, nb):
                    rotations(r - 1, 1 - par)
                if alive(r, nb):
                    normalise(r)

            rounds(pool, step, 2, own, nb)




class Norm:

    def __init__(self, k, ctx, phase):
        nc = k.nc
        sb = lambda name, shape, dt=F32: ctx.enter_context(nc.sbuf_tensor(phase + name, shape, dt))
        sem = lambda n: k.sem(phase + n)
        self.k = k
        self.carry = sb("carry", [TP, 1])
        self.h, self.stats, self.mv = sb("h_loc", [TP, NT * D]), sb("stats", [TP, NT, 6]), sb("mean_var", [TP, NT, 2])
        self.rstd, self.xn, self.xT = sb("rstd", [TP, NT]), sb("xn", [TP, NT, 128]), sb("xT", [96, 2, S])
        self.copied, self.summed, self.var, self.root = sem("copied"), sem("summed"), sem("var"), sem("root")
        self.root_own, self.applied, self.turned, self.kept = sem("root_own"), sem("applied"), sem("turned"), sem("kept")

    def clear(self, dve, own):
        nc = self.k.nc
        own.link(dve, nc.vector.memset(self.xT[:], 0.0))
        own.up(nc.vector.memset(self.xT[D:D + 1], 1.0))
        own.up(nc.vector.memset(self.xn[:, :, D:], 0.0))

    def start(self, dve, b):
        nc = self.k.nc
        wait(dve, self.applied, b)
        nc.vector.tensor_scalar(self.h[:], one(self.k.h, b), 1.0, None, ALU.mult).then_inc(self.copied, 1)
        dve.wait_ge(self.copied, b + 1)
        for it in range(NT):
            last = nc.vector.bn_stats(self.stats[:, it, :], self.h[:, it * D:(it + 1) * D])
        last.then_inc(self.summed, 1)
        dve.wait_ge(self.summed, b + 1)
        nc.vector.memset(self.carry[:], 0.0)
        for it in range(NT):
            last = nc.vector.bn_aggr(self.mv[:, it, :], self.stats[:, it, :])
        last.then_inc(self.var, 1)

    def take_root(self, pool, b):
        nc = self.k.nc
        pool.wait_ge(self.var, b + 1)
        nc.gpsimd.tensor_tensor(self.rstd[:], self.mv[:, :, 1], self.k.F("eps")[:, 0:NT], ALU.add).then_inc(self.root_own, 1)
        pool.wait_ge(self.root_own, b + 1)
        nc.gpsimd.tensor_tensor(self.rstd[:], self.rstd[:], self.k.half[:, 0:NT], ALU.pow).then_inc(self.root, 1)

    def apply(self, dve, b):
        nc = self.k.nc
        dve.wait_ge(self.var, b + 1)
        dve.wait_ge(self.root, b + 1)
        wait(dve, self.turned, b)
        for it in range(NT):
            last = nc.vector.tensor_scalar(self.xn[:, it, 0:D], self.h[:, it * D:(it + 1) * D], self.mv[:, it, 0:1],
                                           self.rstd[:, it:it + 1], ALU.subtract, ALU.mult)
        last.then_inc(self.applied, 1)

    def turn(self, pe, b):
        nc, k = self.k.nc, self.k
        pe.wait_ge(self.applied, b + 1)
        for it in range(NT):
            last = nc.tensor.transpose(k.bank[:, 0, it * TP:(it + 1) * TP], self.xn[:, it, :],
                                       k.F("ident")[0:TP, 0:TP])
        last.then_inc(self.turned, 1)

    def keep(self, act, b, par, users):
        nc, k = self.k.nc, self.k
        act.wait_ge(self.turned, b + 1)
        for s, value in users:
            wait(act, s, value)
        nc.scalar.copy(self.xT[0:D, par, :], k.bank[0:D, 0, 0:S]).then_inc(self.kept, 1)




def experts(k):
    nc, nb, F, B, W, bank = k.nc, k.nb, k.F, k.B, k.W, k.bank
    with ExitStack() as ctx:
        sb = lambda name, shape, dt=F32: ctx.enter_context(nc.sbuf_tensor("x_" + name, shape, dt))
        sem = lambda n: k.sem("x_" + n)
        norm = Norm(k, ctx, "xn_")
        top, shifted, prob = sb("top", [TP, NT]), sb("shifted", [TP, NT * NE]), sb("prob", [TP, NT * NE])
        total = sb("total", [TP, NT])
        ahead, same = sb("ahead", [TP, NT, NE, NE], BF16), sb("same", [TP, NT, NE, NE], BF16)
        rank, cw, rest = sb("rank", [TP, NT * NE]), sb("cw", [TP, NT, NE]), sb("rest", [TP, NT, NE])
        parts = sb("parts", [TP, NT, 3 * NE], BF16)
        partsT, partsTf = sb("partsT", [96, 2, S], BF16), sb("partsTf", [3 * NE, 2, S])
        hid, hidw = sb("hidden", [DE, 3, S]), sb("hidden_w", [DE, 3, S])
        yT = sb("yT", [128, S])
        logits, shift_ready, exp_ready, cw_ready, cw_turned, cw_kept = map(
            sem, ("logits", "shift", "exp", "cw", "cw_turned", "cw_kept"))
        hid_ready, gelu_done, spread, weighed, down = map(sem, ("hid", "gelu", "spread", "weighed", "down"))
        y_kept, out_ready, added, own_dve = map(sem, ("y_kept", "out", "added", "own_dve"))
        own_x = [Tally(sem("own" + n)) for n in ("pe", "act", "pool")]
        cleared = sem("cleared")
        block = ctx.enter_context(nc.Block())

        @block.tensor
        def _(pe):
            pe.wait_ge(cleared, 1)

            def up(b, par, e):
                n = b * NE + e
                if e == 0:
                    pe.wait_ge(norm.kept, b + 1)
                    pe.wait_ge(cw_kept, b + 1)
                wait(pe, gelu_done, n - 1)
                nc.tensor.matmul(bank[:, 2 + e % 2, 0:S], W("w1")[:, e, :], norm.xT[:, par, :], start=True,
                                 stop=True).then_inc(hid_ready, 1)
                wait(pe, weighed, n - 1)
                nc.tensor.matmul(bank[:, 4 + e % 2, 0:S], B("pick_expert")[:, e, :], partsT[:, par, :], start=True,
                                 stop=True).then_inc(spread, 1)

            def go_down(b, e):
                n = b * NE + e
                pe.wait_ge(weighed, n + 1)
                if e == 0:
                    wait(pe, y_kept, b)
                at = D * (e % 2)
                nc.tensor.matmul(bank[at:at + D, 6, 0:S], W("w2")[:, e, :], hidw[:, e % 2, :], start=e < 2,
                                 stop=e >= NE - 2, skip_group_check=True).then_inc(down, 1)

            def gate(b, par):
                pe.wait_ge(norm.kept, b + 1)
                wait(pe, cw_kept, b)
                for it in range(NT):
                    last = nc.tensor.matmul(bank[0:TP, 1, it * NE:(it + 1) * NE], norm.xT[:, par, it * TP:(it + 1) * TP],
                                            W("gate_w"), start=True, stop=True)
                last.then_inc(logits, 1)

            def turn_weights(b):
                pe.wait_ge(cw_ready, b + 1)
                for it in range(NT):
                    last = nc.tensor.matmul(bank[0:3 * NE, 1, it * TP:(it + 1) * TP], parts[:, it, :],
                                            B("ident_b")[0:TP, 0:TP], start=True, stop=True)
                last.then_inc(cw_turned, 1)

            def finish(b, par):
                pe.wait_ge(y_kept, b + 1)
                wait(pe, added, b)
                for it in range(NT):
                    cols = slice(it * TP, (it + 1) * TP)
                    nc.tensor.matmul(bank[0:TP, 7, it * D:(it + 1) * D], yT[:, cols], F("two_halves"), start=True,
                                     stop=False, skip_group_check=True)
                    last = nc.tensor.matmul(bank[0:TP, 7, it * D:(it + 1) * D], partsTf[:, par, cols], W("b2"),
                                            start=False, stop=True, skip_group_check=True)
                last.then_inc(out_ready, 1)

            def step(r, par):
                b = r - 1
                for e in range(NE):
                    if alive(b, nb):
                        up(b, 1 - par, e)
                        if e >= 1:
                            go_down(b, e - 1)
                    if alive(r, nb) and e == 2:
                        norm.turn(pe, r)
                    if alive(r, nb) and e == 4:
                        gate(r, par)
                if alive(b, nb):
                    go_down(b, NE - 1)
                    finish(b, 1 - par)
                if alive(r, nb):
                    turn_weights(r)

            rounds(pe, step, 1, own_x[0], nb)

        @block.scalar
        def _(act):
            def gelu(b, e):
                n = b * NE + e
                act.wait_ge(hid_ready, n + 1)
                wait(act, weighed, n - 1)
                nc.scalar.activation(hid[:, e % 2, :], bank[:, 2 + e % 2, 0:S], ACT.Gelu).then_inc(gelu_done, 1)

            def keep_weights(b, par):
                act.wait_ge(cw_turned, b + 1)
                wait(act, spread, (b - 1) * NE)
                nc.scalar.copy(partsT[0:3 * NE, par, :], bank[0:3 * NE, 1, 0:S])
                wait(act, out_ready, b - 1)
                nc.scalar.copy(partsTf[:, par, :], bank[0:3 * NE, 1, 0:S]).then_inc(cw_kept, 1)

            def step(r, par):
                b = r - 1
                for e in range(NE):
                    if alive(b, nb):
                        gelu(b, e)
                    if alive(r, nb) and e == 2:
                        norm.keep(act, r, par, [(hid_ready, (r - 1) * NE), (logits, r - 1)])
                if alive(b, nb):
                    act.wait_ge(down, b * NE + NE)
                    wait(act, out_ready, b)
                    nc.scalar.copy(yT[:], bank[:, 6, 0:S]).then_inc(y_kept, 1)
                if alive(r, nb):
                    keep_weights(r, par)

            rounds(act, step, 1, own_x[1], nb)

        @block.vector
        def _(dve):
            own = Tally(own_dve)
            norm.clear(dve, own)
            nc.vector.memset(partsT[:], 0.0).then_inc(cleared, 1)

            def weigh(b, e):
                n = b * NE + e
                dve.wait_ge(spread, n + 1)
                dve.wait_ge(gelu_done, n + 1)
                wait(dve, down, n - 1)
                nc.vector.tensor_tensor(hidw[:, e % 2, :], bank[:, 4 + e % 2, 0:S], hid[:, e % 2, :],
                                        ALU.mult).then_inc(weighed, 1)

            v3 = lambda a: a.rearrange("p (t e) -> p t e", t=NT)
            over_e = lambda a: a.rearrange("p (t o) -> p t o", o=1).to_broadcast((TP, NT, NE))

            def shift(b):
                dve.wait_ge(logits, b + 1)
                wait(dve, exp_ready, b)
                lg = bank[0:TP, 1, 0:NT * NE]
                own.link(dve, nc.vector.tensor_reduce(top[:], v3(lg), AX, ALU.max))
                nc.vector.tensor_tensor(v3(shifted[:]), v3(lg), over_e(top[:]), ALU.subtract).then_inc(shift_ready, 1)

            def choose(b):
                dve.wait_ge(exp_ready, b + 1)
                own.link(dve, nc.vector.tensor_reduce(total[:], v3(prob[:]), AX, ALU.add))
                own.link(dve, nc.vector.reciprocal(total[:], total[:]))
                own.link(dve, nc.vector.tensor_tensor(v3(prob[:]), v3(prob[:]), over_e(total[:]), ALU.mult))
                other = prob[:].rearrange("p (t o e) -> p t o e", t=NT, o=1).to_broadcast((TP, NT, NE, NE))
                mine = prob[:].rearrange("p (t e o) -> p t e o", t=NT, o=1).to_broadcast((TP, NT, NE, NE))
                own.up(nc.vector.tensor_tensor(same[:], other, mine, ALU.is_equal))
                own.link(dve, nc.vector.tensor_tensor(ahead[:], other, mine, ALU.is_gt))
                early = B("earlier").rearrange("p (o e) -> p o e", o=1).to_broadcast((TP, NT, NE * NE))
                sf = same[:].rearrange("p t a b -> p t (a b)")
                own.link(dve, nc.vector.tensor_tensor(sf, sf, early, ALU.mult))
                own.link(dve, nc.vector.tensor_tensor(ahead[:], ahead[:], same[:], ALU.add))
                own.link(dve, nc.vector.tensor_reduce(rank[:], ahead[:].rearrange("p t a b -> p (t a) b"), AX, ALU.add))
                own.link(dve, nc.vector.scalar_tensor_tensor(cw[:].rearrange("p t e -> p (t e)"), rank[:], 2.0, prob[:],
                                                             ALU.is_lt, ALU.mult))
                wait(dve, cw_turned, b)
                own.link(dve, nc.vector.tensor_copy(parts[:, :, 0:NE], cw[:]))
                own.link(dve, nc.vector.tensor_tensor(rest[:], cw[:], parts[:, :, 0:NE], ALU.subtract))
                own.link(dve, nc.vector.tensor_copy(parts[:, :, NE:2 * NE], rest[:]))
                nc.vector.tensor_tensor(parts[:, :, 2 * NE:], rest[:], parts[:, :, NE:2 * NE],
                                        ALU.subtract).then_inc(cw_ready, 1)

            def step(r, par):
                b = r - 1
                if alive(r, nb):
                    norm.start(dve, r)
                for e in range(NE):
                    if alive(b, nb):
                        weigh(b, e)
                    if alive(r, nb) and e == 0:
                        norm.apply(dve, r)
                    if alive(r, nb) and e == 4:
                        shift(r)
                if alive(r, nb):
                    choose(r)
                if alive(b, nb):
                    dve.wait_ge(out_ready, b + 1)
                    h = one(k.h, b)
                    nc.vector.tensor_tensor(h, h, bank[0:TP, 7, 0:NT * D], ALU.add).then_inc(added, 1)

            rounds(dve, step, 1, own, nb)

        @block.gpsimd
        def _(pool):
            def step(r, par):
                if alive(r, nb):
                    norm.take_root(pool, r)
                    pool.wait_ge(shift_ready, r + 1)
                    wait(pool, cw_ready, r)
                    nc.gpsimd.tensor_tensor(prob[:], F("euler"), shifted[:], ALU.pow).then_inc(exp_ready, 1)

            rounds(pool, step, 1, own_x[2], nb)




def slices(k):
    nc, nb, F, B, W, bank = k.nc, k.nb, k.F, k.B, k.W, k.bank
    R = HS * DS1
    with ExitStack() as ctx:
        sb = lambda name, shape, dt=F32: ctx.enter_context(nc.sbuf_tensor("s_" + name, shape, dt))
        sem = lambda n: k.sem("s_" + n)
        norm = Norm(k, ctx, "sn_")
        WL, MB, rtemp = sb("WL", [96, HS * G]), sb("MB", [R, R]), sb("rtemp", [96, HS])
        top, neg, maxT = sb("top", [TP, NT * HS]), sb("neg", [TP, NT, 96], BF16), sb("maxT", [96, S], BF16)
        E, ET = sb("E", [TP, NT, HS * G]), sb("ET", [128, 2, PS, S])
        rsum, sumv, tin = sb("rsum", [TP, 2, NT * HS]), sb("sum", [TP, NT * HS]), sb("tin", [TP, NT * HS, DS1])
        rnorm, tok, tokT, bothT = sb("rnorm", [128, PS]), sb("tok", [128, 128]), sb("tokT", [R, 128]), sb("bothT", [R, G])
        keys, kq, vals = sb("keys", [R, PS, G]), sb("kq", [R, 128]), sb("vals", [128, PS * DS])
        topA, shA, EA, EAT = sb("topA", [128, PS]), sb("shA", [128, PS, G]), sb("EA", [128, PS, 128]), sb("EAT", [128, PS * 128])
        sumA, OB = sb("sumA", [128, PS]), sb("OB", [128, PS, 2 * DS])
        att, attT = sb("att", [TP, NT, 128]), sb("attT", [96, S])
        set_up, folded, folded_kept = sem("set_up"), sem("folded"), sem("folded_kept")
        t_ready, l_ready, topped, neg_ready, max_turned, max_kept = map(
            sem, ("t", "logits", "topped", "neg", "max_turned", "max_kept"))
        lm_ready, e_done, g_ready, eT_done, summed, tin_ready, sl_ready = map(
            sem, ("less_max", "e", "g", "eT", "summed", "tin", "slices"))
        tok_ready, tok_turned, tokT_ready, keys_ready, kqv_ready, kq_kept, s_ready = map(
            sem, ("tok", "tok_turned", "tokT", "keys", "kqv", "kq_kept", "scores"))
        shA_ready, eA_done, eA_turned, eAT_kept, o_ready, OB_ready, out_ready = map(
            sem, ("shA", "eA", "eA_turned", "eAT", "o", "OB", "out"))
        att_ready, att_turned, attT_kept, res_ready, added, own_dve = map(
            sem, ("att", "att_turned", "attT", "res", "added", "own_dve"))
        own_x = [Tally(sem("own" + n)) for n in ("pe", "act", "pool")]
        block = ctx.enter_context(nc.Block())
        tile = lambda v, par, it: v[:, par, it * TP:(it + 1) * TP]

        @block.tensor
        def _(pe):
            for h in range(HS):
                nc.tensor.matmul(bank[0:D + 1, 6, h * G:(h + 1) * G], W("w_inT")[:, h, :], W("w_slice"),
                                 start=True, stop=True)
            nc.tensor.matmul(bank[0:R, 7, 0:R], W("wq_sT"), W("wk_sT"), start=True, stop=True).then_inc(folded, 1)
            pe.wait_ge(set_up, 1)
            pe.wait_ge(folded_kept, 1)

            def logits(b, par):
                pe.wait_ge(norm.kept, b + 1)
                wait(pe, tok_ready, b)
                for it in range(NT):
                    last = nc.tensor.matmul(bank[0:TP, 1, it * D:(it + 1) * D], tile(norm.xT, par, it), W("w_in"),
                                            start=True, stop=True)
                last.then_inc(t_ready, 1)
                wait(pe, e_done, b)
                for it in range(NT):
                    last = nc.tensor.matmul(bank[0:TP, 2 + it, :], tile(norm.xT, par, it), WL[:], start=True,
                                            stop=False, skip_group_check=True)
                    last.then_inc(l_ready, 1)

            def turn_max(b):
                pe.wait_ge(neg_ready, b + 1)
                wait(pe, eT_done, b * PS)
                for it in range(NT):
                    last = nc.tensor.matmul(bank[0:96, 6, it * TP:(it + 1) * TP], neg[:, it, :],
                                            B("ident_b")[0:TP, 0:TP], start=True, stop=True)
                last.then_inc(max_turned, 1)

            def less_max(b):
                pe.wait_ge(max_kept, b + 1)
                for it in range(NT):
                    last = nc.tensor.matmul(bank[0:TP, 2 + it, :], maxT[:, it * TP:(it + 1) * TP], B("pick_slices"),
                                            start=False, stop=True, skip_group_check=True)
                last.then_inc(lm_ready, 1)

            def turned_logits(b, par, p):
                wait(pe, eT_done, b * PS + p - 1)
                cols = slice(p * 128, (p + 1) * 128)
                nc.tensor.matmul(bank[:, 6 + p % 2, 0:S], WL[:, cols], norm.xT[:, par, 0:S], start=True, stop=False,
                                 skip_group_check=True)
                nc.tensor.matmul(bank[:, 6 + p % 2, 0:S], B("pick_slices")[:, cols], maxT[:], start=False, stop=True,
                                 skip_group_check=True).then_inc(g_ready, 1)

            def gather_slices(b):
                pe.wait_ge(tin_ready, b + 1)
                flat = tin[:].rearrange("p (t h) d -> p t (h d)", t=NT)
                for p in range(PS):
                    for it in range(NT):
                        last = nc.tensor.matmul(bank[:, 1, p * 2 * DS1:(p + 1) * 2 * DS1],
                                                E[:, it, p * 128:(p + 1) * 128],
                                                flat[:, it, p * 2 * DS1:(p + 1) * 2 * DS1],
                                                start=it == 0, stop=it == NT - 1)
                last.then_inc(sl_ready, 1)

            def turn_tokens(b):
                pe.wait_ge(tok_ready, b + 1)
                wait(pe, added, b)
                nc.tensor.transpose(bank[:, 5, 0:128], tok[:], F("ident")).then_inc(tok_turned, 1)

            def project(b):
                pe.wait_ge(tokT_ready, b + 1)
                nc.tensor.matmul(bank[0:R, 5, 0:128], MB[:], tokT[:], start=True, stop=True)
                nc.tensor.matmul(bank[:, 5, 128:128 + PS * DS], tokT[:], W("wv_s"), start=True,
                                 stop=True).then_inc(kqv_ready, 1)

            def scores(b):
                pe.wait_ge(kq_kept, b + 1)
                pe.wait_ge(keys_ready, b + 1)
                nc.tensor.matmul(bank[:, 5, 0:PS * G], kq[:], keys[:].rearrange("p a g -> p (a g)"), start=True,
                                 stop=True).then_inc(s_ready, 1)

            def turn_attention(b):
                pe.wait_ge(eA_done, b + 1)
                for p in range(PS):
                    last = nc.tensor.transpose(bank[:, 5, p * 128:(p + 1) * 128], EA[:, p, :], F("ident"))
                last.then_inc(eA_turned, 1)

            def attend(b):
                pe.wait_ge(eAT_kept, b + 1)
                for p in range(PS):
                    last = nc.tensor.matmul(bank[:, 5, p * DS:(p + 1) * DS], EAT[:, p * 128:(p + 1) * 128],
                                            vals[:, p * DS:(p + 1) * DS], start=True, stop=True)
                last.then_inc(o_ready, 1)

            def spread(b, par):
                pe.wait_ge(OB_ready, b + 1)
                for it in range(NT):
                    for p in range(PS):
                        at = it * D + p * 2 * DS
                        last = nc.tensor.matmul(bank[0:TP, 5, at:at + 2 * DS], ET[:, par, p, it * TP:(it + 1) * TP],
                                                OB[:, p, :], start=True, stop=True)
                last.then_inc(out_ready, 1)

            def turn_out(b):
                pe.wait_ge(att_ready, b + 1)
                for it in range(NT):
                    last = nc.tensor.transpose(bank[:, 5, it * TP:(it + 1) * TP], att[:, it, :], F("ident")[0:TP, 0:TP])
                last.then_inc(att_turned, 1)

            def project_out(b):
                pe.wait_ge(attT_kept, b + 1)
                for it in range(NT):
                    last = nc.tensor.matmul(bank[0:TP, 5, it * D:(it + 1) * D], attT[:, it * TP:(it + 1) * TP],
                                            W("w_out_s"), start=True, stop=True)
                last.then_inc(res_ready, 1)

            def step(r, par):
                b1, b2 = r - 1, r - 2
                one_, two = alive(b1, nb), alive(b2, nb)
                if one_:
                    logits(b1, 1 - par)
                if two:
                    turn_tokens(b2)
                if one_:
                    turn_max(b1)
                if two:
                    project(b2)
                if one_:
                    less_max(b1)
                    turned_logits(b1, 1 - par, 0)
                    turned_logits(b1, 1 - par, 1)
                if two:
                    scores(b2)
                if one_:
                    turned_logits(b1, 1 - par, 2)
                    turned_logits(b1, 1 - par, 3)
                if two:
                    turn_attention(b2)
                    attend(b2)
                if one_:
                    gather_slices(b1)
                if two:
                    spread(b2, par)
                if alive(r, nb):
                    norm.turn(pe, r)
                if two:
                    turn_out(b2)
                    project_out(b2)

            rounds(pe, step, 2, own_x[0], nb)

        @block.scalar
        def _(act):
            def keep_max(b):
                act.wait_ge(max_turned, b + 1)
                wait(act, g_ready, b * PS)
                nc.scalar.copy(maxT[:], bank[0:96, 6, 0:S]).then_inc(max_kept, 1)

            def exps(b):
                act.wait_ge(lm_ready, b + 1)
                wait(act, sl_ready, b)
                nc.scalar.activation(E[:], bank[0:TP, 2:5, :], ACT.Exp).then_inc(e_done, 1)

            def turned_exps(b, par, p):
                act.wait_ge(g_ready, b * PS + p + 1)
                wait(act, out_ready, b - 1)
                nc.scalar.activation(ET[:, par, p, :], bank[:, 6 + p % 2, 0:S], ACT.Exp).then_inc(eT_done, 1)

            def keep_projected(b):
                act.wait_ge(kqv_ready, b + 1)
                wait(act, o_ready, b)
                nc.scalar.copy(kq[:], bank[0:R, 5, 0:128])
                nc.scalar.copy(vals[:], bank[:, 5, 128:128 + PS * DS]).then_inc(kq_kept, 1)

            def attention_exps(b):
                act.wait_ge(shA_ready, b + 1)
                wait(act, OB_ready, b)
                for hh in range(2):
                    rows = slice(hh * G, (hh + 1) * G)
                    last = nc.scalar.activation(EA[rows, :, rows], shA[rows], ACT.Exp)
                last.then_inc(eA_done, 1)

            def step(r, par):
                b1, b2 = r - 1, r - 2
                one_, two = alive(b1, nb), alive(b2, nb)
                if one_:
                    keep_max(b1)
                if two:
                    keep_projected(b2)
                if one_:
                    exps(b1)
                    turned_exps(b1, 1 - par, 0)
                    turned_exps(b1, 1 - par, 1)
                if two:
                    attention_exps(b2)
                if one_:
                    turned_exps(b1, 1 - par, 2)
                    turned_exps(b1, 1 - par, 3)
                if two:
                    act.wait_ge(eA_turned, b2 + 1)
                    wait(act, o_ready, b2)
                    nc.scalar.copy(EAT[:], bank[:, 5, :]).then_inc(eAT_kept, 1)
                if alive(r, nb):
                    norm.keep(act, r, par, [(g_ready, (r - 1) * PS)])
                if two:
                    act.wait_ge(att_turned, b2 + 1)
                    wait(act, res_ready, b2)
                    nc.scalar.copy(attT[0:D, :], bank[0:D, 5, 0:S]).then_inc(attT_kept, 1)

            rounds(act, step, 2, own_x[1], nb)

        @block.vector
        def _(dve):
            own = Tally(own_dve)
            norm.clear(dve, own)
            own.up(nc.vector.memset(WL[:], 0.0))
            own.up(nc.vector.memset(neg[:], 0.0))
            own.up(nc.vector.memset(att[:], 0.0))
            own.up(nc.vector.memset(EA[:], 0.0))
            own.up(nc.vector.memset(OB[:], 0.0))
            own.up(nc.vector.memset(tok[:], 0.0))
            own.link(dve, nc.vector.memset(attT[:], 0.0))
            own.up(nc.vector.memset(attT[D:D + 1], 1.0))
            owned = tok[:, 0:R].rearrange("p (a e) -> p a e", a=PS)
            for hh in range(2):
                at = hh * DS1 + DS
                own.up(nc.vector.memset(owned[hh * G:(hh + 1) * G, :, at:at + 1], 1.0))
            own.link(dve, nc.vector.reciprocal(rtemp[:], W("temperature")))
            dve.wait_ge(folded, 1)
            own.up(nc.vector.tensor_tensor(WL[0:D + 1].rearrange("p (h g) -> p h g", h=HS),
                                           bank[0:D + 1, 6, :].rearrange("p (h g) -> p h g", h=HS),
                                           rtemp[0:D + 1].rearrange("p (h o) -> p h o", o=1)
                                           .to_broadcast((D + 1, HS, G)), ALU.mult))
            nc.vector.tensor_tensor(MB[:], bank[0:R, 7, 0:R], F("slice_block"), ALU.mult).then_inc(folded_kept, 1)
            nc.vector.memset(norm.carry[:], 0.0).then_inc(set_up, 1)

            def maxima(b):
                for it in range(NT):
                    dve.wait_ge(l_ready, b * NT + it + 1)
                    wait(dve, neg_ready, b)
                    last = nc.vector.tensor_reduce(top[:, it * HS:(it + 1) * HS],
                                                   bank[0:TP, 2 + it, :].rearrange("p (h g) -> p h g", h=HS), AX, ALU.max)
                last.then_inc(topped, 1)
                dve.wait_ge(topped, b + 1)
                wait(dve, max_turned, b)
                nc.vector.tensor_scalar(neg[:, :, 0:HS], top[:].rearrange("p (t h) -> p t h", t=NT), -1.0, None,
                                        ALU.mult).then_inc(neg_ready, 1)

            def divide(b, par):
                dve.wait_ge(e_done, b + 1)
                own.link(dve, nc.vector.tensor_reduce(sumv[:], E[:].rearrange("p t (h g) -> p (t h) g", h=HS), AX, ALU.add))
                wait(dve, att_ready, b - 1)
                own.link(dve, nc.vector.reciprocal(rsum[:, par, :], sumv[:]))
                r = rsum[:, par, :].rearrange("p (a o) -> p a o", o=1)
                dve.wait_ge(t_ready, b + 1)
                wait(dve, sl_ready, b)
                nc.vector.tensor_tensor(tin[:, :, 0:DS], bank[0:TP, 1, 0:NT * D].rearrange("p (a d) -> p a d", d=DS),
                                        r.to_broadcast((TP, NT * HS, DS)), ALU.mult)
                nc.vector.tensor_copy(tin[:, :, DS:DS1], r).then_inc(tin_ready, 1)

            def slice_tokens(b):
                dve.wait_ge(sl_ready, b + 1)
                wait(dve, tok_turned, b)
                sl = bank[:, 1, 0:R].rearrange("p (a e) -> p a e", a=PS)
                for hh in range(2):
                    rows = slice(hh * G, (hh + 1) * G)
                    last = nc.vector.tensor_scalar(rnorm[rows, :], sl[rows, :, hh * DS1 + DS], 1e-5, None, ALU.add)
                own.link(dve, last)
                own.link(dve, nc.vector.reciprocal(rnorm[:], rnorm[:]))
                for hh in range(2):
                    rows, cols = slice(hh * G, (hh + 1) * G), slice(hh * DS1, hh * DS1 + DS)
                    last = nc.vector.tensor_tensor(owned[rows, :, cols], sl[rows, :, cols],
                                                   rnorm[rows, :].rearrange("p (a o) -> p a o", o=1)
                                                   .to_broadcast((G, PS, DS)), ALU.mult)
                last.then_inc(tok_ready, 1)

            def turned_tokens(b):
                dve.wait_ge(tok_turned, b + 1)
                wait(dve, kqv_ready, b)
                nc.vector.tensor_copy(tokT[:], bank[0:R, 5, 0:128])
                wait(dve, s_ready, b)
                own.link(dve, nc.vector.tensor_copy(bothT[:], bank[0:R, 5, 0:G]))
                own.up(nc.vector.tensor_tensor(bothT[:], bothT[:], bank[0:R, 5, G:128], ALU.add))
                own.wait(dve)
                nc.vector.memset(norm.carry[:], 0.0).then_inc(tokT_ready, 1)
                nc.vector.tensor_tensor(keys[:], F("own_pair"), bothT[:].rearrange("p (o g) -> p o g", o=1)
                                        .to_broadcast((R, PS, G)), ALU.mult).then_inc(keys_ready, 1)

            def shift(b):
                dve.wait_ge(s_ready, b + 1)
                sc = bank[:, 5, 0:PS * G].rearrange("p (a g) -> p a g", a=PS)
                own.link(dve, nc.vector.tensor_reduce(topA[:], sc, AX, ALU.max))
                wait(dve, eA_done, b)
                nc.vector.tensor_tensor(shA[:], sc, topA[:].rearrange("p (a o) -> p a o", o=1)
                                        .to_broadcast((128, PS, G)), ALU.subtract).then_inc(shA_ready, 1)

            def attended(b):
                dve.wait_ge(eA_done, b + 1)
                own.link(dve, nc.vector.tensor_reduce(sumA[:], EA[:], AX, ALU.add))
                own.link(dve, nc.vector.reciprocal(sumA[:], sumA[:]))
                dve.wait_ge(o_ready, b + 1)
                wait(dve, out_ready, b)
                o = bank[:, 5, 0:PS * DS].rearrange("p (a d) -> p a d", a=PS)
                for hh in range(2):
                    rows = slice(hh * G, (hh + 1) * G)
                    last = nc.vector.tensor_tensor(OB[rows, :, hh * DS:(hh + 1) * DS], o[rows],
                                                   sumA[rows, :].rearrange("p (a o) -> p a o", o=1)
                                                   .to_broadcast((G, PS, DS)), ALU.mult)
                last.then_inc(OB_ready, 1)

            def out(b, par):
                dve.wait_ge(out_ready, b + 1)
                wait(dve, att_turned, b)
                for it in range(NT):
                    last = nc.vector.tensor_tensor(
                        att[:, it, 0:D].rearrange("p (h d) -> p h d", h=HS),
                        bank[0:TP, 5, it * D:(it + 1) * D].rearrange("p (h d) -> p h d", h=HS),
                        rsum[:, par, it * HS:(it + 1) * HS].rearrange("p (h o) -> p h o", o=1)
                        .to_broadcast((TP, HS, DS)), ALU.mult)
                last.then_inc(att_ready, 1)

            def step(r, par):
                b1, b2 = r - 1, r - 2
                one_, two = alive(b1, nb), alive(b2, nb)
                if alive(r, nb):
                    norm.start(dve, r)
                if two:
                    slice_tokens(b2)
                if one_:
                    maxima(b1)
                if two:
                    turned_tokens(b2)
                if alive(r, nb):
                    norm.apply(dve, r)
                if two:
                    shift(b2)
                if one_:
                    divide(b1, 1 - par)
                if two:
                    attended(b2)
                    out(b2, par)
                    dve.wait_ge(res_ready, b2 + 1)
                    h = one(k.h, b2)
                    nc.vector.tensor_tensor(h, h, bank[0:TP, 5, 0:NT * D], ALU.add).then_inc(added, 1)

            rounds(dve, step, 2, own, nb)

        @block.gpsimd
        def _(pool):
            def step(r, par):
                if alive(r, nb):
                    norm.take_root(pool, r)

            rounds(pool, step, 2, own_x[2], nb)




def first_heads(k, res):
    nc, W, bank = k.nc, k.W, k.bank
    with ExitStack() as ctx:
        norm = Norm(k, ctx, "f_")
        ready, read, own_dve = k.sem("f_ready"), k.sem("f_read"), k.sem("f_own_dve")
        block = ctx.enter_context(nc.Block())

        @block.vector
        def _(dve):
            norm.clear(dve, Tally(own_dve))
            for b in range(HE):
                norm.start(dve, b)
                norm.apply(dve, b)
                dve.wait_ge(ready, b + 1)
                nc.vector.tensor_copy(res[:, :, b * DH2:(b + 1) * DH2],
                                      bank[0:TP, 1, 0:NT * DH2].rearrange("p (t d) -> p t d", t=NT)).then_inc(read, 1)

        @block.gpsimd
        def _(pool):
            for b in range(HE):
                norm.take_root(pool, b)

        @block.tensor
        def _(pe):
            for b in range(HE):
                norm.turn(pe, b)
                pe.wait_ge(norm.kept, b + 1)
                wait(pe, read, b)
                for it in range(NT):
                    last = nc.tensor.matmul(bank[0:TP, 1, it * DH2:(it + 1) * DH2],
                                            norm.xT[:, b % 2, it * TP:(it + 1) * TP],
                                            W("w_sx")[:, b * DH2:(b + 1) * DH2], start=True, stop=True)
                last.then_inc(ready, 1)

        @block.scalar
        def _(act):
            for b in range(HE):
                norm.keep(act, b, b % 2, [(ready, b - 1)])


def query_experts(k, res, qk_dram, out):
    nc, nb, F, B, W, bank = k.nc, k.nb, k.F, k.B, k.W, k.bank
    rounds_of = [(0, (0, 1), 3 * TP, 1), (0, (2, 3), 3 * TP, 1), (1, (0, 1, 2, 3), 2 * TP, 2), (2, (0, 1, 2, 3), TP, 4)]
    NU = EE * len(rounds_of)
    NP = 3
    q_parts, k_parts = (0, 0, 1, 0, 1, 2), (0, 1, 0, 2, 1, 0)
    RS = len(q_parts) * DH2
    with ExitStack() as ctx:
        sb = lambda name, shape, dt=F32: ctx.enter_context(nc.sbuf_tensor("qe_" + name, shape, dt))
        sem = lambda n: k.sem("q_" + n)
        norm = Norm(k, ctx, "qn_")
        WH = sb("WH", [96, NP + 1, 128])
        parts = sb("parts", [128, 3, NP, S], BF16)
        zeros = sb("zeros", [128, S])
        rest = sb("rest", [128, NP, S])
        Q, K = sb("Q", [RS, 3, QE, S], BF16), sb("K", [RS, 3, HE, S], BF16)
        v_aug, nz = sb("v_aug", [TP, 3, NT, 128]), sb("nz", [128, 3, S])
        top, neg, maxT = sb("top", [TP, NT, QE]), sb("neg", [TP, NT, 96], BF16), sb("maxT", [96, S], BF16)
        E, cT = sb("E", [TP, 3, 2, 512]), sb("cT", [128, EE, S])
        FW = HE * VS + QE
        tok = sb("tok", [TP, NT * EE, FW])
        gsel = sb("gsel", [128, EE, FW])
        rs, gp, gl = sb("rs", [TP, NT * EE, HE]), sb("gp", [TP, NT * EE, QE]), sb("gl", [TP, NT, QE])
        gtop, gex, gsum = sb("gtop", [TP, NT * HE]), sb("gex", [TP, NT * HE, EE]), sb("gsum", [TP, NT * HE])
        wt, wc = sb("wt", [TP, NT, EE, HE]), sb("wc", [TP, NT * EE, D])
        y, sq, mean, var = sb("y", [TP, NT * HE, DH2]), sb("sq", [TP, NT * HE, DH2]), sb("mean", [TP, NT * HE]), sb("var", [TP, NT * HE])
        root = sb("root", [TP, NT * HE])
        fx, fxT = sb("fx", [TP, NT, 128]), sb("fxT", [96, S])
        r1, h1T, fo, foT = sb("r1", [D, S]), sb("h1T", [96, S]), sb("fo", [TP, NT, 128]), sb("foT", [D, S])
        fl, fs = sb("fl", [TP, NT * HE]), sb("fs", [TP, NT])
        hout = sb("hout", [TP, 3, NT * D])
        gamma, beta = sb("gamma", [TP, 2, NT * HE, DH2]), sb("beta", [TP, 2, NT * HE, DH2])
        gb = sb("gb", [TP, NT, QE])

        folded, set_up, p_ready, nz_ready, nz_done, v_kept = map(sem, ("folded", "set_up", "p", "nz", "nz_done", "v_kept"))
        hi_done, rest_ready, parts_done, parts_stored, stacked = map(sem, ("hi", "rest", "parts", "parts_stored", "stacked"))
        m_ready, m_read, neg_ready, neg_turned, maxT_kept = map(sem, ("m", "m_read", "neg", "neg_turned", "maxT"))
        e_ready, e_done, v_done, c_kept = map(sem, ("e", "e_done", "v_done", "c_kept"))
        sel_ready, sel_read, g_ready, gex_done, sq_ready, sq_done, vs_ready, root_done = map(
            sem, ("sel", "sel_read", "g", "gex", "c", "sq", "vs", "root"))
        fx_ready, fx_turned, fxT_kept, h1_ready, r1_done, h1T_ready, h2_ready = map(
            sem, ("fx", "fx_turned", "fxT", "h1", "r1", "h1T", "h2"))
        fo_ready, fo_turned, foT_kept, fl_ready, fs_ready, fex_done, h_ready, stored = map(
            sem, ("fo", "fo_turned", "foT", "fl", "fs", "fex", "h", "stored"))
        own_dve, own_pool = sem("own_dve"), sem("own_pool")
        own_x = [Tally(sem("own" + n)) for n in ("pe", "act", "sp")]
        block = ctx.enter_context(nc.Block())

        def place(u, i):
            tile, heads, cols, per = rounds_of[u]
            return i // per, (i % per) * cols

        @block.sync
        def _(sp):
            rows_of = qk_dram.rearrange("(a d) p i s -> p d a i s", d=DH2)
            keys_of = qk_dram.rearrange("(h a d) p i s -> a p i d h s", a=2, d=DH2)

            def stack(b, par):
                sp.wait_ge(parts_done, (b + 1) * NP)
                sp.dma_start(qk_dram, parts[:]).then_inc(parts_stored, 16)
                sp.wait_ge(parts_stored, (b + 1) * 16)
                wait(sp, e_ready, (b - 2) * NU)
                for g, (qp, kp) in enumerate(zip(q_parts, k_parts)):
                    rows = slice(g * DH2, (g + 1) * DH2)
                    sp.dma_start(Q[rows, par].rearrange("d (a i) s -> d a i s", i=2), rows_of[qp, :, :, 0:2]
                                 ).then_inc(stacked, 16)
                    sp.dma_start(K[rows, par], keys_of[0, kp, 2]).then_inc(stacked, 16)
                sp.wait_ge(stacked, (b + 1) * 32 * len(q_parts))

            def step(r, par):
                b = r - 3
                if alive(r, nb):
                    stack(r, par)
                if alive(b, nb):
                    wait(sp, stored, b * 16)
                    sp.wait_ge(h_ready, (b + 1) * 16)
                    sp.dma_start(out[bass.ds(b, 1)].rearrange("o (c p) f -> p (o c) f", p=TP),
                                 hout[:, par, :].rearrange("p (c f) -> p c f", c=NT)).then_inc(stored, 16)

            rounds(sp, step, 3, own_x[2], nb, 3)
            sp.wait_ge(stored, nb * 16)

        @block.tensor
        def _(pe):
            for e in range(NP + 1):
                last = nc.tensor.matmul(bank[0:D + 1, 4, e * 128:(e + 1) * 128], W("w_sxT"),
                                        W("w_heads")[:, e, :], start=True, stop=True)
            last.then_inc(folded, 1)
            pe.wait_ge(set_up, 1)

            def project(b, i):
                x = norm.xT[:, 0, :]
                if i == 0:
                    pe.wait_ge(norm.kept, b + 1)
                    wait(pe, nz_done, b)
                    wait(pe, maxT_kept, b - 1)
                elif i <= NP:
                    pe.wait_ge(rest_ready, b * NP + i)
                if i < NP:
                    nc.tensor.matmul(bank[:, 1, 0:S], WH[:, i, :], x, start=True, stop=True).then_inc(p_ready, 1)
                elif i == NP:
                    for it in range(NT):
                        last = nc.tensor.matmul(bank[0:TP, 1, it * 128:(it + 1) * 128], x[:, it * TP:(it + 1) * TP],
                                                WH[:, NP, :], start=True, stop=True)
                    last.then_inc(p_ready, 1)
                else:
                    pe.wait_ge(v_kept, b + 1)
                    nc.tensor.matmul(bank[:, 1, 0:S], W("w_sx_wide"), x, start=True, stop=True).then_inc(nz_ready, 1)

            def scores_for_max(b, par, n):
                e, u = divmod(n, 4)
                back, heads, cols, per = rounds_of[u]
                it = NT - 1 - back
                wait(pe, m_read, b * NU + n)
                for i, h in enumerate(heads):
                    bk, at = place(u, i)
                    nc.tensor.matmul(bank[0:TP, 6 + bk, at:at + cols], Q[:, par, h * EE + e, it * TP:(it + 1) * TP],
                                     K[:, par, h, 0:cols], start=i % per == 0, stop=False, skip_group_check=True)
                for i in range(len(heads)):
                    bk, at = place(u, i)
                    last = nc.tensor.matmul(bank[0:TP, 6 + bk, at + cols - TP:at + cols], B("ident_b")[0:TP, 0:TP],
                                            B("m_low_q"), start=False, stop=True, skip_group_check=True)
                last.then_inc(m_ready, 1)

            def scores_for_exp(b, par, n):
                e, u = divmod(n, 4)
                jt, heads, cols, per = rounds_of[u]
                if n == 0:
                    pe.wait_ge(maxT_kept, b + 1)
                wait(pe, e_done, b * NU + n)
                for i, h in enumerate(heads):
                    bk, at = place(u, i)
                    nc.tensor.matmul(bank[0:TP, 4 + bk, at:at + cols], K[:, par, h, jt * TP:(jt + 1) * TP],
                                     Q[:, par, h * EE + e, jt * TP:S], start=i % per == 0, stop=False,
                                     skip_group_check=True)
                for i, h in enumerate(heads):
                    bk, at = place(u, i)
                    nc.tensor.matmul(bank[0:TP, 4 + bk, at:at + cols], B("pick_query")[:, h * EE + e, :],
                                     maxT[:, jt * TP:S], start=False, stop=False, skip_group_check=True)
                    last = nc.tensor.matmul(bank[0:TP, 4 + bk, at:at + TP], B("ident_b")[0:TP, 0:TP],
                                            B("m_low_k"), start=False, stop=True, skip_group_check=True)
                last.then_inc(e_ready, 1)

            def weigh_values(b, par, n):
                e, u = divmod(n, 4)
                jt, heads, cols, per = rounds_of[u]
                pe.wait_ge(e_done, b * NU + n + 1)
                if u == 0:
                    wait(pe, c_kept, b * EE + e)
                for i, h in enumerate(heads):
                    bk, at = place(u, i)
                    last = nc.tensor.matmul(bank[32 * h:32 * h + 32, 2, jt * TP:S],
                                            v_aug[:, par, jt, 32 * h:32 * h + 32], E[:, n % 3, bk, at:at + cols],
                                            start=jt == 0, stop=jt == NT - 1, skip_group_check=True)
                last.then_inc(v_done, 1)

            def turn_max(b, projected):
                pe.wait_ge(neg_ready, b + 1)
                pe.wait_ge(nz_done, projected)
                for it in range(NT):
                    last = nc.tensor.matmul(bank[0:96, 1, it * TP:(it + 1) * TP], neg[:, it, :],
                                            B("ident_b")[0:TP, 0:TP], start=True, stop=True)
                last.then_inc(neg_turned, 1)

            def tail(b, n):
                if n < NT:
                    if n == 0:
                        pe.wait_ge(c_kept, (b + 1) * EE)
                        wait(pe, fs_ready, b)
                    wait(pe, sel_read, b * NT + n)
                    for e in range(EE):
                        last = nc.tensor.matmul(bank[0:TP, 3, e * FW:(e + 1) * FW], cT[:, e, n * TP:(n + 1) * TP],
                                                gsel[:, e, :], start=True, stop=True)
                    last.then_inc(sel_ready, 1)
                if n == 7:
                    pe.wait_ge(fx_ready, b + 1)
                    for it in range(NT):
                        last = nc.tensor.transpose(bank[:, 3, it * TP:(it + 1) * TP], fx[:, it, :], F("ident")[0:TP, 0:TP])
                    last.then_inc(fx_turned, 1)
                if n == 8:
                    pe.wait_ge(fxT_kept, b + 1)
                    nc.tensor.matmul(bank[0:D, 3, 0:S], W("fc1"), fxT[:], start=True, stop=True).then_inc(h1_ready, 1)
                if n == 9:
                    pe.wait_ge(h1T_ready, b + 1)
                    for it in range(NT):
                        last = nc.tensor.matmul(bank[0:TP, 3, it * D:(it + 1) * D], h1T[:, it * TP:(it + 1) * TP],
                                                W("fc2"), start=True, stop=True)
                    last.then_inc(h2_ready, 1)
                if n == 12:
                    pe.wait_ge(fo_ready, b + 1)
                    for it in range(NT):
                        last = nc.tensor.transpose(bank[:, 3, it * TP:(it + 1) * TP], fo[:, it, :], F("ident")[0:TP, 0:TP])
                    last.then_inc(fo_turned, 1)
                if n == 13:
                    pe.wait_ge(foT_kept, b + 1)
                    for it in range(NT):
                        last = nc.tensor.matmul(bank[0:TP, 3, it * HE:(it + 1) * HE], foT[:, it * TP:(it + 1) * TP],
                                                W("fgate"), start=True, stop=True)
                    last.then_inc(fl_ready, 1)

            def step(r, par):
                b1, b2, b3 = r - 1, r - 2, r - 3
                if alive(b1, nb):
                    pe.wait_ge(stacked, (b1 + 1) * 32 * len(q_parts))
                for n in range(NU):
                    if alive(b2, nb):
                        scores_for_exp(b2, (par - 2) % 3, n)
                    if alive(b1, nb):
                        scores_for_max(b1, (par - 1) % 3, n)
                    if alive(b2, nb) and n:
                        weigh_values(b2, (par - 2) % 3, n - 1)
                    if alive(b3, nb):
                        tail(b3, n)
                    if alive(r, nb):
                        if n == 2:
                            norm.turn(pe, r)
                        if n in (4, 6, 8, 10, 12):
                            project(r, n // 2 - 2)
                if alive(b2, nb):
                    weigh_values(b2, (par - 2) % 3, NU - 1)
                if alive(b1, nb):
                    turn_max(b1, r + 1 if alive(r, nb) else nb)

            rounds(pe, step, 3, own_x[0], nb, 3)

        @block.scalar
        def _(act):
            def first_part(b, i):
                act.wait_ge(p_ready, b * (NP + 1) + i + 1)
                if i == 0:
                    wait(act, parts_stored, b * 16)
                nc.scalar.copy(parts[:, 0, i, :], bank[:, 1, 0:S]).then_inc(hi_done, 1)

            def keep_values(b, par):
                act.wait_ge(p_ready, (b + 1) * (NP + 1))
                wait(act, v_done, (b - 2) * NU)
                nc.scalar.copy(flat3(v_aug[:, par]), bank[0:TP, 1, 0:NT * 128]).then_inc(v_kept, 1)

            def exponentials(b, n):
                jt, heads, cols, per = rounds_of[n % 4]
                act.wait_ge(e_ready, b * NU + n + 1)
                wait(act, v_done, b * NU + n - 2)
                used = slice(0, per * cols)
                banks = len(heads) // per
                nc.scalar.activation(E[:, n % 3, 0:banks, used], bank[0:TP, 4:4 + banks, used],
                                     ACT.Exp).then_inc(e_done, 1)

            def tail(b, n):
                if n < NT:
                    act.wait_ge(sel_ready, b * NT + n + 1)
                    if n == 0:
                        wait(act, sq_ready, 2 * b)
                    nc.scalar.copy(tok[:, n * EE:(n + 1) * EE, :],
                                   bank[0:TP, 3, 0:EE * FW].rearrange("p (e f) -> p e f", e=EE)).then_inc(sel_read, 1)
                if n == 3:
                    act.wait_ge(g_ready, b + 1)
                    nc.scalar.activation(flat3(gex[:]), flat3(gl[:]), ACT.Exp).then_inc(gex_done, 1)
                if n in (4, 10):
                    act.wait_ge(sq_ready, 2 * b + (n == 10) + 1)
                    nc.scalar.activation(sq[:], y[:], ACT.Square).then_inc(sq_done, 1)
                if n == 7:
                    act.wait_ge(fx_turned, b + 1)
                    wait(act, h1T_ready, b)
                    nc.scalar.copy(fxT[0:D, :], bank[0:D, 3, 0:S]).then_inc(fxT_kept, 1)
                if n == 8:
                    act.wait_ge(h1_ready, b + 1)
                    nc.scalar.activation(r1[:], bank[0:D, 3, 0:S], ACT.Relu).then_inc(r1_done, 1)
                if n == 12:
                    act.wait_ge(fo_turned, b + 1)
                    wait(act, fl_ready, b)
                    nc.scalar.copy(foT[:], bank[0:D, 3, 0:S]).then_inc(foT_kept, 1)
                if n == 14:
                    act.wait_ge(fs_ready, b + 1)
                    nc.scalar.activation(fl[:], fl[:], ACT.Exp).then_inc(fex_done, 1)

            def step(r, par):
                b1, b2, b3 = r - 1, r - 2, r - 3
                for n in range(NU):
                    if alive(b2, nb):
                        exponentials(b2, n)
                    if alive(b3, nb):
                        tail(b3, n)
                    if alive(r, nb):
                        if n == 2:
                            norm.keep(act, r, 0, [(nz_ready, r)])
                        if n in (4, 6, 8):
                            first_part(r, n // 2 - 2)
                        if n == 10:
                            keep_values(r, par)
                if alive(b1, nb):
                    act.wait_ge(neg_turned, b1 + 1)
                    wait(act, e_ready, b1 * NU)
                    nc.scalar.copy(maxT[:], bank[0:96, 1, 0:S]).then_inc(maxT_kept, 1)

            rounds(act, step, 3, own_x[1], nb, 3)

        @block.vector
        def _(dve):
            own = Tally(own_dve)
            norm.clear(dve, own)
            for v in (neg, fx, fo, zeros):
                own.up(nc.vector.memset(v[:], 0.0))
            own.up(nc.vector.memset(WH[:], 0.0))
            for v in (fxT, h1T):
                own.link(dve, nc.vector.memset(v[:], 0.0))
                own.up(nc.vector.memset(v[D:D + 1], 1.0))
            for i, (g, b_) in enumerate((("ln_g", "ln_b"), ("fnorm_g", "fnorm_b"))):
                for dst, src in ((gamma, g), (beta, b_)):
                    own.up(nc.vector.tensor_copy(dst[:, i], W(src).rearrange("p (o d) -> p o d", o=1)
                                                 .to_broadcast((TP, NT * HE, DH2))))
            own.up(nc.vector.tensor_copy(gb[:], W("gate_b2").rearrange("p (o d) -> p o d", o=1).to_broadcast((TP, NT, QE))))
            own.up(nc.vector.tensor_copy(gsel[:, :, 0:HE * VS], F("sel").rearrange("p (o d) -> p o d", o=1)
                                         .to_broadcast((128, EE, HE * VS))))
            own.up(nc.vector.tensor_copy(gsel[:, :, HE * VS:], W("gate_w2")))
            dve.wait_ge(folded, 1)
            own.up(nc.vector.tensor_scalar(flat3(WH[0:D + 1, 0:2, :]), bank[0:D + 1, 4, 0:256], float(DH2) ** 0.5, None, ALU.mult))
            own.link(dve, nc.vector.tensor_copy(flat3(WH[0:D + 1, 2:, :]), bank[0:D + 1, 4, 256:512]))
            own.link(dve, nc.vector.memset(WH[D:D + 1, NP, :].rearrange("p (n d) -> p n d", n=HE)[:, :, DH2:VS], 1.0))
            nc.vector.memset(norm.carry[:], 0.0).then_inc(set_up, 1)

            def maxima(b, n):
                e, u = divmod(n, 4)
                back, heads, cols, per = rounds_of[u]
                it = NT - 1 - back
                dve.wait_ge(m_ready, b * NU + n + 1)
                banks = len(heads) // per
                src = bank[0:TP, 6:6 + banks, 0:per * cols].rearrange("p k (i c) -> p k i c", i=per)
                dst = top[:, it, :].rearrange("p (h e) -> p h e", h=HE)[:, heads[0]:heads[-1] + 1, e]
                nc.vector.tensor_reduce(dst.rearrange("p (k i) -> p k i", k=banks), src, AX, ALU.max).then_inc(m_read, 1)

            def negate_max(b):
                dve.wait_ge(m_read, (b + 1) * NU)
                wait(dve, neg_turned, b)
                nc.vector.tensor_scalar(neg[:, :, 0:QE], top[:], -1.0, None, ALU.mult).then_inc(neg_ready, 1)

            def normalise_start(b, i):
                own.link(dve, nc.vector.tensor_reduce(mean[:], y[:], AX, ALU.add))
                nc.vector.scalar_tensor_tensor(y[:], mean[:].rearrange("p (a o) -> p a o", o=1)
                                               .to_broadcast((TP, NT * HE, DH2)), -1.0 / DH2, y[:],
                                               ALU.mult, ALU.add).then_inc(sq_ready, 1)

            def normalise_sum(b, i):
                dve.wait_ge(sq_done, 2 * b + i + 1)
                nc.vector.tensor_reduce(var[:], sq[:], AX, ALU.add).then_inc(vs_ready, 1)

            def normalise_end(b, i, dst, done):
                dve.wait_ge(root_done, 2 * b + i + 1)
                own.link(dve, nc.vector.tensor_tensor(y[:], y[:], root[:].rearrange("p (a o) -> p a o", o=1)
                                                      .to_broadcast((TP, NT * HE, DH2)), ALU.mult))
                own.link(dve, nc.vector.tensor_tensor(y[:], y[:], gamma[:, i], ALU.mult))
                nc.vector.tensor_tensor(dst, by_tile(y[:]), by_tile(beta[:, i]), ALU.add).then_inc(done, 1)

            by_tile = lambda v: v.rearrange("p (t h) d -> p t (h d)", t=NT)

            def tail(b, par, n):
                if n == 3:
                    dve.wait_ge(sel_read, (b + 1) * NT)
                    sums = tok[:, :, 0:HE * VS].rearrange("p a (h d) -> p a h d", h=HE)[:, :, :, DH2]
                    own.link(dve, nc.vector.reciprocal(rs[:], sums))
                    own.link(dve, nc.vector.tensor_tensor(
                        gp[:].rearrange("p a (h e) -> p a h e", h=HE),
                        tok[:, :, HE * VS:].rearrange("p a (h e) -> p a h e", h=HE),
                        rs[:].rearrange("p a (h o) -> p a h o", o=1).to_broadcast((TP, NT * EE, HE, EE)), ALU.mult))
                    own.link(dve, nc.vector.tensor_reduce(gl[:], gp[:].rearrange("p (t e) f -> p t f e", t=NT), AX, ALU.add))
                    own.link(dve, nc.vector.tensor_tensor(gl[:], gl[:], gb[:], ALU.add))
                    heads = gl[:].rearrange("p t (h e) -> p (t h) e", h=HE)
                    own.link(dve, nc.vector.tensor_reduce(gtop[:], heads, AX, ALU.max))
                    nc.vector.tensor_tensor(heads, heads, gtop[:].rearrange("p (a o) -> p a o", o=1)
                                            .to_broadcast((TP, NT * HE, EE)), ALU.subtract).then_inc(g_ready, 1)
                if n == 4:
                    dve.wait_ge(gex_done, b + 1)
                    own.link(dve, nc.vector.tensor_reduce(gsum[:], gex[:], AX, ALU.add))
                    own.link(dve, nc.vector.reciprocal(gsum[:], gsum[:]))
                    own.link(dve, nc.vector.tensor_tensor(gex[:], gex[:], gsum[:].rearrange("p (a o) -> p a o", o=1)
                                                          .to_broadcast((TP, NT * HE, EE)), ALU.mult))
                    own.link(dve, nc.vector.tensor_tensor(wt[:], gex[:].rearrange("p (t h) e -> p t e h", t=NT),
                                                          rs[:].rearrange("p (t e) h -> p t e h", t=NT), ALU.mult))
                    own.link(dve, nc.vector.tensor_tensor(
                        wc[:].rearrange("p a (h d) -> p a h d", h=HE),
                        tok[:, :, 0:HE * VS].rearrange("p a (h d) -> p a h d", h=HE)[:, :, :, 0:DH2],
                        wt[:].rearrange("p t e h -> p (t e) h").rearrange("p a (h o) -> p a h o", o=1)
                        .to_broadcast((TP, NT * EE, HE, DH2)), ALU.mult))
                    own.link(dve, nc.vector.tensor_reduce(by_tile(y[:]), wc[:].rearrange("p (t e) f -> p t f e", t=NT),
                                                          AX, ALU.add))
                    own.link(dve, nc.vector.tensor_tensor(by_tile(y[:]), by_tile(y[:]), res[:], ALU.add))
                    normalise_start(b, 0)
                if n == 5:
                    normalise_sum(b, 0)
                if n == 6:
                    normalise_end(b, 0, fx[:, :, 0:D], fx_ready)
                if n == 9:
                    dve.wait_ge(r1_done, b + 1)
                    wait(dve, h2_ready, b)
                    nc.vector.scalar_tensor_tensor(h1T[0:D, :], fxT[0:D, :], 0.0, r1[:], ALU.not_equal,
                                                   ALU.mult).then_inc(h1T_ready, 1)
                if n == 10:
                    dve.wait_ge(h2_ready, b + 1)
                    h2 = bank[0:TP, 3, 0:NT * D].rearrange("p (t f) -> p t f", t=NT)
                    own.link(dve, nc.vector.scalar_tensor_tensor(by_tile(y[:]), fx[:, :, 0:D], 0.0, h2, ALU.not_equal, ALU.mult))
                    own.link(dve, nc.vector.tensor_tensor(by_tile(y[:]), by_tile(y[:]), fx[:, :, 0:D], ALU.add))
                    normalise_start(b, 1)
                if n == 11:
                    normalise_sum(b, 1)
                if n == 12:
                    normalise_end(b, 1, fo[:, :, 0:D], fo_ready)
                if n == 14:
                    dve.wait_ge(fl_ready, b + 1)
                    lg = bank[0:TP, 3, 0:NT * HE].rearrange("p (t h) -> p t h", t=NT)
                    own.link(dve, nc.vector.tensor_reduce(fs[:], lg, AX, ALU.max))
                    nc.vector.tensor_tensor(fl[:].rearrange("p (t h) -> p t h", t=NT), lg,
                                            fs[:].rearrange("p (t o) -> p t o", o=1).to_broadcast((TP, NT, HE)),
                                            ALU.subtract).then_inc(fs_ready, 1)
                if n == 15:
                    dve.wait_ge(fex_done, b + 1)
                    l3 = fl[:].rearrange("p (t h) -> p t h", t=NT)
                    own.link(dve, nc.vector.tensor_reduce(fs[:], l3, AX, ALU.add))
                    own.link(dve, nc.vector.reciprocal(fs[:], fs[:]))
                    own.link(dve, nc.vector.tensor_tensor(l3, l3, fs[:].rearrange("p (t o) -> p t o", o=1)
                                                          .to_broadcast((TP, NT, HE)), ALU.mult))
                    own.link(dve, nc.vector.tensor_tensor(
                        sq[:].rearrange("p (t h) d -> p t h d", t=NT), y_of(fo), fl[:].rearrange("p (t h o) -> p t h o", t=NT, o=1)
                        .to_broadcast((TP, NT, HE, DH2)), ALU.mult))
                    wait(dve, stored, (b - 1) * 16)
                    nc.vector.tensor_tensor(hout[:, par, :], sq[:].rearrange("p a d -> p (a d)"), one(k.h, b),
                                            ALU.add).then_inc(h_ready, 16)

            def y_of(v):
                return v[:, :, 0:D].rearrange("p t (h d) -> p t h d", h=HE)

            def leave_rest(b, i):
                dve.wait_ge(hi_done, b * NP + i + 1)
                wait(dve, parts_done, (b - 1) * NP + i + 1)
                nc.vector.tensor_tensor(rest[:, i, :], bank[:, 1, 0:S], parts[:, 0, i, :],
                                        ALU.subtract).then_inc(rest_ready, 1)

            def step(r, par):
                b1, b2, b3 = r - 1, r - 2, r - 3
                if alive(r, nb):
                    norm.start(dve, r)
                for n in range(NU):
                    if alive(b1, nb):
                        maxima(b1, n)
                    if alive(b2, nb) and n % 4 == 1 and n > 4:
                        keep_context(b2, (par - 2) % 3, n // 4 - 1)
                    if alive(b3, nb):
                        tail(b3, par, n)
                    if alive(r, nb):
                        if n == 1:
                            norm.apply(dve, r)
                        if n in (4, 6, 8):
                            leave_rest(r, n // 2 - 2)
                        if n == 12:
                            dve.wait_ge(nz_ready, r + 1)
                            nc.vector.tensor_scalar(nz[:, par, :], bank[:, 1, 0:S], 0.0, None,
                                                    ALU.not_equal).then_inc(nz_done, 1)
                if alive(b2, nb):
                    keep_context(b2, (par - 2) % 3, EE - 1)
                if alive(b1, nb):
                    negate_max(b1)

            def keep_context(b, par, e):
                dve.wait_ge(v_done, b * NU + 4 * (e + 1))
                wait(dve, sel_ready, b * NT)
                nc.vector.tensor_tensor(cT[:, e, :], bank[:, 2, 0:S], nz[:, par, :], ALU.mult).then_inc(c_kept, 1)

            rounds(dve, step, 3, own, nb, 3)

        @block.gpsimd
        def _(pool):
            own = Tally(own_pool)

            def other_parts(b, i):
                pool.wait_ge(rest_ready, b * NP + i + 1)
                own.link(pool, nc.gpsimd.tensor_tensor(parts[:, 1, i, :], rest[:, i, :], zeros[:], ALU.add))
                nc.gpsimd.tensor_tensor(parts[:, 2, i, :], rest[:, i, :], parts[:, 1, i, :],
                                        ALU.subtract).then_inc(parts_done, 1)

            def step(r, par):
                b = r - 3
                if alive(r, nb):
                    norm.take_root(pool, r)
                    other_parts(r, 0)
                if alive(b, nb):
                    take_root(b, 0)
                if alive(r, nb):
                    other_parts(r, 1)
                    other_parts(r, 2)
                if alive(b, nb):
                    take_root(b, 1)

            def take_root(b, i):
                pool.wait_ge(vs_ready, 2 * b + i + 1)
                own.link(pool, nc.gpsimd.tensor_tensor(root[:], var[:], F("per_width"), ALU.mult))
                own.link(pool, nc.gpsimd.tensor_tensor(root[:], root[:], F("eps2"), ALU.add))
                nc.gpsimd.tensor_tensor(root[:], root[:], k.half[:], ALU.pow).then_inc(root_done, 1)

            rounds(pool, step, 3, own, nb, 3)


def flat3(ap):
    return ap.rearrange("p a b -> p (a b)")


def one(h, b):
    return h[:, bass.ds(b, 1), :].rearrange("p o f -> p (o f)")


def tower(nc, nb, x, fpack, bpack, wpack, packs, s_dram, qk_dram, out):
    with ExitStack() as ctx:
        k = Core(nc, ctx, packs, nb)
        with nc.cleanup_on_exit(), ExitStack() as c:
            t = SelectAttend(k, c)
            score_tokens(k, x, fpack, bpack, wpack, s_dram, t)
            select_attend(k, t, x, s_dram)
        with nc.cleanup_on_exit():
            experts(k)
        with nc.cleanup_on_exit():
            slices(k)
        res = k.sb("first_heads", [TP, NT, D])
        with nc.cleanup_on_exit():
            first_heads(k, res)
            query_experts(k, res, qk_dram, out)


def kernel(**inputs):
    import concourse.bacc as bacc
    from concourse.bass_utils import run_bass_kernel_spmd

    weights = {n: np.asarray(v) for n, v in inputs.items() if n != "x"}
    x = np.ascontiguousarray(inputs["x"])
    f, b = shape_constants()
    w = weight_layout(weights)
    arrays = {"x": x, "fconst_in": f.build(np.float32),
              "bconst_in": b.build(mybir.dt.np(BF16)), "weights_in": w.build(np.float32)}
    nc = bacc.Bacc("TRN2", target_bir_lowering=False, num_devices=1)
    args = [nc.dram_tensor(n, a.shape, mybir.dt.from_np(a.dtype), kind="ExternalInput").ap()
            for n, a in arrays.items()]
    nb = x.shape[0]
    out = nc.dram_tensor("out", (nb, S, D), F32, kind="ExternalOutput").ap()
    qk_dram = nc.dram_tensor("query_key_parts", (128, 3, 3, S), BF16).ap()
    s_dram = nc.dram_tensor("scores", (nb * CI, TP), F32).ap()
    tower(nc, nb, *args, (f, b, w), s_dram, qk_dram, out)
    r = run_bass_kernel_spmd(nc, [arrays], core_ids=[0])
    return r.results[0]["out"]
```

```python
from contextlib import ExitStack

import numpy as np

import concourse.bass as bass
from concourse import mybir

F32 = mybir.dt.float32
BF16 = mybir.dt.bfloat16
ALU = mybir.AluOpType
ACT = mybir.ActivationFunctionType
AX = mybir.AxisListType.X

NB = 32
N_IN = 750
S = N_IN // 2
D = 64
TP = 125
CI = N_IN // TP
NT = S // TP
H0, DH = 4, 16
NE, DE = 8, 128
HS, DS, G = 8, 8, 64
PS = HS // 2
DS1 = DS + 1
HE, EE, DH2 = 4, 4, 16
QE = HE * EE
VS = DH2 + 1
EPS = 1e-5
EPS2 = 1e-8
BIG = -1e30
TINY = 2.0 ** -126




class Pack:

    def __init__(self):
        self.parts, self.at, self.width = [], {}, 0

    def add(self, name, array):
        array = np.asarray(array)
        rows, shape = array.shape[0], array.shape[1:]
        cols = int(np.prod(shape))
        self.at[name] = (rows, self.width, shape)
        self.parts.append(array.reshape(rows, cols))
        self.width += cols

    def build(self, dtype):
        out = np.zeros((128, self.width), dtype)
        at = 0
        for part in self.parts:
            out[:part.shape[0], at:at + part.shape[1]] = part
            at += part.shape[1]
        return out

    def view(self, tile, name):
        rows, at, shape = self.at[name]
        v = tile[0:rows, at:at + int(np.prod(shape))]
        if len(shape) == 2:
            v = v.rearrange("p (a b) -> p a b", a=shape[0])
        if len(shape) == 3:
            v = v.rearrange("p (a b c) -> p a b c", a=shape[0], b=shape[1])
        return v


def shape_constants():
    f, b = Pack(), Pack()
    f.add("ident", np.eye(128))
    w = np.exp(np.arange(0, D, 2, dtype=np.float32) * np.float32(-np.log(10000.0) / D)).astype(np.float64)
    wf = np.repeat(w, 2)[:, None]
    is_cos = (np.arange(D) % 2 == 1)[:, None]
    sign = np.where(is_cos, 1.0, -1.0)
    j = np.arange(S)[None, :]
    pe = np.where(is_cos, np.cos(j * wf), np.sin(j * wf))
    f.add("pe", np.concatenate([pe, pe]))
    c = (S - 1 - j)
    f.add("cos_low", np.tile(np.cos(c * wf), (2, 1)))
    f.add("sin_low", np.tile(sign * np.sin(c * wf), (2, 1)))
    c = -(np.arange(1, S)[None, :] + 1)
    f.add("cos_up", np.tile(np.cos(c * wf), (2, 1)))
    f.add("sin_up", np.tile(sign * np.sin(c * wf), (2, 1)))
    for name, value in (("eps", EPS), ("one_eps", 1.0 + EPS), ("eps_eps", EPS * EPS)):
        f.add(name, np.full((TP, 4 * NT), value))
    f.add("iota", np.tile(np.arange(S)[None, :], (TP, 1)))
    last = np.zeros((TP, NT, H0))
    last[TP - 1, NT - 1] = BIG
    f.add("no_next", last)
    p = np.arange(TP)[:, None]
    b.add("ident_b", np.eye(128))
    tie = np.zeros((TP, CI, N_IN))
    for t in range(CI):
        tie[:, t] = np.where(np.arange(N_IN)[None, :] < t * TP + p, 0.0, TINY)
    b.add("tie", tie)
    q = np.arange(TP)[None, :]
    q2 = np.arange(2 * TP)[None, :]
    b.add("m_low_q", np.where(q > p, BIG, 0.0))
    b.add("m_up_q", np.where(q2 < p + 2, BIG, 0.0))
    b.add("m_low_k", np.where(q < p, BIG, 0.0))
    b.add("m_up_k", np.where(q2 - TP > p - 2, BIG, 0.0))
    pick = np.zeros((96, H0, TP))
    for h in range(H0):
        pick[h, h] = 1.0
    b.add("pick_head", pick)
    expert = np.zeros((96, NE, 128))
    for e in range(NE):
        expert[e:3 * NE:NE, e] = 1.0
    b.add("pick_expert", expert)
    b.add("earlier", np.tile(np.tril(np.ones((NE, NE)), -1).reshape(1, NE * NE), (TP, 1)))
    f.add("slice_block", np.kron(np.eye(HS), np.full((DS1, DS1), 1 / np.sqrt(np.float64(DS)))))
    own_pair = np.zeros((HS * DS1, PS, G))
    for h in range(HS):
        own_pair[h * DS1:(h + 1) * DS1, h // 2] = 1.0
    f.add("own_pair", own_pair)
    slices = np.zeros((96, HS * G))
    for h in range(HS):
        slices[h, h * G:(h + 1) * G] = 1.0
    b.add("pick_slices", slices)
    sel = np.zeros((128, HE * VS))
    for n in range(HE):
        sel[32 * n:32 * n + VS, n * VS:(n + 1) * VS] = np.eye(VS)
    f.add("sel", sel)
    f.add("eps2", np.full((TP, NT * HE), EPS2))
    f.add("per_width", np.full((TP, NT * HE), 1.0 / DH2))
    expert_row = np.zeros((96, QE, TP))
    for n in range(QE):
        expert_row[n, n] = 1.0
    b.add("pick_query", expert_row)
    f.add("two_halves", np.concatenate([np.eye(D), np.eye(D)]))
    f.add("euler", np.full((TP, NT * NE), np.e))
    return f, b


def weight_layout(w):
    k = Pack()
    z = lambda *s: np.zeros(s, np.float32)

    def over(matrix, *rows):
        out = z(96, matrix.shape[1])
        out[:matrix.shape[0]] = matrix
        for n, r in enumerate(rows):
            out[matrix.shape[0] + n] = r
        return out

    g = {n[len("L0_attn_"):]: v for n, v in w.items() if n.startswith("L0_attn_")}
    k.add("score_w", np.broadcast_to(w["L0_tok_score_proj"].reshape(1, D), (TP, D)))
    k.add("gamma", g["ln_gamma"].reshape(D, 1))
    k.add("beta", g["ln_beta"].reshape(D, 1))
    wq = over(g["Wq"], g["bq"], g["u_bias"].reshape(D))
    wk = over(g["Wk"], g["bk"])
    wv = over(g["Wv"], g["bv"])
    cq, ck = z(96, 2, 128), z(96, 2, 128)
    for h in range(H0):
        at = 64 if h % 2 == 0 else 0
        cq[:, h // 2, at:at + DH] = wq[:, h * DH:(h + 1) * DH]
        ck[:, h // 2, at:at + DH] = wk[:, h * DH:(h + 1) * DH]
    k.add("wcq", cq)
    k.add("wck", ck)
    va = z(96, H0, 32)
    va[:, :, :DH] = wv.reshape(96, H0, DH)
    va[D, :, DH] = 1.0
    k.add("wq_tok", wq)
    k.add("wv_aug", va.reshape(96, 128))
    k.add("wkv_next", np.concatenate([wk, wv], 1))
    k.add("wout", over(g["Wout"], g["bout"]))
    qT = z(DH, H0, 66)
    qT[:, :, :D] = g["Wq"].reshape(D, H0, DH).transpose(2, 1, 0)
    qT[:, :, D] = g["bq"].reshape(H0, DH).T
    qT[:, :, D + 1] = g["v_bias"].T
    posT = g["Wpos"].reshape(D, H0, DH).transpose(2, 1, 0)
    k.add("wqT", qT)
    k.add("wposT", np.ascontiguousarray(posT))
    m = {n[len("L0_ffn_"):]: v for n, v in w.items() if n.startswith("L0_ffn_")}
    k.add("gate_w", over(m["gate_w"], m["gate_b"]))
    w1 = z(96, NE, DE)
    w1[:D] = m["W1"].transpose(1, 0, 2)
    w1[D] = m["b1"]
    k.add("w1", w1)
    k.add("w2", m["W2"].transpose(1, 0, 2))
    k.add("b2", np.tile(m["b2"], (3, 1)))
    a = {n[len("L1_attn_"):]: v for n, v in w.items() if n.startswith("L1_attn_")}
    k.add("w_in", over(a["W_in"], a["b_in"]))
    inT = z(DS1, HS, D + 1)
    inT[:DS, :, :D] = a["W_in"].reshape(D, HS, DS).transpose(2, 1, 0)
    inT[:DS, :, D] = a["b_in"].reshape(HS, DS).T
    inT[DS, :, D] = 1.0
    k.add("w_inT", inT)
    k.add("w_slice", np.concatenate([a["W_slice"], a["b_slice"][None, :]]))
    k.add("temperature", np.broadcast_to(a["temperature"].reshape(1, HS), (96, HS)))
    k.add("wq_sT", np.tile(np.concatenate([a["W_q"], a["b_q"][None, :]]).T, (1, HS)))
    k.add("wk_sT", np.tile(np.concatenate([a["W_k"], a["b_k"][None, :]]).T, (1, HS)))
    wv9 = np.concatenate([a["W_v"], a["b_v"][None, :]])
    bdv = z(HS * DS1, PS, DS)
    for h in range(HS):
        bdv[h * DS1:(h + 1) * DS1, h // 2] = wv9
    k.add("wv_s", bdv.reshape(HS * DS1, PS * DS))
    k.add("w_out_s", over(a["W_out"], a["b_out"]))
    l = {n[len("L1_ffn_"):]: v for n, v in w.items() if n.startswith("L1_ffn_")}
    sx = over(l["hl_w"].reshape(D, D).T, l["hl_b"].reshape(D))
    k.add("w_sx", sx)
    wide = z(96, HE, 32)
    wide[:, :, :DH2] = sx.reshape(96, HE, DH2)
    wide[D, :, DH2] = 1.0
    k.add("w_sx_wide", wide.reshape(96, 128))
    k.add("w_sxT", np.concatenate([l["hl_w"].reshape(D, D), l["hl_b"].reshape(D, 1)], 1))
    heads = z(D, 4, HE, 2, DH2)
    for n in range(HE):
        rows = slice(n * DH2, (n + 1) * DH2)
        for e in range(EE):
            heads[rows, e % 2, n, e // 2] = l["wq"][n, e].T
        heads[rows, 2, n, 0] = l["wk"][n].T
        heads[rows, 3, n, 0] = l["wv"][n].T
    k.add("w_heads", heads.reshape(D, 4, 128))
    gw = z(128, EE, HE * EE)
    for n in range(HE):
        for e in range(EE):
            gw[32 * n:32 * n + DH2, e, n * EE:(n + 1) * EE] = l["gate_w"][n, :, e * DH2:(e + 1) * DH2].T
    k.add("gate_w2", gw)
    k.add("gate_b2", np.broadcast_to(l["gate_b"].reshape(1, QE), (TP, QE)))
    for name in ("ln_g", "ln_b", "fnorm_g", "fnorm_b"):
        k.add(name, np.broadcast_to(l[name].reshape(1, DH2), (TP, DH2)))
    for name in ("fc1", "fc2"):
        block = z(D, D)
        for n in range(HE):
            block[n * DH2:(n + 1) * DH2, n * DH2:(n + 1) * DH2] = l[name + "_w"].T
        k.add(name, over(block, np.tile(l[name + "_b"], HE)))
    k.add("fgate", l["fgate_w"].T)
    k.add("wposT_swap", posT.reshape(DH, H0, D // 2, 2)[..., ::-1].reshape(DH, H0, D))
    return k




class Tally:

    def __init__(self, sem):
        self.sem, self.base, self.n = sem, 0, 0

    def up(self, instruction):
        instruction.then_inc(self.sem, 1)
        self.n += 1

    def wait(self, eng):
        eng.wait_ge(self.sem, self.base + self.n)

    def link(self, eng, instruction):
        self.up(instruction)
        self.wait(eng)


def wait(eng, sem, value):
    if not isinstance(value, int) or value > 0:
        eng.wait_ge(sem, value)


def rounds(eng, step, lags, tally, n, period=2):
    peel = lags + period
    peel += (n - peel) % period
    for t in range(peel):
        if t == peel - period:
            before = tally.n
        step(t, t % period)
    per = tally.n - before
    entry = tally.base + tally.n
    count = (n - peel) // period
    if count:
        with eng.Fori(0, count) as g:
            tally.base, tally.n = g * per + entry, 0
            for i in range(period):
                step(g * period + (peel + i), (peel + i) % period)
            assert tally.n == per
    tally.base, tally.n = entry + count * per, 0
    for t in range(n, n + lags):
        step(t, t % period)


def alive(b, n):
    return not isinstance(b, int) or 0 <= b < n


class Core:

    def __init__(self, nc, ctx, packs, nb):
        self.nc, self.nb = nc, nb
        fpack, bpack, wpack = packs
        self.sb = lambda name, shape, dt=F32: ctx.enter_context(nc.sbuf_tensor(name, shape, dt))
        self.sem = lambda name: nc.alloc_semaphore(name=name)
        self.fc = self.sb("fconst", [128, fpack.width])
        self.bc = self.sb("bconst", [128, bpack.width], BF16)
        self.wc = self.sb("weights", [128, wpack.width])
        self.F = lambda name: fpack.view(self.fc, name)
        self.B = lambda name: bpack.view(self.bc, name)
        self.W = lambda name: wpack.view(self.wc, name)
        self.bank = ctx.enter_context(nc.psum_tensor("psum", [128, 8, 512], F32))
        self.h = self.sb("h_all", [TP, nb, NT * D])
        self.half = self.sb("minus_half", [TP, 4 * NT])





def score_tokens(k, x_dram, fpack_dram, bpack_dram, wpack_dram, s_dram, t):
    nc, nb = k.nc, k.nb
    tiles = nb * CI
    chunk = 4 * CI if nb % 4 == 0 else CI
    n_chunks = tiles // chunk
    loaded, multiplied = (k.sem("x_even_loaded"), k.sem("x_odd_loaded")), k.sem("x_multiplied")
    half_set = k.sem("half_set")
    const_loaded, w_loaded = k.sem("const_loaded"), k.sem("weights_loaded")
    dve_own, scored = k.sem("score_dve_own"), k.sem("scored")
    s_turned, s_copied, s_stored = k.sem("scores_turned"), k.sem("scores_copied"), k.sem("scores_stored")
    gate_exp, folded, folded_copied = k.sem("gate_exp"), k.sem("folded"), k.sem("folded_copied")
    W, F = k.W, k.F
    with ExitStack() as ctx:
        xs = ctx.enter_context(nc.sbuf_tensor("x_chunks", [TP, 2, chunk, D], F32))
        prod = ctx.enter_context(nc.sbuf_tensor("prod", [TP, chunk, D], F32))
        s_rows = ctx.enter_context(nc.sbuf_tensor("s_rows", [128, 2, TP], F32))
        block = ctx.enter_context(nc.Block())
        groups = [(a, min(a + 128, tiles)) for a in range(0, tiles, 128)]

        @block.sync
        def _(sp):
            sp.dma_start(k.wc[:], wpack_dram).then_inc(w_loaded, 16)
            for i in range(n_chunks):
                src = x_dram.rearrange("b (c p) f -> p (b c) f", p=TP)[:, i * chunk:(i + 1) * chunk, :]
                wait(sp, multiplied, i - 1)
                sp.dma_start(xs[:, i % 2], src).then_inc(loaded[i % 2], 16)
                if i == 0:
                    sp.dma_start(k.fc[:], fpack_dram).then_inc(const_loaded, 16)
                    sp.dma_start(k.bc[:], bpack_dram).then_inc(const_loaded, 16)
            sp.wait_ge(s_copied, len(groups))
            for n, (a, e) in enumerate(groups):
                sp.dma_start(s_dram[a:e, :], s_rows[0:e - a, n, :]).then_inc(s_stored, 16)
            sp.wait_ge(s_stored, 16 * len(groups))

        @block.vector
        def _(dve):
            own = Tally(dve_own)
            nc.vector.memset(k.half[:], -0.5).then_inc(half_set, 1)
            own.link(dve, nc.vector.memset(t.xT[:], 0.0))
            own.up(nc.vector.memset(t.xT[D:D + 2], 1.0))
            own.up(nc.vector.memset(t.xn[:, :, D:], 0.0))
            own.up(nc.vector.memset(t.ctx[:, :, D:], 0.0))
            own.up(nc.vector.memset(t.RW[:], 0.0))
            own.up(nc.vector.memset(t.maxT[:], 0.0))
            own.up(nc.vector.memset(t.neg_max[:], 0.0))
            own.up(nc.vector.memset(t.Q[:], 0.0))
            own.link(dve, nc.vector.memset(t.K[:], 0.0))
            own.up(nc.vector.memset(t.ctxT[:], 0.0))
            own.wait(dve)
            own.up(nc.vector.memset(t.ctxT[D:D + 1], 1.0))
            dve.wait_ge(w_loaded, 16)
            w = W("score_w").rearrange("p (o f) -> p o f", o=1).to_broadcast((TP, chunk, D))
            for i in range(n_chunks):
                dve.wait_ge(loaded[i % 2], 16 * (i // 2 + 1))
                nc.vector.tensor_tensor(prod[:], xs[:, i % 2], w, ALU.mult).then_inc(multiplied, 1)
                dve.wait_ge(multiplied, i + 1)
                width = D
                while width > 2:
                    width //= 2
                    own.link(dve, nc.vector.tensor_tensor(prod[:, :, 0:width], prod[:, :, 0:width],
                                                          prod[:, :, width:2 * width], ALU.add))
                own.link(dve, nc.vector.tensor_tensor(t.score[:, i * chunk:(i + 1) * chunk],
                                                      prod[:, :, 0], prod[:, :, 1], ALU.add))
            own.up(nc.vector.memset(prod[:, 0, 0:1], 0.0))
            nc.vector.tensor_scalar(t.score[:], t.score[:], 1.0, None, ALU.mult).then_inc(scored, 1)
            for n, (a, e) in enumerate(groups):
                dve.wait_ge(s_turned, n + 1)
                nc.vector.tensor_copy(s_rows[0:e - a, n, :], k.bank[0:e - a, n, 0:TP]).then_inc(s_copied, 1)
            dve.wait_ge(gate_exp, 1)
            own.link(dve, nc.vector.tensor_scalar(t.gate[:], t.gate[:], 1.0, None, ALU.add))
            own.link(dve, nc.vector.reciprocal(t.gate[:], t.gate[:]))
            dve.wait_ge(const_loaded, 32)
            for par in range(2):
                for h in range(H0):
                    at = 0 if h % 2 == 0 else D
                    own.up(nc.vector.tensor_copy(t.K[at:at + D, par, h, :], F("pe")[at:at + D, :]))
            dve.wait_ge(folded, 1)
            for n in range(2):
                own.up(nc.vector.tensor_copy(t.RW[0:D + 2, n, :], k.bank[0:D + 2, 2 + n, 0:H0 * D]))

        @block.scalar
        def _(act):
            act.wait_ge(scored, 1)
            nc.scalar.activation(t.gate[:], t.score[:], ACT.Exp, scale=-1.0).then_inc(gate_exp, 1)

        @block.tensor
        def _(pe):
            pe.wait_ge(w_loaded, 16)
            for n, name in enumerate(("wposT", "wposT_swap")):
                for h in range(H0):
                    last = nc.tensor.matmul(k.bank[0:D + 2, 2 + n, h * D:(h + 1) * D], W("wqT")[:, h, :],
                                            W(name)[:, h, :], start=True, stop=True)
            last.then_inc(folded, 1)
            pe.wait_ge(const_loaded, 32)
            pe.wait_ge(scored, 1)
            for n, (a, e) in enumerate(groups):
                nc.tensor.transpose(k.bank[0:e - a, n, 0:TP], t.score[:, a:e],
                                    F("ident")[0:TP, 0:TP]).then_inc(s_turned, 1)




class SelectAttend:

    def __init__(self, k, ctx):
        nb = k.nb
        sb = lambda name, shape, dt=F32: ctx.enter_context(k.nc.sbuf_tensor(name, shape, dt))
        self.x = sb("x_tokens", [TP, 2, CI, D])
        self.score = sb("score", [TP, nb * CI])
        self.gate = sb("gate", [TP, nb * CI])
        self.s_row = sb("s_row", [TP, 2, N_IN])
        self.s_loc = sb("s_loc", [TP, CI])
        self.xg = sb("x_gated", [TP, CI, D])
        self.counted = sb("counted", [TP, N_IN], BF16)
        self.rank = sb("rank", [TP, CI])
        self.hot = sb("one_hot", [TP, CI, S])
        self.h_new = sb("h_new", [TP, NT * D])
        self.stats = sb("stats", [TP, NT, 6])
        self.mv = sb("mean_var", [TP, NT, 2])
        self.rstd = sb("rstd", [TP, NT])
        self.xn = sb("xn", [TP, NT, 128])
        self.xT = sb("xT", [96, 2, S + 1])
        self.RW = sb("RW", [96, 2, H0 * D])
        self.rot = sb("rot", [128, 4, S])
        self.Q = sb("Q", [128, 2 * H0, 2, S])
        self.K = sb("K", [128, 2, H0, S])
        self.q_tok = sb("q_tok", [TP, NT, D])
        self.v_aug = sb("v_aug", [TP, 2, NT, 128])
        self.v_next = sb("v_next", [TP, 2, NT, D])
        self.qk = sb("qk_next", [TP, NT, D])
        self.s_next = sb("s_next", [TP, NT, H0])
        self.mx = sb("mx", [TP, NT, H0])
        self.neg_max = sb("neg_max", [TP, NT, 96], BF16)
        self.maxT = sb("maxT", [96, 2, S], BF16)
        self.e_next = sb("e_next", [TP, 2, NT * H0])
        self.E = sb("E", [TP, 4, 4 * TP])
        self.cT = sb("cT", [128, S])
        self.e_v = sb("e_v", [TP, NT * H0, DH])
        self.den = sb("den", [TP, NT, H0])
        self.ctx = sb("ctx", [TP, NT, 128])
        self.ctxT = sb("ctxT", [96, S])

    def Qb(self, par):
        return self.Q[:, par * H0:(par + 1) * H0]


def select_attend(k, t, x_dram, s_dram):
    nc, nb, F, B, W, bank = k.nc, k.nb, k.F, k.B, k.W, k.bank
    sem = lambda n: k.sem("a_" + n)
    row_loaded, x_loaded, ranked, hot_ready, gathered, h_copied = map(sem, ("row_loaded", "x_loaded", "ranked", "hot", "gathered", "h_copied"))
    var_ready, rstd_ready, xn_ready, x_turned, xT_ready = map(sem, ("var", "rstd", "xn", "x_turned", "xT"))
    pv_ready, pa_ready = sem("proj_for_dve"), sem("proj_for_act")
    pv_free, pa_free = sem("proj_by_dve"), sem("proj_by_act")
    Q_rows = sem("Q_rows")
    m_ready, m_free, e_ready, e_done, pv_done = map(sem, ("m_ready", "m_free", "e_ready", "e_done", "pv_done"))
    neg_ready, neg_turned, maxT_ready, snext_ready, enext_ready = map(sem, ("neg", "neg_turned", "maxT", "snext", "enext"))
    cT_ready, ctx_turned, tok_ready, ctx_ready, ctxT_turned, ctxT_ready, out_ready, out_added = map(
        sem, ("cT", "c_turned", "tok", "ctx", "ctx_turned", "ctxT", "out", "out_added"))
    own_dve, own_act, own_pool, own_pe, own_sp = map(sem, ("own_dve", "own_act", "own_pool", "own_pe", "own_sp"))

    def q_unit(it):
        return ((0, 0, 0, TP * (it + 1)), (1, TP * it, TP * (it + 1), TP * (NT - it)))

    def k_unit(jt):
        return ((0, TP * jt, 0, TP * (NT - jt)), (1, 0, TP * (NT - jt), TP * (jt + 1)))

    def rows(h):
        return 96 if h % 2 == 0 else 128

    units = [(tile, h) for tile in range(NT) for h in range(H0)]
    NU = len(units)
    LAG = 2

    with nc.Block() as block:

        @block.sync
        def _(sp):
            def step(b, par):
                if alive(b, nb):
                    wait(sp, ranked, (b - 1) * CI)
                    wait(sp, x_loaded, b * 16)
                    wait(sp, row_loaded, b * 16)
                    sp.dma_start(t.s_row[:, par, :], s_row_of(b)).then_inc(row_loaded, 16)
                    sp.dma_start(t.x[:, par], x_dram[bass.ds(b, 1)].rearrange("o (c p) f -> p (o c) f", p=TP)
                                 ).then_inc(x_loaded, 16)

            def s_row_of(b):
                flat = s_dram.rearrange("(b c) p -> b (c p)", c=CI)
                return flat[bass.ds(b, 1), :].to_broadcast((TP, N_IN))

            rounds(sp, step, 3, Tally(own_sp), nb)

        @block.tensor
        def _(pe):
            def project(b, par, third):
                xT = t.xT[:, par, :]
                if third == 0:
                    pe.wait_ge(xT_ready, b + 1)
                    wait(pe, maxT_ready, b - 1)
                n = [b * 6 + 2 * third, b * 5 + 2 * third]

                def fill(which, parts):
                    wait(pe, (pv_free, pa_free)[which], n[which])
                    for out, lhsT, rhs in parts:
                        last = nc.tensor.matmul(out, lhsT, rhs, start=True, stop=True)
                    last.then_inc((pv_ready, pa_ready)[which], 1)
                    n[which] = n[which] + 1

                x = xT[:, 0:S]
                full = lambda bk: bank[:, bk, 0:S]
                tile = lambda it: xT[:, it * TP:(it + 1) * TP]
                after = lambda it: xT[:, it * TP + 1:(it + 1) * TP + 1]
                if third < 2:
                    cols = slice(third * 128, (third + 1) * 128)
                    fill(0, [(full(1), t.RW[:, 0, cols], x)])
                    fill(1, [(full(2), W("wck")[:, third, :], x)])
                    fill(0, [(full(1), t.RW[:, 1, cols], x)])
                    fill(1, [(full(2), W("wcq")[:, third, :], x)])
                    return
                fill(0, [(bank[0:TP, 1, it * D:(it + 1) * D], tile(it), W("wq_tok")) for it in range(NT)])
                fill(1, [(bank[0:TP, 2, it * 128:(it + 1) * 128], tile(it), W("wv_aug")) for it in range(NT)])
                fill(0, [(bank[0:TP, 1, it * 128:(it + 1) * 128], after(it), W("wkv_next")) for it in range(NT)])

            def scores_for_exp(b, par, n):
                jt, h = units[n]
                if n == 0:
                    pe.wait_ge(maxT_ready, b + 1)
                wait(pe, e_done, b * NU + n - 1)
                out = bank[0:TP, 4 + n % 2, :]
                key = t.K[0:rows(h), par, h, jt * TP:(jt + 1) * TP]
                for part, q0, c0, cols in k_unit(jt):
                    nc.tensor.matmul(out[:, c0:c0 + cols], key, t.Qb(par)[0:rows(h), h, part, q0:q0 + cols],
                                     start=part == 0, stop=False, skip_group_check=True)
                    nc.tensor.matmul(out[:, c0:c0 + cols], B("pick_head")[:, h, :], t.maxT[:, par, q0:q0 + cols],
                                     start=False, stop=False, skip_group_check=True)
                nc.tensor.matmul(out[:, 0:TP], B("ident_b")[0:TP, 0:TP], B("m_low_k"),
                                 start=False, stop=False, skip_group_check=True)
                w = TP if jt == 0 else 2 * TP
                nc.tensor.matmul(out[:, 4 * TP - w:4 * TP], B("ident_b")[0:TP, 0:TP], B("m_up_k")[:, 2 * TP - w:],
                                 start=False, stop=True, skip_group_check=True).then_inc(e_ready, 1)

            def scores_for_max(b, par, n):
                it, h = units[n]
                if n == 0:
                    pe.wait_ge(Q_rows, (b + 1) * 2)
                    pe.wait_ge(pa_free, b * 5 + 5)
                wait(pe, m_free, b * NU + n - 1)
                out = bank[0:TP, 6 + n % 2, :]
                for part, j0, c0, cols in q_unit(it):
                    nc.tensor.matmul(out[:, c0:c0 + cols], t.Qb(par)[0:rows(h), h, part, it * TP:(it + 1) * TP],
                                     t.K[0:rows(h), par, h, j0:j0 + cols],
                                     start=part == 0, stop=False, skip_group_check=True)
                nc.tensor.matmul(out[:, it * TP:(it + 1) * TP], B("ident_b")[0:TP, 0:TP], B("m_low_q"),
                                 start=False, stop=False, skip_group_check=True)
                w = TP if it == NT - 1 else 2 * TP
                c0 = TP * (it + 1)
                nc.tensor.matmul(out[:, c0:c0 + w], B("ident_b")[0:TP, 0:TP], B("m_up_q")[:, 0:w],
                                 start=False, stop=True, skip_group_check=True).then_inc(m_ready, 1)

            def weigh_values(b, par, n):
                jt, h = units[n]
                pe.wait_ge(e_done, b * NU + n + 1)
                if n == 0:
                    wait(pe, out_added, b)
                for part, q0, c0, cols in k_unit(jt):
                    last = nc.tensor.matmul(bank[32 * h:32 * h + 32, 3, q0:q0 + cols],
                                            t.v_aug[:, par, jt, 32 * h:32 * h + 32], t.E[:, n % 4, c0:c0 + cols],
                                            start=(jt == 0 and part == 0), stop=(jt == NT - 1 and part == 1),
                                            skip_group_check=True)
                last.then_inc(pv_done, 1)

            def turn_context(b):
                pe.wait_ge(cT_ready, b + 1)
                for it in range(NT):
                    last = nc.tensor.transpose(bank[0:TP, 3, it * 128:(it + 1) * 128],
                                               t.cT[:, it * TP:(it + 1) * TP], F("ident"))
                last.then_inc(ctx_turned, 1)

            def turn_divided(b):
                pe.wait_ge(ctx_ready, b + 1)
                for it in range(NT):
                    last = nc.tensor.transpose(bank[:, 3, it * TP:(it + 1) * TP], t.ctx[:, it, :],
                                               F("ident")[0:TP, 0:TP])
                last.then_inc(ctxT_turned, 1)

            def project_out(b):
                pe.wait_ge(ctxT_ready, b + 1)
                for it in range(NT):
                    last = nc.tensor.matmul(bank[0:TP, 3, it * D:(it + 1) * D], t.ctxT[:, it * TP:(it + 1) * TP],
                                            W("wout"), start=True, stop=True)
                last.then_inc(out_ready, 1)

            def turn_max(b):
                pe.wait_ge(neg_ready, b + 1)
                pe.wait_ge(pa_free, 5 * (min(b + 2, nb) if isinstance(b, int) else b + 2))
                for it in range(NT):
                    last = nc.tensor.matmul(bank[0:96, 2, it * TP:(it + 1) * TP], t.neg_max[:, it, :],
                                            B("ident_b")[0:TP, 0:TP], start=True, stop=True)
                last.then_inc(neg_turned, 1)

            def gather(b, par):
                pe.wait_ge(hot_ready, b + 1)
                wait(pe, xT_ready, b)
                for it in range(NT):
                    for c in range(CI):
                        last = nc.tensor.matmul(bank[0:TP, 0, it * D:(it + 1) * D],
                                                t.hot[:, c, it * TP:(it + 1) * TP], t.xg[:, c, :],
                                                start=c == 0, stop=c == CI - 1)
                last.then_inc(gathered, 1)

            def turn_tokens(b):
                pe.wait_ge(xn_ready, b + 1)
                for it in range(NT):
                    last = nc.tensor.transpose(bank[:, 0, it * TP:(it + 1) * TP], t.xn[:, it, :],
                                               F("ident")[0:TP, 0:TP])
                last.then_inc(x_turned, 1)

            def step(r, par):
                b1, b2, b3 = r - 1, r - 2, r - 3
                for third in range(3):
                    if alive(b1, nb):
                        project(b1, 1 - par, third)
                    if alive(b3, nb):
                        (turn_context, turn_divided, project_out)[third](b3)
                for n in range(NU + LAG):
                    if alive(b1, nb) and n < NU:
                        scores_for_max(b1, 1 - par, n)
                    if alive(b2, nb):
                        if n == 1:
                            turn_max(b2)
                        if n >= LAG:
                            scores_for_exp(b2, par, n - LAG)
                        if n >= LAG + 2:
                            weigh_values(b2, par, n - LAG - 2)
                    if alive(r, nb):
                        if n == 8:
                            gather(r, par)
                        if n == 13:
                            turn_tokens(r)
                if alive(b2, nb):
                    weigh_values(b2, par, NU - 2)
                    weigh_values(b2, par, NU - 1)

            rounds(pe, step, 3, Tally(own_pe), nb)

        @block.vector
        def _(dve):
            own = Tally(own_dve)

            def projections(b, par, third):
                n = b * 6
                if third < 2:
                    wait(dve, Q_rows, b * 2 + third)
                    for i, (low, up) in enumerate((("cos_low", "cos_up"), ("sin_low", "sin_up"))):
                        dve.wait_ge(pv_ready, n + 2 * third + i + 1)
                        nc.vector.tensor_tensor(t.rot[:, i, :], bank[:, 1, 0:S], F(low), ALU.mult)
                        nc.vector.tensor_tensor(t.rot[:, 2 + i, 0:S - 1], bank[:, 1, 1:S], F(up),
                                                ALU.mult).then_inc(pv_free, 1)
                    return
                dve.wait_ge(pv_ready, n + 5)
                nc.vector.tensor_copy(flat3(t.q_tok[:]), bank[0:TP, 1, 0:NT * D]).then_inc(pv_free, 1)
                dve.wait_ge(pv_free, n + 5)
                dve.wait_ge(pv_ready, n + 6)
                kv = bank[0:TP, 1, 0:NT * 128].rearrange("p (a b) -> p a b", a=NT)
                nc.vector.tensor_tensor(t.qk[:], t.q_tok[:], kv[:, :, 0:D], ALU.mult)
                wait(dve, ctx_ready, b - 1)
                nc.vector.tensor_copy(t.v_next[:, par], kv[:, :, D:2 * D]).then_inc(pv_free, 1)
                dve.wait_ge(pv_free, n + 6)
                wait(dve, enext_ready, b)
                own.link(dve, nc.vector.tensor_reduce(flat3(t.s_next[:]), t.qk[:].rearrange("p a (h d) -> p (a h) d", h=H0),
                                                      AX, ALU.add))
                own.up(nc.vector.tensor_tensor(t.s_next[:], t.s_next[:], F("no_next"), ALU.add))

            def maxima(b, n):
                it, h = units[n]
                if n == 0:
                    wait(dve, neg_ready, b)
                dve.wait_ge(m_ready, b * NU + n + 1)
                nc.vector.tensor_reduce(t.mx[:, it, h:h + 1], bank[0:TP, 6 + n % 2, 0:4 * TP], AX,
                                        ALU.max).then_inc(m_free, 1)

            def negate_max(b):
                dve.wait_ge(m_free, (b + 1) * NU)
                own.link(dve, nc.vector.tensor_tensor(t.mx[:], t.mx[:], t.s_next[:], ALU.max))
                wait(dve, neg_turned, b)
                nc.vector.tensor_scalar(t.neg_max[:, :, 0:H0], t.mx[:], -1.0, None, ALU.mult).then_inc(neg_ready, 1)
                dve.wait_ge(neg_ready, b + 1)
                nc.vector.tensor_tensor(t.s_next[:], t.s_next[:], t.neg_max[:, :, 0:H0], ALU.add).then_inc(snext_ready, 1)

            def take(b, par):
                own.up(nc.vector.tensor_scalar(t.s_loc[:], t.score[:, bass.ds(b * CI, CI)], 1.0, None, ALU.mult))
                wait(dve, gathered, b)
                dve.wait_ge(x_loaded, (b + 1) * 16)
                own.up(nc.vector.tensor_tensor(t.xg[:], t.x[:, par],
                                               t.gate[:, bass.ds(b * CI, CI)].rearrange("p (c o) -> p c o", o=1)
                                               .to_broadcast((TP, CI, D)), ALU.mult))
                own.wait(dve)
                dve.wait_ge(row_loaded, (b + 1) * 16)

            def count(b, par, c):
                wait(dve, ranked, b * CI + c)
                nc.vector.scalar_tensor_tensor(t.counted[:], t.s_row[:, par, :], t.s_loc[:, c:c + 1], B("tie")[:, c, :],
                                               ALU.subtract, ALU.is_ge,
                                               accum_out=t.rank[:, c:c + 1]).then_inc(ranked, 1)

            def one_hot(b):
                wait(dve, gathered, b)
                dve.wait_ge(ranked, (b + 1) * CI)
                for c in range(CI):
                    last = nc.vector.tensor_scalar(t.hot[:, c, :], F("iota"), t.rank[:, c:c + 1], None, ALU.is_equal)
                last.then_inc(hot_ready, 1)

            def divide(b, par):
                dve.wait_ge(enext_ready, b + 1)
                e = t.e_next[:, par, :]
                wide = lambda v: v.rearrange("p (a o) -> p a o", o=1).to_broadcast((TP, NT * H0, DH))
                own.up(nc.vector.tensor_tensor(t.e_v[:], t.v_next[:, par].rearrange("p a (h d) -> p (a h) d", h=H0),
                                               wide(e), ALU.mult))
                own.wait(dve)
                dve.wait_ge(ctx_turned, b + 1)
                c = bank[0:TP, 3, 0:NT * 128].rearrange("p (a d) -> p a d", d=32)
                den = flat3(t.den[:])
                own.link(dve, nc.vector.tensor_tensor(den, c[:, :, DH], e, ALU.add))
                own.up(nc.vector.reciprocal(den, den))
                wait(dve, ctxT_turned, b)
                own.link(dve, nc.vector.tensor_tensor(t.e_v[:], c[:, :, 0:DH], t.e_v[:], ALU.add))
                for it in range(NT):
                    heads = slice(it * H0, (it + 1) * H0)
                    last = nc.vector.tensor_tensor(t.ctx[:, it, 0:D].rearrange("p (h d) -> p h d", h=H0), t.e_v[:, heads, :],
                                                   den[:, heads].rearrange("p (h o) -> p h o", o=1)
                                                   .to_broadcast((TP, H0, DH)), ALU.mult)
                last.then_inc(ctx_ready, 1)

            def add_out(b):
                dve.wait_ge(out_ready, b + 1)
                h = one(k.h, b)
                nc.vector.tensor_tensor(h, h, bank[0:TP, 3, 0:NT * D], ALU.add).then_inc(out_added, 1)

            def receive(b):
                dve.wait_ge(gathered, b + 1)
                wait(dve, xn_ready, b)
                nc.vector.tensor_copy(t.h_new[:], bank[0:TP, 0, 0:NT * D]).then_inc(h_copied, 1)
                dve.wait_ge(h_copied, b + 1)
                for it in range(NT):
                    own.up(nc.vector.bn_stats(t.stats[:, it, :], t.h_new[:, it * D:(it + 1) * D]))
                own.wait(dve)
                own.up(nc.vector.tensor_scalar(one(k.h, b), t.h_new[:], 1.0, None, ALU.mult))
                for it in range(NT):
                    last = nc.vector.bn_aggr(t.mv[:, it, :], t.stats[:, it, :])
                last.then_inc(var_ready, 1)

            def normalise(b):
                dve.wait_ge(var_ready, b + 1)
                dve.wait_ge(rstd_ready, b + 1)
                wait(dve, x_turned, b)
                for it in range(NT):
                    last = nc.vector.tensor_scalar(t.xn[:, it, 0:D], t.h_new[:, it * D:(it + 1) * D],
                                                   t.mv[:, it, 0:1], t.rstd[:, it:it + 1], ALU.subtract, ALU.mult)
                last.then_inc(xn_ready, 1)

            def step(r, par):
                b1, b2, b3 = r - 1, r - 2, r - 3
                for third in range(3):
                    if alive(b1, nb):
                        projections(b1, 1 - par, third)
                    if third == 0 and alive(b3, nb):
                        divide(b3, 1 - par)
                if alive(b3, nb):
                    add_out(b3)
                if alive(r, nb):
                    take(r, par)
                for n in range(NU):
                    if alive(b1, nb):
                        maxima(b1, n)
                    if alive(r, nb):
                        if n < CI:
                            count(r, par, n)
                        if n == CI:
                            one_hot(r)
                        if n == 8:
                            receive(r)
                        if n == 10:
                            normalise(r)
                if alive(b1, nb):
                    negate_max(b1)

            rounds(dve, step, 3, own, nb)

        @block.scalar
        def _(act):
            def projections(b, par, third):
                n = b * 5
                if third == 0:
                    wait(act, e_ready, (b - 1) * NU)
                if third < 2:
                    for i in range(2):
                        act.wait_ge(pa_ready, n + 2 * third + i + 1)
                        for h in (2 * third, 2 * third + 1):
                            at = D if h % 2 == 0 else 0
                            src = bank[at:at + 32, 2, 0:S]
                            if i == 0:
                                last = nc.scalar.copy(t.K[at:at + 32, par, h, :], src)
                            else:
                                last = nc.scalar.copy(t.Qb(par)[at:at + 32, h, :, :],
                                                      src.rearrange("p (o q) -> p o q", o=1).to_broadcast((32, 2, S)))
                        last.then_inc(pa_free, 1)
                    return
                act.wait_ge(pa_ready, n + 5)
                wait(act, pv_done, (b - 1) * NU)
                nc.scalar.copy(flat3(t.v_aug[:, par]), bank[0:TP, 2, 0:NT * 128]).then_inc(pa_free, 1)

            def exponentials(b, n):
                act.wait_ge(e_ready, b * NU + n + 1)
                wait(act, pv_done, b * NU + n - 3)
                nc.scalar.activation(t.E[:, n % 4], bank[0:TP, 4 + n % 2, 0:4 * TP], ACT.Exp,
                                     scale=float(D) ** -0.5).then_inc(e_done, 1)

            def keep_context(b):
                act.wait_ge(pv_done, (b + 1) * NU)
                wait(act, ctx_turned, b)
                nc.scalar.copy(t.cT[:], bank[:, 3, 0:S]).then_inc(cT_ready, 1)

            def keep_divided(b):
                act.wait_ge(ctxT_turned, b + 1)
                wait(act, out_ready, b)
                nc.scalar.copy(t.ctxT[0:D, :], bank[0:D, 3, 0:S]).then_inc(ctxT_ready, 1)

            def keep_max(b, par):
                act.wait_ge(neg_turned, b + 1)
                wait(act, e_ready, (b - 1) * NU)
                nc.scalar.copy(t.maxT[:, par, :], bank[0:96, 2, 0:S]).then_inc(maxT_ready, 1)

            def weigh_next(b, par):
                act.wait_ge(snext_ready, b + 1)
                wait(act, out_added, b - 1)
                nc.scalar.activation(t.e_next[:, par, :], flat3(t.s_next[:]), ACT.Exp,
                                     scale=float(D) ** -0.5).then_inc(enext_ready, 1)

            def receive(b, par):
                act.wait_ge(x_turned, b + 1)
                wait(act, pv_ready, (b - 1) * 6)
                nc.scalar.activation(t.xT[0:D, par, 0:S], bank[0:D, 0, 0:S], ACT.Identity, bias=W("beta"),
                                     scale=W("gamma")).then_inc(xT_ready, 1)

            def step(r, par):
                b1, b2, b3 = r - 1, r - 2, r - 3
                if alive(b3, nb):
                    keep_context(b3)
                for third in range(3):
                    if alive(b1, nb):
                        projections(b1, 1 - par, third)
                    if third == 0 and alive(b2, nb):
                        weigh_next(b2, par)
                    if third == 1 and alive(b3, nb):
                        keep_divided(b3)
                for n in range(NU + LAG):
                    if alive(b2, nb):
                        if n == 1:
                            keep_max(b2, par)
                        if n >= LAG:
                            exponentials(b2, n - LAG)
                    if alive(r, nb) and n == 13:
                        receive(r, par)

            rounds(act, step, 3, Tally(own_act), nb)

        @block.gpsimd
        def _(pool):
            own = Tally(own_pool)

            def rotations(b, par):
                wait(pool, e_ready, (b - 1) * NU)
                for p in range(2):
                    pool.wait_ge(pv_free, b * 6 + 2 * p + 2)
                    for h in (2 * p, 2 * p + 1):
                        at = 0 if h % 2 == 0 else D
                        for part, cols in ((0, S), (1, S - 1)):
                            a = t.rot[at:at + D, 2 * part, 0:cols]
                            c = t.rot[at:at + D, 2 * part + 1, 0:cols]
                            last = nc.gpsimd.tensor_tensor(t.Qb(par)[at:at + D, h, part, 0:cols], a, c, ALU.add)
                    last.then_inc(Q_rows, 1)

            def normalise(b):
                pool.wait_ge(var_ready, b + 1)
                own.link(pool, nc.gpsimd.tensor_tensor(t.rstd[:], t.mv[:, :, 1], F("one_eps")[:, 0:NT], ALU.mult))
                own.link(pool, nc.gpsimd.tensor_tensor(t.rstd[:], t.rstd[:], F("eps_eps")[:, 0:NT], ALU.add))
                nc.gpsimd.tensor_tensor(t.rstd[:], t.rstd[:], k.half[:, 0:NT], ALU.pow).then_inc(rstd_ready, 1)

            def step(r, par):
                if alive(r - 1, nb):
                    rotations(r - 1, 1 - par)
                if alive(r, nb):
                    normalise(r)

            rounds(pool, step, 3, own, nb)




class Norm:

    def __init__(self, k, ctx, phase, bank=0):
        nc = k.nc
        self.bank = k.bank[:, bank]
        sb = lambda name, shape, dt=F32: ctx.enter_context(nc.sbuf_tensor(phase + name, shape, dt))
        sem = lambda n: k.sem(phase + n)
        self.k = k
        self.carry = sb("carry", [TP, 1])
        self.h, self.stats, self.mv = sb("h_loc", [TP, NT * D]), sb("stats", [TP, NT, 6]), sb("mean_var", [TP, NT, 2])
        self.rstd, self.xn, self.xT = sb("rstd", [TP, NT]), sb("xn", [TP, NT, 128]), sb("xT", [96, 2, S])
        self.copied, self.summed, self.var, self.root = sem("copied"), sem("summed"), sem("var"), sem("root")
        self.root_own, self.applied, self.turned, self.kept = sem("root_own"), sem("applied"), sem("turned"), sem("kept")

    def clear(self, dve, own):
        nc = self.k.nc
        own.link(dve, nc.vector.memset(self.xT[:], 0.0))
        own.up(nc.vector.memset(self.xT[D:D + 1], 1.0))
        own.up(nc.vector.memset(self.xn[:, :, D:], 0.0))

    def start(self, dve, b):
        nc = self.k.nc
        wait(dve, self.applied, b)
        nc.vector.tensor_scalar(self.h[:], one(self.k.h, b), 1.0, None, ALU.mult).then_inc(self.copied, 1)
        dve.wait_ge(self.copied, b + 1)
        for it in range(NT):
            last = nc.vector.bn_stats(self.stats[:, it, :], self.h[:, it * D:(it + 1) * D])
        last.then_inc(self.summed, 1)
        dve.wait_ge(self.summed, b + 1)
        nc.vector.memset(self.carry[:], 0.0)
        for it in range(NT):
            last = nc.vector.bn_aggr(self.mv[:, it, :], self.stats[:, it, :])
        last.then_inc(self.var, 1)

    def take_root(self, pool, b):
        nc = self.k.nc
        pool.wait_ge(self.var, b + 1)
        nc.gpsimd.tensor_tensor(self.rstd[:], self.mv[:, :, 1], self.k.F("eps")[:, 0:NT], ALU.add).then_inc(self.root_own, 1)
        pool.wait_ge(self.root_own, b + 1)
        nc.gpsimd.tensor_tensor(self.rstd[:], self.rstd[:], self.k.half[:, 0:NT], ALU.pow).then_inc(self.root, 1)

    def apply(self, dve, b):
        nc = self.k.nc
        dve.wait_ge(self.var, b + 1)
        dve.wait_ge(self.root, b + 1)
        wait(dve, self.turned, b)
        for it in range(NT):
            last = nc.vector.tensor_scalar(self.xn[:, it, 0:D], self.h[:, it * D:(it + 1) * D], self.mv[:, it, 0:1],
                                           self.rstd[:, it:it + 1], ALU.subtract, ALU.mult)
        last.then_inc(self.applied, 1)

    def turn(self, pe, b):
        nc, k = self.k.nc, self.k
        pe.wait_ge(self.applied, b + 1)
        for it in range(NT):
            last = nc.tensor.transpose(self.bank[:, it * TP:(it + 1) * TP], self.xn[:, it, :],
                                       k.F("ident")[0:TP, 0:TP])
        last.then_inc(self.turned, 1)

    def keep(self, act, b, par, users):
        nc, k = self.k.nc, self.k
        act.wait_ge(self.turned, b + 1)
        for s, value in users:
            wait(act, s, value)
        nc.scalar.copy(self.xT[0:D, par, :], self.bank[0:D, 0:S]).then_inc(self.kept, 1)




def experts(k):
    nc, nb, F, B, W, bank = k.nc, k.nb, k.F, k.B, k.W, k.bank
    with ExitStack() as ctx:
        sb = lambda name, shape, dt=F32: ctx.enter_context(nc.sbuf_tensor("x_" + name, shape, dt))
        sem = lambda n: k.sem("x_" + n)
        norm = Norm(k, ctx, "xn_")
        top, shifted, prob = sb("top", [TP, NT]), sb("shifted", [TP, NT * NE]), sb("prob", [TP, NT * NE])
        total = sb("total", [TP, NT])
        ahead, same = sb("ahead", [TP, NT, NE, NE], BF16), sb("same", [TP, NT, NE, NE], BF16)
        rank, cw, rest = sb("rank", [TP, NT * NE]), sb("cw", [TP, NT, NE]), sb("rest", [TP, NT, NE])
        parts = sb("parts", [TP, NT, 3 * NE], BF16)
        partsT, partsTf = sb("partsT", [96, 2, S], BF16), sb("partsTf", [3 * NE, 2, S])
        hid, hidw = sb("hidden", [DE, 3, S]), sb("hidden_w", [DE, 3, S])
        yT = sb("yT", [128, S])
        logits, shift_ready, exp_ready, cw_ready, cw_turned, cw_kept = map(
            sem, ("logits", "shift", "exp", "cw", "cw_turned", "cw_kept"))
        hid_ready, gelu_done, spread, weighed, down = map(sem, ("hid", "gelu", "spread", "weighed", "down"))
        y_kept, out_ready, added, own_dve = map(sem, ("y_kept", "out", "added", "own_dve"))
        own_x = [Tally(sem("own" + n)) for n in ("pe", "act", "pool")]
        cleared = sem("cleared")
        block = ctx.enter_context(nc.Block())

        @block.tensor
        def _(pe):
            pe.wait_ge(cleared, 1)

            def up(b, par, e):
                n = b * NE + e
                if e == 0:
                    pe.wait_ge(norm.kept, b + 1)
                    pe.wait_ge(cw_kept, b + 1)
                wait(pe, gelu_done, n - 1)
                nc.tensor.matmul(bank[:, 2 + e % 2, 0:S], W("w1")[:, e, :], norm.xT[:, par, :], start=True,
                                 stop=True).then_inc(hid_ready, 1)
                wait(pe, weighed, n - 1)
                nc.tensor.matmul(bank[:, 4 + e % 2, 0:S], B("pick_expert")[:, e, :], partsT[:, par, :], start=True,
                                 stop=True).then_inc(spread, 1)

            def go_down(b, e):
                n = b * NE + e
                pe.wait_ge(weighed, n + 1)
                if e == 0:
                    wait(pe, y_kept, b)
                at = D * (e % 2)
                nc.tensor.matmul(bank[at:at + D, 6, 0:S], W("w2")[:, e, :], hidw[:, e % 2, :], start=e < 2,
                                 stop=e >= NE - 2, skip_group_check=True).then_inc(down, 1)

            def gate(b, par):
                pe.wait_ge(norm.kept, b + 1)
                wait(pe, cw_kept, b)
                for it in range(NT):
                    last = nc.tensor.matmul(bank[0:TP, 1, it * NE:(it + 1) * NE], norm.xT[:, par, it * TP:(it + 1) * TP],
                                            W("gate_w"), start=True, stop=True)
                last.then_inc(logits, 1)

            def turn_weights(b):
                pe.wait_ge(cw_ready, b + 1)
                for it in range(NT):
                    last = nc.tensor.matmul(bank[0:3 * NE, 1, it * TP:(it + 1) * TP], parts[:, it, :],
                                            B("ident_b")[0:TP, 0:TP], start=True, stop=True)
                last.then_inc(cw_turned, 1)

            def finish(b, par):
                pe.wait_ge(y_kept, b + 1)
                wait(pe, added, b)
                for it in range(NT):
                    cols = slice(it * TP, (it + 1) * TP)
                    nc.tensor.matmul(bank[0:TP, 7, it * D:(it + 1) * D], yT[:, cols], F("two_halves"), start=True,
                                     stop=False, skip_group_check=True)
                    last = nc.tensor.matmul(bank[0:TP, 7, it * D:(it + 1) * D], partsTf[:, par, cols], W("b2"),
                                            start=False, stop=True, skip_group_check=True)
                last.then_inc(out_ready, 1)

            def step(r, par):
                b = r - 1
                for e in range(NE):
                    if alive(b, nb):
                        up(b, 1 - par, e)
                        if e >= 1:
                            go_down(b, e - 1)
                    if alive(r, nb) and e == 2:
                        norm.turn(pe, r)
                    if alive(r, nb) and e == 4:
                        gate(r, par)
                if alive(b, nb):
                    go_down(b, NE - 1)
                    finish(b, 1 - par)
                if alive(r, nb):
                    turn_weights(r)

            rounds(pe, step, 1, own_x[0], nb)

        @block.scalar
        def _(act):
            def gelu(b, e):
                n = b * NE + e
                act.wait_ge(hid_ready, n + 1)
                wait(act, weighed, n - 1)
                nc.scalar.activation(hid[:, e % 2, :], bank[:, 2 + e % 2, 0:S], ACT.Gelu).then_inc(gelu_done, 1)

            def keep_weights(b, par):
                act.wait_ge(cw_turned, b + 1)
                wait(act, spread, (b - 1) * NE)
                nc.scalar.copy(partsT[0:3 * NE, par, :], bank[0:3 * NE, 1, 0:S])
                wait(act, out_ready, b - 1)
                nc.scalar.copy(partsTf[:, par, :], bank[0:3 * NE, 1, 0:S]).then_inc(cw_kept, 1)

            def step(r, par):
                b = r - 1
                for e in range(NE):
                    if alive(b, nb):
                        gelu(b, e)
                    if alive(r, nb) and e == 2:
                        norm.keep(act, r, par, [(hid_ready, (r - 1) * NE), (logits, r - 1)])
                if alive(b, nb):
                    act.wait_ge(down, b * NE + NE)
                    wait(act, out_ready, b)
                    nc.scalar.copy(yT[:], bank[:, 6, 0:S]).then_inc(y_kept, 1)
                if alive(r, nb):
                    keep_weights(r, par)

            rounds(act, step, 1, own_x[1], nb)

        @block.vector
        def _(dve):
            own = Tally(own_dve)
            norm.clear(dve, own)
            nc.vector.memset(partsT[:], 0.0).then_inc(cleared, 1)

            def weigh(b, e):
                n = b * NE + e
                dve.wait_ge(spread, n + 1)
                dve.wait_ge(gelu_done, n + 1)
                wait(dve, down, n - 1)
                nc.vector.tensor_tensor(hidw[:, e % 2, :], bank[:, 4 + e % 2, 0:S], hid[:, e % 2, :],
                                        ALU.mult).then_inc(weighed, 1)

            v3 = lambda a: a.rearrange("p (t e) -> p t e", t=NT)
            over_e = lambda a: a.rearrange("p (t o) -> p t o", o=1).to_broadcast((TP, NT, NE))

            def shift(b):
                dve.wait_ge(logits, b + 1)
                wait(dve, exp_ready, b)
                lg = bank[0:TP, 1, 0:NT * NE]
                own.link(dve, nc.vector.tensor_reduce(top[:], v3(lg), AX, ALU.max))
                nc.vector.tensor_tensor(v3(shifted[:]), v3(lg), over_e(top[:]), ALU.subtract).then_inc(shift_ready, 1)

            def choose(b):
                dve.wait_ge(exp_ready, b + 1)
                own.link(dve, nc.vector.tensor_reduce(total[:], v3(prob[:]), AX, ALU.add))
                own.link(dve, nc.vector.reciprocal(total[:], total[:]))
                own.link(dve, nc.vector.tensor_tensor(v3(prob[:]), v3(prob[:]), over_e(total[:]), ALU.mult))
                other = prob[:].rearrange("p (t o e) -> p t o e", t=NT, o=1).to_broadcast((TP, NT, NE, NE))
                mine = prob[:].rearrange("p (t e o) -> p t e o", t=NT, o=1).to_broadcast((TP, NT, NE, NE))
                own.up(nc.vector.tensor_tensor(same[:], other, mine, ALU.is_equal))
                own.link(dve, nc.vector.tensor_tensor(ahead[:], other, mine, ALU.is_gt))
                early = B("earlier").rearrange("p (o e) -> p o e", o=1).to_broadcast((TP, NT, NE * NE))
                sf = same[:].rearrange("p t a b -> p t (a b)")
                own.link(dve, nc.vector.tensor_tensor(sf, sf, early, ALU.mult))
                own.link(dve, nc.vector.tensor_tensor(ahead[:], ahead[:], same[:], ALU.add))
                own.link(dve, nc.vector.tensor_reduce(rank[:], ahead[:].rearrange("p t a b -> p (t a) b"), AX, ALU.add))
                own.link(dve, nc.vector.scalar_tensor_tensor(cw[:].rearrange("p t e -> p (t e)"), rank[:], 2.0, prob[:],
                                                             ALU.is_lt, ALU.mult))
                wait(dve, cw_turned, b)
                own.link(dve, nc.vector.tensor_copy(parts[:, :, 0:NE], cw[:]))
                own.link(dve, nc.vector.tensor_tensor(rest[:], cw[:], parts[:, :, 0:NE], ALU.subtract))
                own.link(dve, nc.vector.tensor_copy(parts[:, :, NE:2 * NE], rest[:]))
                nc.vector.tensor_tensor(parts[:, :, 2 * NE:], rest[:], parts[:, :, NE:2 * NE],
                                        ALU.subtract).then_inc(cw_ready, 1)

            def step(r, par):
                b = r - 1
                if alive(r, nb):
                    norm.start(dve, r)
                for e in range(NE):
                    if alive(b, nb):
                        weigh(b, e)
                    if alive(r, nb) and e == 0:
                        norm.apply(dve, r)
                    if alive(r, nb) and e == 4:
                        shift(r)
                if alive(r, nb):
                    choose(r)
                if alive(b, nb):
                    dve.wait_ge(out_ready, b + 1)
                    h = one(k.h, b)
                    nc.vector.tensor_tensor(h, h, bank[0:TP, 7, 0:NT * D], ALU.add).then_inc(added, 1)

            rounds(dve, step, 1, own, nb)

        @block.gpsimd
        def _(pool):
            def step(r, par):
                if alive(r, nb):
                    norm.take_root(pool, r)
                    pool.wait_ge(shift_ready, r + 1)
                    wait(pool, cw_ready, r)
                    nc.gpsimd.tensor_tensor(prob[:], F("euler"), shifted[:], ALU.pow).then_inc(exp_ready, 1)

            rounds(pool, step, 1, own_x[2], nb)




def slices(k):
    nc, nb, F, B, W, bank = k.nc, k.nb, k.F, k.B, k.W, k.bank
    R = HS * DS1
    with ExitStack() as ctx:
        sb = lambda name, shape, dt=F32: ctx.enter_context(nc.sbuf_tensor("s_" + name, shape, dt))
        sem = lambda n: k.sem("s_" + n)
        norm = Norm(k, ctx, "sn_")
        WL, MB, rtemp = sb("WL", [96, HS * G]), sb("MB", [R, R]), sb("rtemp", [96, HS])
        top, neg, maxT = sb("top", [TP, NT * HS]), sb("neg", [TP, NT, 96], BF16), sb("maxT", [96, S], BF16)
        E, ET = sb("E", [TP, NT, HS * G]), sb("ET", [128, 2, PS, S])
        rsum, sumv, tin = sb("rsum", [TP, 2, NT * HS]), sb("sum", [TP, NT * HS]), sb("tin", [TP, NT * HS, DS1])
        rnorm, tok, tokT, bothT = sb("rnorm", [128, PS]), sb("tok", [128, 128]), sb("tokT", [R, 128]), sb("bothT", [R, G])
        keys, kq, vals = sb("keys", [R, PS, G]), sb("kq", [R, 128]), sb("vals", [128, PS * DS])
        topA, shA, EA, EAT = sb("topA", [128, PS]), sb("shA", [128, PS, G]), sb("EA", [128, PS, 128]), sb("EAT", [128, PS * 128])
        sumA, OB = sb("sumA", [128, PS]), sb("OB", [128, PS, 2 * DS])
        att, attT = sb("att", [TP, NT, 128]), sb("attT", [96, S])
        set_up, folded, folded_kept = sem("set_up"), sem("folded"), sem("folded_kept")
        t_ready, l_ready, topped, neg_ready, max_turned, max_kept = map(
            sem, ("t", "logits", "topped", "neg", "max_turned", "max_kept"))
        lm_ready, e_done, g_ready, eT_done, summed, tin_ready, sl_ready = map(
            sem, ("less_max", "e", "g", "eT", "summed", "tin", "slices"))
        tok_ready, tok_turned, tokT_ready, keys_ready, kqv_ready, kq_kept, s_ready = map(
            sem, ("tok", "tok_turned", "tokT", "keys", "kqv", "kq_kept", "scores"))
        shA_ready, eA_done, eA_turned, eAT_kept, o_ready, OB_ready, out_ready = map(
            sem, ("shA", "eA", "eA_turned", "eAT", "o", "OB", "out"))
        att_ready, att_turned, attT_kept, res_ready, added, own_dve = map(
            sem, ("att", "att_turned", "attT", "res", "added", "own_dve"))
        own_x = [Tally(sem("own" + n)) for n in ("pe", "act", "pool")]
        block = ctx.enter_context(nc.Block())
        tile = lambda v, par, it: v[:, par, it * TP:(it + 1) * TP]

        @block.tensor
        def _(pe):
            for h in range(HS):
                nc.tensor.matmul(bank[0:D + 1, 6, h * G:(h + 1) * G], W("w_inT")[:, h, :], W("w_slice"),
                                 start=True, stop=True)
            nc.tensor.matmul(bank[0:R, 7, 0:R], W("wq_sT"), W("wk_sT"), start=True, stop=True).then_inc(folded, 1)
            pe.wait_ge(set_up, 1)
            pe.wait_ge(folded_kept, 1)

            def logits(b, par):
                pe.wait_ge(norm.kept, b + 1)
                wait(pe, tok_ready, b)
                for it in range(NT):
                    last = nc.tensor.matmul(bank[0:TP, 1, it * D:(it + 1) * D], tile(norm.xT, par, it), W("w_in"),
                                            start=True, stop=True)
                last.then_inc(t_ready, 1)
                wait(pe, e_done, b)
                for it in range(NT):
                    last = nc.tensor.matmul(bank[0:TP, 2 + it, :], tile(norm.xT, par, it), WL[:], start=True,
                                            stop=False, skip_group_check=True)
                    last.then_inc(l_ready, 1)

            def turn_max(b):
                pe.wait_ge(neg_ready, b + 1)
                wait(pe, eT_done, b * PS)
                for it in range(NT):
                    last = nc.tensor.matmul(bank[0:96, 6, it * TP:(it + 1) * TP], neg[:, it, :],
                                            B("ident_b")[0:TP, 0:TP], start=True, stop=True)
                last.then_inc(max_turned, 1)

            def less_max(b):
                pe.wait_ge(max_kept, b + 1)
                for it in range(NT):
                    last = nc.tensor.matmul(bank[0:TP, 2 + it, :], maxT[:, it * TP:(it + 1) * TP], B("pick_slices"),
                                            start=False, stop=True, skip_group_check=True)
                last.then_inc(lm_ready, 1)

            def turned_logits(b, par, p):
                wait(pe, eT_done, b * PS + p - 1)
                cols = slice(p * 128, (p + 1) * 128)
                nc.tensor.matmul(bank[:, 6 + p % 2, 0:S], WL[:, cols], norm.xT[:, par, 0:S], start=True, stop=False,
                                 skip_group_check=True)
                nc.tensor.matmul(bank[:, 6 + p % 2, 0:S], B("pick_slices")[:, cols], maxT[:], start=False, stop=True,
                                 skip_group_check=True).then_inc(g_ready, 1)

            def gather_slices(b):
                pe.wait_ge(tin_ready, b + 1)
                flat = tin[:].rearrange("p (t h) d -> p t (h d)", t=NT)
                for p in range(PS):
                    for it in range(NT):
                        last = nc.tensor.matmul(bank[:, 1, p * 2 * DS1:(p + 1) * 2 * DS1],
                                                E[:, it, p * 128:(p + 1) * 128],
                                                flat[:, it, p * 2 * DS1:(p + 1) * 2 * DS1],
                                                start=it == 0, stop=it == NT - 1)
                last.then_inc(sl_ready, 1)

            def turn_tokens(b):
                pe.wait_ge(tok_ready, b + 1)
                wait(pe, added, b)
                nc.tensor.transpose(bank[:, 5, 0:128], tok[:], F("ident")).then_inc(tok_turned, 1)

            def project(b):
                pe.wait_ge(tokT_ready, b + 1)
                nc.tensor.matmul(bank[0:R, 5, 0:128], MB[:], tokT[:], start=True, stop=True)
                nc.tensor.matmul(bank[:, 5, 128:128 + PS * DS], tokT[:], W("wv_s"), start=True,
                                 stop=True).then_inc(kqv_ready, 1)

            def scores(b):
                pe.wait_ge(kq_kept, b + 1)
                pe.wait_ge(keys_ready, b + 1)
                nc.tensor.matmul(bank[:, 5, 0:PS * G], kq[:], keys[:].rearrange("p a g -> p (a g)"), start=True,
                                 stop=True).then_inc(s_ready, 1)

            def turn_attention(b):
                pe.wait_ge(eA_done, b + 1)
                for p in range(PS):
                    last = nc.tensor.transpose(bank[:, 5, p * 128:(p + 1) * 128], EA[:, p, :], F("ident"))
                last.then_inc(eA_turned, 1)

            def attend(b):
                pe.wait_ge(eAT_kept, b + 1)
                for p in range(PS):
                    last = nc.tensor.matmul(bank[:, 5, p * DS:(p + 1) * DS], EAT[:, p * 128:(p + 1) * 128],
                                            vals[:, p * DS:(p + 1) * DS], start=True, stop=True)
                last.then_inc(o_ready, 1)

            def spread(b, par):
                pe.wait_ge(OB_ready, b + 1)
                for it in range(NT):
                    for p in range(PS):
                        at = it * D + p * 2 * DS
                        last = nc.tensor.matmul(bank[0:TP, 5, at:at + 2 * DS], ET[:, par, p, it * TP:(it + 1) * TP],
                                                OB[:, p, :], start=True, stop=True)
                last.then_inc(out_ready, 1)

            def turn_out(b):
                pe.wait_ge(att_ready, b + 1)
                for it in range(NT):
                    last = nc.tensor.transpose(bank[:, 5, it * TP:(it + 1) * TP], att[:, it, :], F("ident")[0:TP, 0:TP])
                last.then_inc(att_turned, 1)

            def project_out(b):
                pe.wait_ge(attT_kept, b + 1)
                for it in range(NT):
                    last = nc.tensor.matmul(bank[0:TP, 5, it * D:(it + 1) * D], attT[:, it * TP:(it + 1) * TP],
                                            W("w_out_s"), start=True, stop=True)
                last.then_inc(res_ready, 1)

            def step(r, par):
                b1, b2 = r - 1, r - 2
                one_, two = alive(b1, nb), alive(b2, nb)
                if one_:
                    logits(b1, 1 - par)
                if two:
                    turn_tokens(b2)
                if one_:
                    turn_max(b1)
                if two:
                    project(b2)
                if one_:
                    less_max(b1)
                    turned_logits(b1, 1 - par, 0)
                    turned_logits(b1, 1 - par, 1)
                if two:
                    scores(b2)
                if one_:
                    turned_logits(b1, 1 - par, 2)
                    turned_logits(b1, 1 - par, 3)
                if two:
                    turn_attention(b2)
                    attend(b2)
                if one_:
                    gather_slices(b1)
                if two:
                    spread(b2, par)
                if alive(r, nb):
                    norm.turn(pe, r)
                if two:
                    turn_out(b2)
                    project_out(b2)

            rounds(pe, step, 2, own_x[0], nb)

        @block.scalar
        def _(act):
            def keep_max(b):
                act.wait_ge(max_turned, b + 1)
                wait(act, g_ready, b * PS)
                nc.scalar.copy(maxT[:], bank[0:96, 6, 0:S]).then_inc(max_kept, 1)

            def exps(b):
                act.wait_ge(lm_ready, b + 1)
                wait(act, sl_ready, b)
                nc.scalar.activation(E[:], bank[0:TP, 2:5, :], ACT.Exp).then_inc(e_done, 1)

            def turned_exps(b, par, p):
                act.wait_ge(g_ready, b * PS + p + 1)
                wait(act, out_ready, b - 1)
                nc.scalar.activation(ET[:, par, p, :], bank[:, 6 + p % 2, 0:S], ACT.Exp).then_inc(eT_done, 1)

            def keep_projected(b):
                act.wait_ge(kqv_ready, b + 1)
                wait(act, o_ready, b)
                nc.scalar.copy(kq[:], bank[0:R, 5, 0:128])
                nc.scalar.copy(vals[:], bank[:, 5, 128:128 + PS * DS]).then_inc(kq_kept, 1)

            def attention_exps(b):
                act.wait_ge(shA_ready, b + 1)
                wait(act, OB_ready, b)
                for hh in range(2):
                    rows = slice(hh * G, (hh + 1) * G)
                    last = nc.scalar.activation(EA[rows, :, rows], shA[rows], ACT.Exp)
                last.then_inc(eA_done, 1)

            def step(r, par):
                b1, b2 = r - 1, r - 2
                one_, two = alive(b1, nb), alive(b2, nb)
                if one_:
                    keep_max(b1)
                if two:
                    keep_projected(b2)
                if one_:
                    exps(b1)
                    turned_exps(b1, 1 - par, 0)
                    turned_exps(b1, 1 - par, 1)
                if two:
                    attention_exps(b2)
                if one_:
                    turned_exps(b1, 1 - par, 2)
                    turned_exps(b1, 1 - par, 3)
                if two:
                    act.wait_ge(eA_turned, b2 + 1)
                    wait(act, o_ready, b2)
                    nc.scalar.copy(EAT[:], bank[:, 5, :]).then_inc(eAT_kept, 1)
                if alive(r, nb):
                    norm.keep(act, r, par, [(g_ready, (r - 1) * PS)])
                if two:
                    act.wait_ge(att_turned, b2 + 1)
                    wait(act, res_ready, b2)
                    nc.scalar.copy(attT[0:D, :], bank[0:D, 5, 0:S]).then_inc(attT_kept, 1)

            rounds(act, step, 2, own_x[1], nb)

        @block.vector
        def _(dve):
            own = Tally(own_dve)
            norm.clear(dve, own)
            own.up(nc.vector.memset(WL[:], 0.0))
            own.up(nc.vector.memset(neg[:], 0.0))
            own.up(nc.vector.memset(att[:], 0.0))
            own.up(nc.vector.memset(EA[:], 0.0))
            own.up(nc.vector.memset(OB[:], 0.0))
            own.up(nc.vector.memset(tok[:], 0.0))
            own.link(dve, nc.vector.memset(attT[:], 0.0))
            own.up(nc.vector.memset(attT[D:D + 1], 1.0))
            owned = tok[:, 0:R].rearrange("p (a e) -> p a e", a=PS)
            for hh in range(2):
                at = hh * DS1 + DS
                own.up(nc.vector.memset(owned[hh * G:(hh + 1) * G, :, at:at + 1], 1.0))
            own.link(dve, nc.vector.reciprocal(rtemp[:], W("temperature")))
            dve.wait_ge(folded, 1)
            own.up(nc.vector.tensor_tensor(WL[0:D + 1].rearrange("p (h g) -> p h g", h=HS),
                                           bank[0:D + 1, 6, :].rearrange("p (h g) -> p h g", h=HS),
                                           rtemp[0:D + 1].rearrange("p (h o) -> p h o", o=1)
                                           .to_broadcast((D + 1, HS, G)), ALU.mult))
            nc.vector.tensor_tensor(MB[:], bank[0:R, 7, 0:R], F("slice_block"), ALU.mult).then_inc(folded_kept, 1)
            nc.vector.memset(norm.carry[:], 0.0).then_inc(set_up, 1)

            def maxima(b):
                for it in range(NT):
                    dve.wait_ge(l_ready, b * NT + it + 1)
                    wait(dve, neg_ready, b)
                    last = nc.vector.tensor_reduce(top[:, it * HS:(it + 1) * HS],
                                                   bank[0:TP, 2 + it, :].rearrange("p (h g) -> p h g", h=HS), AX, ALU.max)
                last.then_inc(topped, 1)
                dve.wait_ge(topped, b + 1)
                wait(dve, max_turned, b)
                nc.vector.tensor_scalar(neg[:, :, 0:HS], top[:].rearrange("p (t h) -> p t h", t=NT), -1.0, None,
                                        ALU.mult).then_inc(neg_ready, 1)

            def divide(b, par):
                dve.wait_ge(e_done, b + 1)
                own.link(dve, nc.vector.tensor_reduce(sumv[:], E[:].rearrange("p t (h g) -> p (t h) g", h=HS), AX, ALU.add))
                wait(dve, att_ready, b - 1)
                own.link(dve, nc.vector.reciprocal(rsum[:, par, :], sumv[:]))
                r = rsum[:, par, :].rearrange("p (a o) -> p a o", o=1)
                dve.wait_ge(t_ready, b + 1)
                wait(dve, sl_ready, b)
                nc.vector.tensor_tensor(tin[:, :, 0:DS], bank[0:TP, 1, 0:NT * D].rearrange("p (a d) -> p a d", d=DS),
                                        r.to_broadcast((TP, NT * HS, DS)), ALU.mult)
                nc.vector.tensor_copy(tin[:, :, DS:DS1], r).then_inc(tin_ready, 1)

            def slice_tokens(b):
                dve.wait_ge(sl_ready, b + 1)
                wait(dve, tok_turned, b)
                sl = bank[:, 1, 0:R].rearrange("p (a e) -> p a e", a=PS)
                for hh in range(2):
                    rows = slice(hh * G, (hh + 1) * G)
                    last = nc.vector.tensor_scalar(rnorm[rows, :], sl[rows, :, hh * DS1 + DS], 1e-5, None, ALU.add)
                own.link(dve, last)
                own.link(dve, nc.vector.reciprocal(rnorm[:], rnorm[:]))
                for hh in range(2):
                    rows, cols = slice(hh * G, (hh + 1) * G), slice(hh * DS1, hh * DS1 + DS)
                    last = nc.vector.tensor_tensor(owned[rows, :, cols], sl[rows, :, cols],
                                                   rnorm[rows, :].rearrange("p (a o) -> p a o", o=1)
                                                   .to_broadcast((G, PS, DS)), ALU.mult)
                last.then_inc(tok_ready, 1)

            def turned_tokens(b):
                dve.wait_ge(tok_turned, b + 1)
                wait(dve, kqv_ready, b)
                nc.vector.tensor_copy(tokT[:], bank[0:R, 5, 0:128])
                wait(dve, s_ready, b)
                own.link(dve, nc.vector.tensor_copy(bothT[:], bank[0:R, 5, 0:G]))
                own.up(nc.vector.tensor_tensor(bothT[:], bothT[:], bank[0:R, 5, G:128], ALU.add))
                own.wait(dve)
                nc.vector.memset(norm.carry[:], 0.0).then_inc(tokT_ready, 1)
                nc.vector.tensor_tensor(keys[:], F("own_pair"), bothT[:].rearrange("p (o g) -> p o g", o=1)
                                        .to_broadcast((R, PS, G)), ALU.mult).then_inc(keys_ready, 1)

            def shift(b):
                dve.wait_ge(s_ready, b + 1)
                sc = bank[:, 5, 0:PS * G].rearrange("p (a g) -> p a g", a=PS)
                own.link(dve, nc.vector.tensor_reduce(topA[:], sc, AX, ALU.max))
                wait(dve, eA_done, b)
                nc.vector.tensor_tensor(shA[:], sc, topA[:].rearrange("p (a o) -> p a o", o=1)
                                        .to_broadcast((128, PS, G)), ALU.subtract).then_inc(shA_ready, 1)

            def attended(b):
                dve.wait_ge(eA_done, b + 1)
                own.link(dve, nc.vector.tensor_reduce(sumA[:], EA[:], AX, ALU.add))
                own.link(dve, nc.vector.reciprocal(sumA[:], sumA[:]))
                dve.wait_ge(o_ready, b + 1)
                wait(dve, out_ready, b)
                o = bank[:, 5, 0:PS * DS].rearrange("p (a d) -> p a d", a=PS)
                for hh in range(2):
                    rows = slice(hh * G, (hh + 1) * G)
                    last = nc.vector.tensor_tensor(OB[rows, :, hh * DS:(hh + 1) * DS], o[rows],
                                                   sumA[rows, :].rearrange("p (a o) -> p a o", o=1)
                                                   .to_broadcast((G, PS, DS)), ALU.mult)
                last.then_inc(OB_ready, 1)

            def out(b, par):
                dve.wait_ge(out_ready, b + 1)
                wait(dve, att_turned, b)
                for it in range(NT):
                    last = nc.vector.tensor_tensor(
                        att[:, it, 0:D].rearrange("p (h d) -> p h d", h=HS),
                        bank[0:TP, 5, it * D:(it + 1) * D].rearrange("p (h d) -> p h d", h=HS),
                        rsum[:, par, it * HS:(it + 1) * HS].rearrange("p (h o) -> p h o", o=1)
                        .to_broadcast((TP, HS, DS)), ALU.mult)
                last.then_inc(att_ready, 1)

            def step(r, par):
                b1, b2 = r - 1, r - 2
                one_, two = alive(b1, nb), alive(b2, nb)
                if alive(r, nb):
                    norm.start(dve, r)
                if two:
                    slice_tokens(b2)
                if one_:
                    maxima(b1)
                if two:
                    turned_tokens(b2)
                if alive(r, nb):
                    norm.apply(dve, r)
                if two:
                    shift(b2)
                if one_:
                    divide(b1, 1 - par)
                if two:
                    attended(b2)
                    out(b2, par)
                    dve.wait_ge(res_ready, b2 + 1)
                    h = one(k.h, b2)
                    nc.vector.tensor_tensor(h, h, bank[0:TP, 5, 0:NT * D], ALU.add).then_inc(added, 1)

            rounds(dve, step, 2, own, nb)

        @block.gpsimd
        def _(pool):
            def step(r, par):
                if alive(r, nb):
                    norm.take_root(pool, r)

            rounds(pool, step, 2, own_x[2], nb)




def first_heads(k, res):
    nc, W, bank = k.nc, k.W, k.bank
    with ExitStack() as ctx:
        norm = Norm(k, ctx, "f_")
        ready, read, own_dve = k.sem("f_ready"), k.sem("f_read"), k.sem("f_own_dve")
        block = ctx.enter_context(nc.Block())

        @block.vector
        def _(dve):
            norm.clear(dve, Tally(own_dve))
            for b in range(HE):
                norm.start(dve, b)
                norm.apply(dve, b)
                dve.wait_ge(ready, b + 1)
                nc.vector.tensor_copy(res[:, :, b * DH2:(b + 1) * DH2],
                                      bank[0:TP, 1, 0:NT * DH2].rearrange("p (t d) -> p t d", t=NT)).then_inc(read, 1)

        @block.gpsimd
        def _(pool):
            for b in range(HE):
                norm.take_root(pool, b)

        @block.tensor
        def _(pe):
            for b in range(HE):
                norm.turn(pe, b)
                pe.wait_ge(norm.kept, b + 1)
                wait(pe, read, b)
                for it in range(NT):
                    last = nc.tensor.matmul(bank[0:TP, 1, it * DH2:(it + 1) * DH2],
                                            norm.xT[:, b % 2, it * TP:(it + 1) * TP],
                                            W("w_sx")[:, b * DH2:(b + 1) * DH2], start=True, stop=True)
                last.then_inc(ready, 1)

        @block.scalar
        def _(act):
            for b in range(HE):
                norm.keep(act, b, b % 2, [(ready, b - 1)])


def query_experts(k, res, qk_dram, out):
    nc, nb, F, B, W, bank = k.nc, k.nb, k.F, k.B, k.W, k.bank
    units = [(0, (h,), 3 * TP) for h in range(HE)] + [(1, (0, 1), 2 * TP), (1, (2, 3), 2 * TP), (2, (0, 1, 2, 3), TP)]
    UE = len(units)
    LAG = 2
    NU = EE * UE
    NP = 3
    q_parts, k_parts = (0, 0, 1, 0, 1, 2), (0, 1, 0, 2, 1, 0)
    RS = len(q_parts) * DH2
    with ExitStack() as ctx:
        sb = lambda name, shape, dt=F32: ctx.enter_context(nc.sbuf_tensor("qe_" + name, shape, dt))
        sem = lambda n: k.sem("q_" + n)
        norm = Norm(k, ctx, "qn_", 1)
        WH = sb("WH", [96, NP + 1, 128])
        parts = sb("parts", [128, 3, NP, S], BF16)
        zeros = sb("zeros", [128, S])
        rest = sb("rest", [128, NP, S])
        Q, K = sb("Q", [RS, 3, QE, S], BF16), sb("K", [RS, 3, HE, S], BF16)
        v_aug, nz = sb("v_aug", [TP, 3, NT, 128]), sb("nz", [128, 3, S])
        top, neg, maxT = sb("top", [TP, NT, QE]), sb("neg", [TP, NT, 96], BF16), sb("maxT", [96, S], BF16)
        E, cT = sb("E", [TP, 4, 512]), sb("cT", [128, EE, S])
        FW = HE * VS + QE
        tok = sb("tok", [TP, NT * EE, FW])
        gsel = sb("gsel", [128, EE, FW])
        rs, gp, gl = sb("rs", [TP, NT * EE, HE]), sb("gp", [TP, NT * EE, QE]), sb("gl", [TP, NT, QE])
        gtop, gex, gsum = sb("gtop", [TP, NT * HE]), sb("gex", [TP, NT * HE, EE]), sb("gsum", [TP, NT * HE])
        wt, wc = sb("wt", [TP, NT, EE, HE]), sb("wc", [TP, NT * EE, D])
        y, sq, mean, var = sb("y", [TP, NT * HE, DH2]), sb("sq", [TP, NT * HE, DH2]), sb("mean", [TP, NT * HE]), sb("var", [TP, NT * HE])
        root = sb("root", [TP, NT * HE])
        fx, fxT = sb("fx", [TP, NT, 128]), sb("fxT", [96, S])
        r1, h1T, fo, foT = sb("r1", [D, S]), sb("h1T", [96, S]), sb("fo", [TP, NT, 128]), sb("foT", [D, S])
        fl, fs = sb("fl", [TP, NT * HE]), sb("fs", [TP, NT])
        hout = sb("hout", [TP, 3, NT * D])
        gamma, beta = sb("gamma", [TP, 2, NT * HE, DH2]), sb("beta", [TP, 2, NT * HE, DH2])
        gb = sb("gb", [TP, NT, QE])

        folded, set_up, p_ready, nz_ready, nz_done, v_kept = map(sem, ("folded", "set_up", "p", "nz", "nz_done", "v_kept"))
        hi_done, rest_ready, parts_done, parts_stored, stacked = map(sem, ("hi", "rest", "parts", "parts_stored", "stacked"))
        m_ready, m_read, neg_ready, neg_turned, maxT_kept = map(sem, ("m", "m_read", "neg", "neg_turned", "maxT"))
        e_ready, e_done, v_done, c_kept = map(sem, ("e", "e_done", "v_done", "c_kept"))
        sel_ready, sel_read, g_ready, gex_done, sq_ready, sq_done, vs_ready, root_done = map(
            sem, ("sel", "sel_read", "g", "gex", "c", "sq", "vs", "root"))
        fx_ready, fx_turned, fxT_kept, h1_ready, r1_done, h1T_ready, h2_ready = map(
            sem, ("fx", "fx_turned", "fxT", "h1", "r1", "h1T", "h2"))
        fo_ready, fo_turned, foT_kept, fl_ready, fs_ready, fex_done, h_ready, stored = map(
            sem, ("fo", "fo_turned", "foT", "fl", "fs", "fex", "h", "stored"))
        own_dve, own_pool = sem("own_dve"), sem("own_pool")
        own_x = [Tally(sem("own" + n)) for n in ("pe", "act", "sp")]
        block = ctx.enter_context(nc.Block())
        steps = {i * NU // 20: i for i in range(20)}

        def step_behind(n):
            return steps.get(n)

        @block.sync
        def _(sp):
            rows_of = qk_dram.rearrange("(a d) p i s -> p d a i s", d=DH2)
            keys_of = qk_dram.rearrange("(h a d) p i s -> a p i d h s", a=2, d=DH2)

            def stack(b, par):
                wait(sp, e_ready, (b - 2) * NU)
                wait(sp, stacked, b * 32 * len(q_parts))
                sp.wait_ge(parts_done, (b + 1) * NP)
                sp.dma_start(qk_dram, parts[:]).then_inc(parts_stored, 16)
                sp.wait_ge(parts_stored, (b + 1) * 16)
                for g, (qp, kp) in enumerate(zip(q_parts, k_parts)):
                    rows = slice(g * DH2, (g + 1) * DH2)
                    sp.dma_start(Q[rows, par].rearrange("d (a i) s -> d a i s", i=2), rows_of[qp, :, :, 0:2]
                                 ).then_inc(stacked, 16)
                    sp.dma_start(K[rows, par], keys_of[0, kp, 2]).then_inc(stacked, 16)

            def step(r, par):
                b = r - 3
                if alive(r, nb):
                    stack(r, par)
                if alive(b, nb):
                    sp.wait_ge(h_ready, (b + 1) * 16)
                    wait(sp, stored, b * 16)
                    sp.dma_start(out[bass.ds(b, 1)].rearrange("o (c p) f -> p (o c) f", p=TP),
                                 hout[:, par, :].rearrange("p (c f) -> p c f", c=NT)).then_inc(stored, 16)

            rounds(sp, step, 3, own_x[2], nb, 3)
            sp.wait_ge(stored, nb * 16)

        @block.tensor
        def _(pe):
            for e in range(NP + 1):
                last = nc.tensor.matmul(bank[0:D + 1, 4, e * 128:(e + 1) * 128], W("w_sxT"),
                                        W("w_heads")[:, e, :], start=True, stop=True)
            last.then_inc(folded, 1)
            pe.wait_ge(set_up, 1)

            def project(b, i):
                x = norm.xT[:, 0, :]
                if i == 0:
                    pe.wait_ge(norm.kept, b + 1)
                elif i <= NP:
                    pe.wait_ge(rest_ready, b * NP + i)
                if i < NP:
                    nc.tensor.matmul(bank[:, 1, 0:S], WH[:, i, :], x, start=True, stop=True).then_inc(p_ready, 1)
                elif i == NP:
                    for it in range(NT):
                        last = nc.tensor.matmul(bank[0:TP, 1, it * 128:(it + 1) * 128], x[:, it * TP:(it + 1) * TP],
                                                WH[:, NP, :], start=True, stop=True)
                    last.then_inc(p_ready, 1)
                else:
                    pe.wait_ge(v_kept, b + 1)
                    nc.tensor.matmul(bank[:, 1, 0:S], W("w_sx_wide"), x, start=True, stop=True).then_inc(nz_ready, 1)

            def mask(out, heads, cols, at, name):
                out = out[:, 0:len(heads) * cols].rearrange("p (i c) -> p i c", c=cols)[:, :, at:at + TP]
                rhs = B(name).rearrange("p (o c) -> p o c", o=1).to_broadcast((TP, len(heads), TP))
                return nc.tensor.matmul(out, B("ident_b")[0:TP, 0:TP], rhs, start=False, stop=True, skip_group_check=True)

            def scores_for_max(b, par, n):
                e, u = divmod(n, UE)
                back, heads, cols = units[u]
                it = NT - 1 - back
                out = bank[0:TP, 6 + n % 2, :]
                wait(pe, m_read, b * NU + n - 1)
                for i, h in enumerate(heads):
                    nc.tensor.matmul(out[:, i * cols:(i + 1) * cols], Q[:, par, h * EE + e, it * TP:(it + 1) * TP],
                                     K[:, par, h, 0:cols], start=i == 0, stop=False, skip_group_check=True)
                mask(out, heads, cols, cols - TP, "m_low_q").then_inc(m_ready, 1)

            def scores_for_exp(b, par, n):
                e, u = divmod(n, UE)
                jt, heads, cols = units[u]
                out = bank[0:TP, 4 + n % 2, :]
                if n == 0:
                    pe.wait_ge(maxT_kept, b + 1)
                wait(pe, e_done, b * NU + n - 1)
                for i, h in enumerate(heads):
                    nc.tensor.matmul(out[:, i * cols:(i + 1) * cols], K[:, par, h, jt * TP:(jt + 1) * TP],
                                     Q[:, par, h * EE + e, jt * TP:S], start=i == 0, stop=False, skip_group_check=True)
                    nc.tensor.matmul(out[:, i * cols:(i + 1) * cols], B("pick_query")[:, h * EE + e, :], maxT[:, jt * TP:S],
                                     start=False, stop=False, skip_group_check=True)
                mask(out, heads, cols, 0, "m_low_k").then_inc(e_ready, 1)

            def weigh_values(b, par, n):
                e, u = divmod(n, UE)
                jt, heads, cols = units[u]
                pe.wait_ge(e_done, b * NU + n + 1)
                if u == 0:
                    wait(pe, c_kept, b * EE + e - 1)
                for i, h in enumerate(heads):
                    last = nc.tensor.matmul(bank[32 * h:32 * h + 32, 2 - 2 * (e % 2), jt * TP:S],
                                            v_aug[:, par, jt, 32 * h:32 * h + 32], E[:, n % 4, i * cols:(i + 1) * cols],
                                            start=jt == 0, stop=jt == NT - 1, skip_group_check=True)
                last.then_inc(v_done, 1)

            def turn_max(b):
                pe.wait_ge(neg_ready, b + 1)
                pe.wait_ge(nz_done, min(b + 2, nb) if isinstance(b, int) else b + 2)
                for it in range(NT):
                    last = nc.tensor.matmul(bank[0:96, 1, it * TP:(it + 1) * TP], neg[:, it, :],
                                            B("ident_b")[0:TP, 0:TP], start=True, stop=True)
                last.then_inc(neg_turned, 1)

            def tail(b, n):
                if n < NT:
                    if n == 0:
                        pe.wait_ge(c_kept, (b + 1) * EE)
                        wait(pe, fs_ready, b)
                    wait(pe, sel_read, b * NT + n)
                    for e in range(EE):
                        last = nc.tensor.matmul(bank[0:TP, 3, e * FW:(e + 1) * FW], cT[:, e, n * TP:(n + 1) * TP],
                                                gsel[:, e, :], start=True, stop=True)
                    last.then_inc(sel_ready, 1)
                if n == 8:
                    pe.wait_ge(fx_ready, b + 1)
                    for it in range(NT):
                        last = nc.tensor.transpose(bank[:, 3, it * TP:(it + 1) * TP], fx[:, it, :], F("ident")[0:TP, 0:TP])
                    last.then_inc(fx_turned, 1)
                if n == 9:
                    pe.wait_ge(fxT_kept, b + 1)
                    nc.tensor.matmul(bank[0:D, 3, 0:S], W("fc1"), fxT[:], start=True, stop=True).then_inc(h1_ready, 1)
                if n == 11:
                    pe.wait_ge(h1T_ready, b + 1)
                    for it in range(NT):
                        last = nc.tensor.matmul(bank[0:TP, 3, it * D:(it + 1) * D], h1T[:, it * TP:(it + 1) * TP],
                                                W("fc2"), start=True, stop=True)
                    last.then_inc(h2_ready, 1)
                if n == 16:
                    pe.wait_ge(fo_ready, b + 1)
                    for it in range(NT):
                        last = nc.tensor.transpose(bank[:, 3, it * TP:(it + 1) * TP], fo[:, it, :], F("ident")[0:TP, 0:TP])
                    last.then_inc(fo_turned, 1)
                if n == 17:
                    pe.wait_ge(foT_kept, b + 1)
                    for it in range(NT):
                        last = nc.tensor.matmul(bank[0:TP, 3, it * HE:(it + 1) * HE], foT[:, it * TP:(it + 1) * TP],
                                                W("fgate"), start=True, stop=True)
                    last.then_inc(fl_ready, 1)

            def step(r, par):
                b1, b2, b3 = r - 1, r - 2, r - 3
                if alive(b1, nb):
                    pe.wait_ge(stacked, (b1 + 1) * 32 * len(q_parts))
                for n in range(NU + LAG):
                    if alive(b1, nb) and n < NU:
                        scores_for_max(b1, (par - 1) % 3, n)
                    if alive(b2, nb):
                        if n == 1:
                            turn_max(b2)
                        if n >= LAG:
                            scores_for_exp(b2, (par - 2) % 3, n - LAG)
                        if n >= LAG + 2:
                            weigh_values(b2, (par - 2) % 3, n - LAG - 2)
                    m = step_behind(n)
                    if alive(b3, nb) and m is not None:
                        tail(b3, m)
                    if alive(r, nb):
                        if m == 2:
                            wait(pe, nz_done, r)
                            wait(pe, maxT_kept, r - 1)
                            norm.turn(pe, r)
                        if m in (4, 6, 8, 10, 12):
                            project(r, m // 2 - 2)
                if alive(b2, nb):
                    weigh_values(b2, (par - 2) % 3, NU - 2)
                    weigh_values(b2, (par - 2) % 3, NU - 1)

            rounds(pe, step, 3, own_x[0], nb, 3)

        @block.scalar
        def _(act):
            def first_part(b, i):
                act.wait_ge(p_ready, b * (NP + 1) + i + 1)
                if i == 0:
                    wait(act, parts_stored, b * 16)
                nc.scalar.copy(parts[:, 0, i, :], bank[:, 1, 0:S]).then_inc(hi_done, 1)

            def keep_values(b, par):
                act.wait_ge(p_ready, (b + 1) * (NP + 1))
                wait(act, v_done, (b - 2) * NU)
                nc.scalar.copy(flat3(v_aug[:, par]), bank[0:TP, 1, 0:NT * 128]).then_inc(v_kept, 1)

            def exponentials(b, n):
                jt, heads, cols = units[n % UE]
                act.wait_ge(e_ready, b * NU + n + 1)
                wait(act, v_done, b * NU + n - 3)
                used = slice(0, len(heads) * cols)
                nc.scalar.activation(E[:, n % 4, used], bank[0:TP, 4 + n % 2, used], ACT.Exp).then_inc(e_done, 1)

            def tail(b, n):
                if n < NT:
                    act.wait_ge(sel_ready, b * NT + n + 1)
                    if n == 0:
                        wait(act, sq_ready, 2 * b)
                    nc.scalar.copy(tok[:, n * EE:(n + 1) * EE, :],
                                   bank[0:TP, 3, 0:EE * FW].rearrange("p (e f) -> p e f", e=EE)).then_inc(sel_read, 1)
                if n == 3:
                    act.wait_ge(g_ready, b + 1)
                    nc.scalar.activation(flat3(gex[:]), flat3(gl[:]), ACT.Exp).then_inc(gex_done, 1)
                if n in (4, 12):
                    act.wait_ge(sq_ready, 2 * b + (n == 12) + 1)
                    nc.scalar.activation(sq[:], y[:], ACT.Square).then_inc(sq_done, 1)
                if n == 8:
                    act.wait_ge(fx_turned, b + 1)
                    wait(act, h1T_ready, b)
                    nc.scalar.copy(fxT[0:D, :], bank[0:D, 3, 0:S]).then_inc(fxT_kept, 1)
                if n == 9:
                    act.wait_ge(h1_ready, b + 1)
                    nc.scalar.activation(r1[:], bank[0:D, 3, 0:S], ACT.Relu).then_inc(r1_done, 1)
                if n == 16:
                    act.wait_ge(fo_turned, b + 1)
                    wait(act, fl_ready, b)
                    nc.scalar.copy(foT[:], bank[0:D, 3, 0:S]).then_inc(foT_kept, 1)
                if n == 18:
                    act.wait_ge(fs_ready, b + 1)
                    nc.scalar.activation(fl[:], fl[:], ACT.Exp).then_inc(fex_done, 1)

            def step(r, par):
                b1, b2, b3 = r - 1, r - 2, r - 3
                for n in range(NU + LAG):
                    if alive(b2, nb):
                        if n == 1:
                            act.wait_ge(neg_turned, b2 + 1)
                            wait(act, e_ready, b2 * NU)
                            nc.scalar.copy(maxT[:], bank[0:96, 1, 0:S]).then_inc(maxT_kept, 1)
                        if n >= LAG:
                            exponentials(b2, n - LAG)
                    m = step_behind(n)
                    if alive(b3, nb) and m is not None:
                        tail(b3, m)
                    if alive(r, nb):
                        if m == 2:
                            norm.keep(act, r, 0, [(nz_ready, r)])
                        if m in (4, 6, 8):
                            first_part(r, m // 2 - 2)
                        if m == 10:
                            keep_values(r, par)

            rounds(act, step, 3, own_x[1], nb, 3)

        @block.vector
        def _(dve):
            own = Tally(own_dve)
            norm.clear(dve, own)
            for v in (neg, fx, fo, zeros):
                own.up(nc.vector.memset(v[:], 0.0))
            own.up(nc.vector.memset(WH[:], 0.0))
            for v in (fxT, h1T):
                own.link(dve, nc.vector.memset(v[:], 0.0))
                own.up(nc.vector.memset(v[D:D + 1], 1.0))
            for i, (g, b_) in enumerate((("ln_g", "ln_b"), ("fnorm_g", "fnorm_b"))):
                for dst, src in ((gamma, g), (beta, b_)):
                    own.up(nc.vector.tensor_copy(dst[:, i], W(src).rearrange("p (o d) -> p o d", o=1)
                                                 .to_broadcast((TP, NT * HE, DH2))))
            own.up(nc.vector.tensor_copy(gb[:], W("gate_b2").rearrange("p (o d) -> p o d", o=1).to_broadcast((TP, NT, QE))))
            own.up(nc.vector.tensor_copy(gsel[:, :, 0:HE * VS], F("sel").rearrange("p (o d) -> p o d", o=1)
                                         .to_broadcast((128, EE, HE * VS))))
            own.up(nc.vector.tensor_copy(gsel[:, :, HE * VS:], W("gate_w2")))
            dve.wait_ge(folded, 1)
            own.up(nc.vector.tensor_scalar(flat3(WH[0:D + 1, 0:2, :]), bank[0:D + 1, 4, 0:256], float(DH2) ** 0.5, None, ALU.mult))
            own.link(dve, nc.vector.tensor_copy(flat3(WH[0:D + 1, 2:, :]), bank[0:D + 1, 4, 256:512]))
            own.link(dve, nc.vector.memset(WH[D:D + 1, NP, :].rearrange("p (n d) -> p n d", n=HE)[:, :, DH2:VS], 1.0))
            nc.vector.memset(norm.carry[:], 0.0).then_inc(set_up, 1)

            def maxima(b, n):
                e, u = divmod(n, UE)
                back, heads, cols = units[u]
                it = NT - 1 - back
                if n == 0:
                    wait(dve, neg_ready, b)
                dve.wait_ge(m_ready, b * NU + n + 1)
                src = bank[0:TP, 6 + n % 2, 0:len(heads) * cols].rearrange("p (i c) -> p i c", c=cols)
                dst = top[:, it, :].rearrange("p (h e) -> p h e", h=HE)[:, heads[0]:heads[-1] + 1, e]
                nc.vector.tensor_reduce(dst, src, AX, ALU.max).then_inc(m_read, 1)

            def negate_max(b):
                dve.wait_ge(m_read, (b + 1) * NU)
                wait(dve, neg_turned, b)
                nc.vector.tensor_scalar(neg[:, :, 0:QE], top[:], -1.0, None, ALU.mult).then_inc(neg_ready, 1)

            def normalise_start(b, i):
                own.link(dve, nc.vector.tensor_reduce(mean[:], y[:], AX, ALU.add))
                nc.vector.scalar_tensor_tensor(y[:], mean[:].rearrange("p (a o) -> p a o", o=1)
                                               .to_broadcast((TP, NT * HE, DH2)), -1.0 / DH2, y[:],
                                               ALU.mult, ALU.add).then_inc(sq_ready, 1)

            def normalise_sum(b, i):
                dve.wait_ge(sq_done, 2 * b + i + 1)
                nc.vector.tensor_reduce(var[:], sq[:], AX, ALU.add).then_inc(vs_ready, 1)

            def normalise_end(b, i, dst, done):
                dve.wait_ge(root_done, 2 * b + i + 1)
                own.link(dve, nc.vector.tensor_tensor(y[:], y[:], root[:].rearrange("p (a o) -> p a o", o=1)
                                                      .to_broadcast((TP, NT * HE, DH2)), ALU.mult))
                own.link(dve, nc.vector.tensor_tensor(y[:], y[:], gamma[:, i], ALU.mult))
                nc.vector.tensor_tensor(dst, by_tile(y[:]), by_tile(beta[:, i]), ALU.add).then_inc(done, 1)

            by_tile = lambda v: v.rearrange("p (t h) d -> p t (h d)", t=NT)

            def tail(b, par, n):
                if n == 3:
                    dve.wait_ge(sel_read, (b + 1) * NT)
                    sums = tok[:, :, 0:HE * VS].rearrange("p a (h d) -> p a h d", h=HE)[:, :, :, DH2]
                    own.link(dve, nc.vector.reciprocal(rs[:], sums))
                    own.link(dve, nc.vector.tensor_tensor(
                        gp[:].rearrange("p a (h e) -> p a h e", h=HE),
                        tok[:, :, HE * VS:].rearrange("p a (h e) -> p a h e", h=HE),
                        rs[:].rearrange("p a (h o) -> p a h o", o=1).to_broadcast((TP, NT * EE, HE, EE)), ALU.mult))
                    own.link(dve, nc.vector.tensor_reduce(gl[:], gp[:].rearrange("p (t e) f -> p t f e", t=NT), AX, ALU.add))
                    own.link(dve, nc.vector.tensor_tensor(gl[:], gl[:], gb[:], ALU.add))
                    heads = gl[:].rearrange("p t (h e) -> p (t h) e", h=HE)
                    own.link(dve, nc.vector.tensor_reduce(gtop[:], heads, AX, ALU.max))
                    nc.vector.tensor_tensor(heads, heads, gtop[:].rearrange("p (a o) -> p a o", o=1)
                                            .to_broadcast((TP, NT * HE, EE)), ALU.subtract).then_inc(g_ready, 1)
                if n == 4:
                    dve.wait_ge(gex_done, b + 1)
                    own.link(dve, nc.vector.tensor_reduce(gsum[:], gex[:], AX, ALU.add))
                    own.link(dve, nc.vector.reciprocal(gsum[:], gsum[:]))
                    own.link(dve, nc.vector.tensor_tensor(gex[:], gex[:], gsum[:].rearrange("p (a o) -> p a o", o=1)
                                                          .to_broadcast((TP, NT * HE, EE)), ALU.mult))
                    own.link(dve, nc.vector.tensor_tensor(wt[:], gex[:].rearrange("p (t h) e -> p t e h", t=NT),
                                                          rs[:].rearrange("p (t e) h -> p t e h", t=NT), ALU.mult))
                    own.link(dve, nc.vector.tensor_tensor(
                        wc[:].rearrange("p a (h d) -> p a h d", h=HE),
                        tok[:, :, 0:HE * VS].rearrange("p a (h d) -> p a h d", h=HE)[:, :, :, 0:DH2],
                        wt[:].rearrange("p t e h -> p (t e) h").rearrange("p a (h o) -> p a h o", o=1)
                        .to_broadcast((TP, NT * EE, HE, DH2)), ALU.mult))
                    own.link(dve, nc.vector.tensor_reduce(by_tile(y[:]), wc[:].rearrange("p (t e) f -> p t f e", t=NT),
                                                          AX, ALU.add))
                    own.link(dve, nc.vector.tensor_tensor(by_tile(y[:]), by_tile(y[:]), res[:], ALU.add))
                    normalise_start(b, 0)
                if n == 5:
                    normalise_sum(b, 0)
                if n == 7:
                    normalise_end(b, 0, fx[:, :, 0:D], fx_ready)
                if n == 10:
                    dve.wait_ge(r1_done, b + 1)
                    wait(dve, h2_ready, b)
                    nc.vector.scalar_tensor_tensor(h1T[0:D, :], fxT[0:D, :], 0.0, r1[:], ALU.not_equal,
                                                   ALU.mult).then_inc(h1T_ready, 1)
                if n == 12:
                    dve.wait_ge(h2_ready, b + 1)
                    h2 = bank[0:TP, 3, 0:NT * D].rearrange("p (t f) -> p t f", t=NT)
                    own.link(dve, nc.vector.scalar_tensor_tensor(by_tile(y[:]), fx[:, :, 0:D], 0.0, h2, ALU.not_equal, ALU.mult))
                    own.link(dve, nc.vector.tensor_tensor(by_tile(y[:]), by_tile(y[:]), fx[:, :, 0:D], ALU.add))
                    normalise_start(b, 1)
                if n == 13:
                    normalise_sum(b, 1)
                if n == 15:
                    normalise_end(b, 1, fo[:, :, 0:D], fo_ready)
                if n == 18:
                    dve.wait_ge(fl_ready, b + 1)
                    lg = bank[0:TP, 3, 0:NT * HE].rearrange("p (t h) -> p t h", t=NT)
                    own.link(dve, nc.vector.tensor_reduce(fs[:], lg, AX, ALU.max))
                    nc.vector.tensor_tensor(fl[:].rearrange("p (t h) -> p t h", t=NT), lg,
                                            fs[:].rearrange("p (t o) -> p t o", o=1).to_broadcast((TP, NT, HE)),
                                            ALU.subtract).then_inc(fs_ready, 1)
                if n == 19:
                    dve.wait_ge(fex_done, b + 1)
                    l3 = fl[:].rearrange("p (t h) -> p t h", t=NT)
                    own.link(dve, nc.vector.tensor_reduce(fs[:], l3, AX, ALU.add))
                    own.link(dve, nc.vector.reciprocal(fs[:], fs[:]))
                    own.link(dve, nc.vector.tensor_tensor(l3, l3, fs[:].rearrange("p (t o) -> p t o", o=1)
                                                          .to_broadcast((TP, NT, HE)), ALU.mult))
                    own.link(dve, nc.vector.tensor_tensor(
                        sq[:].rearrange("p (t h) d -> p t h d", t=NT), y_of(fo), fl[:].rearrange("p (t h o) -> p t h o", t=NT, o=1)
                        .to_broadcast((TP, NT, HE, DH2)), ALU.mult))
                    wait(dve, stored, (b - 1) * 16)
                    nc.vector.tensor_tensor(hout[:, par, :], sq[:].rearrange("p a d -> p (a d)"), one(k.h, b),
                                            ALU.add).then_inc(h_ready, 16)

            def y_of(v):
                return v[:, :, 0:D].rearrange("p t (h d) -> p t h d", h=HE)

            def leave_rest(b, i):
                dve.wait_ge(hi_done, b * NP + i + 1)
                wait(dve, parts_done, (b - 1) * NP + i + 1)
                nc.vector.tensor_tensor(rest[:, i, :], bank[:, 1, 0:S], parts[:, 0, i, :],
                                        ALU.subtract).then_inc(rest_ready, 1)

            def step(r, par):
                b1, b2, b3 = r - 1, r - 2, r - 3
                if alive(r, nb):
                    norm.start(dve, r)
                for n in range(NU + LAG):
                    if alive(b1, nb) and n < NU:
                        maxima(b1, n)
                    if alive(b2, nb) and n % UE == LAG + 2 and n > UE:
                        keep_context(b2, (par - 2) % 3, n // UE - 1)
                    m = step_behind(n)
                    if alive(b3, nb) and m is not None:
                        tail(b3, par, m)
                    if alive(r, nb):
                        if m == 1:
                            norm.apply(dve, r)
                        if m in (5, 7, 9):
                            leave_rest(r, m // 2 - 2)
                        if m == 13:
                            dve.wait_ge(nz_ready, r + 1)
                            nc.vector.tensor_scalar(nz[:, par, :], bank[:, 1, 0:S], 0.0, None,
                                                    ALU.not_equal).then_inc(nz_done, 1)
                if alive(b2, nb):
                    keep_context(b2, (par - 2) % 3, EE - 1)
                if alive(b1, nb):
                    negate_max(b1)

            def keep_context(b, par, e):
                dve.wait_ge(v_done, b * NU + UE * (e + 1))
                wait(dve, sel_ready, b * NT)
                nc.vector.tensor_tensor(cT[:, e, :], bank[:, 2 - 2 * (e % 2), 0:S], nz[:, par, :], ALU.mult).then_inc(c_kept, 1)

            rounds(dve, step, 3, own, nb, 3)

        @block.gpsimd
        def _(pool):
            own = Tally(own_pool)

            def other_parts(b, i):
                pool.wait_ge(rest_ready, b * NP + i + 1)
                own.link(pool, nc.gpsimd.tensor_tensor(parts[:, 1, i, :], rest[:, i, :], zeros[:], ALU.add))
                nc.gpsimd.tensor_tensor(parts[:, 2, i, :], rest[:, i, :], parts[:, 1, i, :],
                                        ALU.subtract).then_inc(parts_done, 1)

            def step(r, par):
                b = r - 3
                if alive(r, nb):
                    norm.take_root(pool, r)
                if alive(b, nb):
                    take_root(b, 0)
                if alive(r, nb):
                    other_parts(r, 0)
                    other_parts(r, 1)
                    other_parts(r, 2)
                if alive(b, nb):
                    take_root(b, 1)

            def take_root(b, i):
                pool.wait_ge(vs_ready, 2 * b + i + 1)
                own.link(pool, nc.gpsimd.tensor_tensor(root[:], var[:], F("per_width"), ALU.mult))
                own.link(pool, nc.gpsimd.tensor_tensor(root[:], root[:], F("eps2"), ALU.add))
                nc.gpsimd.tensor_tensor(root[:], root[:], k.half[:], ALU.pow).then_inc(root_done, 1)

            rounds(pool, step, 3, own, nb, 3)


def flat3(ap):
    return ap.rearrange("p a b -> p (a b)")


def one(h, b):
    return h[:, bass.ds(b, 1), :].rearrange("p o f -> p (o f)")


def tower(nc, nb, x, fpack, bpack, wpack, packs, s_dram, qk_dram, out):
    with ExitStack() as ctx:
        k = Core(nc, ctx, packs, nb)
        with nc.cleanup_on_exit(), ExitStack() as c:
            t = SelectAttend(k, c)
            score_tokens(k, x, fpack, bpack, wpack, s_dram, t)
            select_attend(k, t, x, s_dram)
        with nc.cleanup_on_exit():
            experts(k)
        with nc.cleanup_on_exit():
            slices(k)
        res = k.sb("first_heads", [TP, NT, D])
        with nc.cleanup_on_exit():
            first_heads(k, res)
            query_experts(k, res, qk_dram, out)


def kernel(**inputs):
    import concourse.bacc as bacc
    from concourse.bass_utils import run_bass_kernel_spmd

    weights = {n: np.asarray(v) for n, v in inputs.items() if n != "x"}
    x = np.ascontiguousarray(inputs["x"])
    f, b = shape_constants()
    w = weight_layout(weights)
    arrays = {"x": x, "fconst_in": f.build(np.float32),
              "bconst_in": b.build(mybir.dt.np(BF16)), "weights_in": w.build(np.float32)}
    nc = bacc.Bacc("TRN2", target_bir_lowering=False, num_devices=1)
    args = [nc.dram_tensor(n, a.shape, mybir.dt.from_np(a.dtype), kind="ExternalInput").ap()
            for n, a in arrays.items()]
    nb = x.shape[0]
    out = nc.dram_tensor("out", (nb, S, D), F32, kind="ExternalOutput").ap()
    qk_dram = nc.dram_tensor("query_key_parts", (128, 3, 3, S), BF16).ap()
    s_dram = nc.dram_tensor("scores", (nb * CI, TP), F32).ap()
    tower(nc, nb, *args, (f, b, w), s_dram, qk_dram, out)
    r = run_bass_kernel_spmd(nc, [arrays], core_ids=[0])
    return r.results[0]["out"]
```

```python
from contextlib import ExitStack

import numpy as np

import concourse.bass as bass
from concourse import mybir

F32 = mybir.dt.float32
BF16 = mybir.dt.bfloat16
ALU = mybir.AluOpType
ACT = mybir.ActivationFunctionType
AX = mybir.AxisListType.X

NB = 32
N_IN = 750
S = N_IN // 2
D = 64
TP = 125
CI = N_IN // TP
NT = S // TP
H0, DH = 4, 16
NE, DE = 8, 128
HS, DS, G = 8, 8, 64
PS = HS // 2
DS1 = DS + 1
HE, EE, DH2 = 4, 4, 16
QE = HE * EE
VS = DH2 + 1
EPS = 1e-5
EPS2 = 1e-8
BIG = -1e30
TINY = 2.0 ** -126




class Pack:

    def __init__(self):
        self.parts, self.at, self.width = [], {}, 0

    def add(self, name, array):
        array = np.asarray(array)
        rows, shape = array.shape[0], array.shape[1:]
        cols = int(np.prod(shape))
        self.at[name] = (rows, self.width, shape)
        self.parts.append(array.reshape(rows, cols))
        self.width += cols

    def build(self, dtype):
        out = np.zeros((128, self.width), dtype)
        at = 0
        for part in self.parts:
            out[:part.shape[0], at:at + part.shape[1]] = part
            at += part.shape[1]
        return out

    def view(self, tile, name):
        rows, at, shape = self.at[name]
        v = tile[0:rows, at:at + int(np.prod(shape))]
        if len(shape) == 2:
            v = v.rearrange("p (a b) -> p a b", a=shape[0])
        if len(shape) == 3:
            v = v.rearrange("p (a b c) -> p a b c", a=shape[0], b=shape[1])
        return v


def shape_constants():
    f, b = Pack(), Pack()
    f.add("ident", np.eye(128))
    w = np.exp(np.arange(0, D, 2, dtype=np.float32) * np.float32(-np.log(10000.0) / D)).astype(np.float64)
    wf = np.repeat(w, 2)[:, None]
    is_cos = (np.arange(D) % 2 == 1)[:, None]
    sign = np.where(is_cos, 1.0, -1.0)
    j = np.arange(S)[None, :]
    pe = np.where(is_cos, np.cos(j * wf), np.sin(j * wf))
    f.add("pe", np.concatenate([pe, pe]))
    c = (S - 1 - j)
    f.add("cos_low", np.tile(np.cos(c * wf), (2, 1)))
    f.add("sin_low", np.tile(sign * np.sin(c * wf), (2, 1)))
    c = -(np.arange(1, S)[None, :] + 1)
    f.add("cos_up", np.tile(np.cos(c * wf), (2, 1)))
    f.add("sin_up", np.tile(sign * np.sin(c * wf), (2, 1)))
    for name, value in (("eps", EPS), ("one_eps", 1.0 + EPS), ("eps_eps", EPS * EPS)):
        f.add(name, np.full((TP, 4 * NT), value))
    f.add("iota", np.tile(np.arange(S)[None, :], (TP, 1)))
    last = np.zeros((TP, NT, H0))
    last[TP - 1, NT - 1] = BIG
    f.add("no_next", last)
    p = np.arange(TP)[:, None]
    b.add("ident_b", np.eye(128))
    tie = np.zeros((TP, CI, N_IN))
    for t in range(CI):
        tie[:, t] = np.where(np.arange(N_IN)[None, :] < t * TP + p, 0.0, TINY)
    b.add("tie", tie)
    q = np.arange(TP)[None, :]
    q2 = np.arange(2 * TP)[None, :]
    b.add("m_low_q", np.where(q > p, BIG, 0.0))
    b.add("m_up_q", np.where(q2 < p + 2, BIG, 0.0))
    b.add("m_low_k", np.where(q < p, BIG, 0.0))
    b.add("m_up_k", np.where(q2 - TP > p - 2, BIG, 0.0))
    pick = np.zeros((96, H0, TP))
    for h in range(H0):
        pick[h, h] = 1.0
    b.add("pick_head", pick)
    expert = np.zeros((96, NE, 128))
    for e in range(NE):
        expert[e:3 * NE:NE, e] = 1.0
    b.add("pick_expert", expert)
    b.add("earlier", np.tile(np.tril(np.ones((NE, NE)), -1).reshape(1, NE * NE), (TP, 1)))
    f.add("slice_block", np.kron(np.eye(HS), np.full((DS1, DS1), 1 / np.sqrt(np.float64(DS)))))
    own_pair = np.zeros((HS * DS1, PS, G))
    for h in range(HS):
        own_pair[h * DS1:(h + 1) * DS1, h // 2] = 1.0
    f.add("own_pair", own_pair)
    sel = np.zeros((128, HE * VS))
    for n in range(HE):
        sel[32 * n:32 * n + VS, n * VS:(n + 1) * VS] = np.eye(VS)
    f.add("sel", sel)
    f.add("eps2", np.full((TP, NT * HE), EPS2))
    f.add("per_width", np.full((TP, NT * HE), 1.0 / DH2))
    f.add("two_halves", np.concatenate([np.eye(D), np.eye(D)]))
    f.add("euler", np.full((TP, NT * NE), np.e))
    return f, b


def weight_layout(w):
    k = Pack()
    z = lambda *s: np.zeros(s, np.float32)

    def over(matrix, *rows):
        out = z(96, matrix.shape[1])
        out[:matrix.shape[0]] = matrix
        for n, r in enumerate(rows):
            out[matrix.shape[0] + n] = r
        return out

    g = {n[len("L0_attn_"):]: v for n, v in w.items() if n.startswith("L0_attn_")}
    k.add("score_w", np.broadcast_to(w["L0_tok_score_proj"].reshape(1, D), (TP, D)))
    k.add("gamma", g["ln_gamma"].reshape(D, 1))
    k.add("beta", g["ln_beta"].reshape(D, 1))
    wq = over(g["Wq"], g["bq"], g["u_bias"].reshape(D))
    wk = over(g["Wk"], g["bk"])
    wv = over(g["Wv"], g["bv"])
    cq, ck = z(96, 2, 128), z(96, 2, 128)
    for h in range(H0):
        at = 64 if h % 2 == 0 else 0
        cq[:, h // 2, at:at + DH] = wq[:, h * DH:(h + 1) * DH]
        ck[:, h // 2, at:at + DH] = wk[:, h * DH:(h + 1) * DH]
    k.add("wcq", cq)
    k.add("wck", ck)
    va = z(96, H0, 32)
    va[:, :, :DH] = wv.reshape(96, H0, DH)
    va[D, :, DH] = 1.0
    k.add("wq_tok", wq)
    k.add("wv_aug", va.reshape(96, 128))
    k.add("wkv_next", np.concatenate([wk, wv], 1))
    k.add("wout", over(g["Wout"], g["bout"]))
    qT = z(DH, H0, 66)
    qT[:, :, :D] = g["Wq"].reshape(D, H0, DH).transpose(2, 1, 0)
    qT[:, :, D] = g["bq"].reshape(H0, DH).T
    qT[:, :, D + 1] = g["v_bias"].T
    posT = g["Wpos"].reshape(D, H0, DH).transpose(2, 1, 0)
    k.add("wqT", qT)
    k.add("wposT", np.ascontiguousarray(posT))
    m = {n[len("L0_ffn_"):]: v for n, v in w.items() if n.startswith("L0_ffn_")}
    k.add("gate_w", over(m["gate_w"], m["gate_b"]))
    w1 = z(96, NE, DE)
    w1[:D] = m["W1"].transpose(1, 0, 2)
    w1[D] = m["b1"]
    k.add("w1", w1)
    k.add("w2", m["W2"].transpose(1, 0, 2))
    k.add("b2", np.tile(m["b2"], (3, 1)))
    a = {n[len("L1_attn_"):]: v for n, v in w.items() if n.startswith("L1_attn_")}
    k.add("w_in", over(a["W_in"], a["b_in"]))
    inT = z(DS1, HS, D + 1)
    inT[:DS, :, :D] = a["W_in"].reshape(D, HS, DS).transpose(2, 1, 0)
    inT[:DS, :, D] = a["b_in"].reshape(HS, DS).T
    inT[DS, :, D] = 1.0
    k.add("w_inT", inT)
    k.add("w_slice", np.concatenate([a["W_slice"], a["b_slice"][None, :]]))
    k.add("temperature", np.broadcast_to(a["temperature"].reshape(1, HS), (96, HS)))
    k.add("wq_sT", np.tile(np.concatenate([a["W_q"], a["b_q"][None, :]]).T, (1, HS)))
    k.add("wk_sT", np.tile(np.concatenate([a["W_k"], a["b_k"][None, :]]).T, (1, HS)))
    wv9 = np.concatenate([a["W_v"], a["b_v"][None, :]])
    bdv = z(HS * DS1, PS, DS)
    for h in range(HS):
        bdv[h * DS1:(h + 1) * DS1, h // 2] = wv9
    k.add("wv_s", bdv.reshape(HS * DS1, PS * DS))
    pairs = z(HS // 2, 32, D)
    pairs[:, :2 * DS] = a["W_out"].reshape(HS // 2, 2 * DS, D)
    k.add("w_out_s", pairs.reshape(128, D))
    k.add("b_out_s", over(z(D, D), a["b_out"]))
    l = {n[len("L1_ffn_"):]: v for n, v in w.items() if n.startswith("L1_ffn_")}
    sx = over(l["hl_w"].reshape(D, D).T, l["hl_b"].reshape(D))
    k.add("w_sx", sx)
    wide = z(96, HE, 32)
    wide[:, :, :DH2] = sx.reshape(96, HE, DH2)
    wide[D, :, DH2] = 1.0
    k.add("w_sx_wide", wide.reshape(96, 128))
    k.add("w_sxT", np.concatenate([l["hl_w"].reshape(D, D), l["hl_b"].reshape(D, 1)], 1))
    heads = z(D, 4, HE, 2, DH2)
    for n in range(HE):
        rows = slice(n * DH2, (n + 1) * DH2)
        for e in range(EE):
            heads[rows, e % 2, n, e // 2] = l["wq"][n, e].T
        heads[rows, 2, n, 0] = l["wk"][n].T
        heads[rows, 3, n, 0] = l["wv"][n].T
    k.add("w_heads", heads.reshape(D, 4, 128))
    gw = z(128, EE, HE * EE)
    for n in range(HE):
        for e in range(EE):
            gw[32 * n:32 * n + DH2, e, n * EE:(n + 1) * EE] = l["gate_w"][n, :, e * DH2:(e + 1) * DH2].T
    k.add("gate_w2", gw)
    k.add("gate_b2", np.broadcast_to(l["gate_b"].reshape(1, QE), (TP, QE)))
    for name in ("ln_g", "ln_b", "fnorm_g", "fnorm_b"):
        k.add(name, np.broadcast_to(l[name].reshape(1, DH2), (TP, DH2)))
    for name in ("fc1", "fc2"):
        block = z(D, D)
        for n in range(HE):
            block[n * DH2:(n + 1) * DH2, n * DH2:(n + 1) * DH2] = l[name + "_w"].T
        k.add(name, over(block, np.tile(l[name + "_b"], HE)))
    k.add("fgate", l["fgate_w"].T)
    k.add("wposT_swap", posT.reshape(DH, H0, D // 2, 2)[..., ::-1].reshape(DH, H0, D))
    return k




class Tally:

    def __init__(self, sem):
        self.sem, self.base, self.n = sem, 0, 0

    def up(self, instruction):
        instruction.then_inc(self.sem, 1)
        self.n += 1

    def wait(self, eng):
        eng.wait_ge(self.sem, self.base + self.n)

    def link(self, eng, instruction):
        self.up(instruction)
        self.wait(eng)


def wait(eng, sem, value):
    if not isinstance(value, int) or value > 0:
        eng.wait_ge(sem, value)


def rounds(eng, step, lags, tally, n, period=2):
    peel = lags + period
    peel += (n - peel) % period
    for t in range(peel):
        if t == peel - period:
            before = tally.n
        step(t, t % period)
    per = tally.n - before
    entry = tally.base + tally.n
    count = (n - peel) // period
    if count:
        with eng.Fori(0, count) as g:
            tally.base, tally.n = g * per + entry, 0
            for i in range(period):
                step(g * period + (peel + i), (peel + i) % period)
            assert tally.n == per
    tally.base, tally.n = entry + count * per, 0
    for t in range(n, n + lags):
        step(t, t % period)


def alive(b, n):
    return not isinstance(b, int) or 0 <= b < n


class Core:

    def __init__(self, nc, ctx, packs, nb):
        self.nc, self.nb = nc, nb
        fpack, bpack, wpack = packs
        self.sb = lambda name, shape, dt=F32: ctx.enter_context(nc.sbuf_tensor(name, shape, dt))
        self.sem = lambda name: nc.alloc_semaphore(name=name)
        self.fc = self.sb("fconst", [128, fpack.width])
        self.bc = self.sb("bconst", [128, bpack.width], BF16)
        self.wc = self.sb("weights", [128, wpack.width])
        self.F = lambda name: fpack.view(self.fc, name)
        self.B = lambda name: bpack.view(self.bc, name)
        self.W = lambda name: wpack.view(self.wc, name)
        self.bank = ctx.enter_context(nc.psum_tensor("psum", [128, 8, 512], F32))
        self.h = self.sb("h_all", [TP, nb, NT * D])
        self.half = self.sb("minus_half", [TP, 4 * NT])





def score_tokens(k, x_dram, fpack_dram, bpack_dram, wpack_dram, s_dram, t):
    nc, nb = k.nc, k.nb
    tiles = nb * CI
    chunk = 4 * CI if nb % 4 == 0 else CI
    n_chunks = tiles // chunk
    loaded, multiplied = (k.sem("x_even_loaded"), k.sem("x_odd_loaded")), k.sem("x_multiplied")
    half_set = k.sem("half_set")
    const_loaded, w_loaded = k.sem("const_loaded"), k.sem("weights_loaded")
    dve_own, scored = k.sem("score_dve_own"), k.sem("scored")
    s_turned, s_copied, s_stored = k.sem("scores_turned"), k.sem("scores_copied"), k.sem("scores_stored")
    gate_exp, folded = k.sem("gate_exp"), k.sem("folded")
    W, F = k.W, k.F
    with ExitStack() as ctx:
        xs = ctx.enter_context(nc.sbuf_tensor("x_chunks", [TP, 2, chunk, D], F32))
        prod = ctx.enter_context(nc.sbuf_tensor("prod", [TP, chunk, D], F32))
        s_rows = ctx.enter_context(nc.sbuf_tensor("s_rows", [128, 2, TP], F32))
        block = ctx.enter_context(nc.Block())
        groups = [(a, min(a + 128, tiles)) for a in range(0, tiles, 128)]

        @block.sync
        def _(sp):
            sp.dma_start(k.wc[:], wpack_dram).then_inc(w_loaded, 16)
            for i in range(n_chunks):
                src = x_dram.rearrange("b (c p) f -> p (b c) f", p=TP)[:, i * chunk:(i + 1) * chunk, :]
                wait(sp, multiplied, i - 1)
                sp.dma_start(xs[:, i % 2], src).then_inc(loaded[i % 2], 16)
                if i == 0:
                    sp.dma_start(k.fc[:], fpack_dram).then_inc(const_loaded, 16)
                    sp.dma_start(k.bc[:], bpack_dram).then_inc(const_loaded, 16)
            sp.wait_ge(s_copied, len(groups))
            for n, (a, e) in enumerate(groups):
                sp.dma_start(s_dram[a:e, :], s_rows[0:e - a, n, :]).then_inc(s_stored, 16)
            sp.wait_ge(s_stored, 16 * len(groups))

        @block.vector
        def _(dve):
            own = Tally(dve_own)
            nc.vector.memset(k.half[:], -0.5).then_inc(half_set, 1)
            own.link(dve, nc.vector.memset(t.xT[:], 0.0))
            own.up(nc.vector.memset(t.xT[D:D + 2], 1.0))
            own.up(nc.vector.memset(t.xn[:, :, D:], 0.0))
            own.up(nc.vector.memset(t.ctx[:, :, D:], 0.0))
            own.up(nc.vector.memset(t.RW[:], 0.0))
            own.up(nc.vector.memset(t.maxT[:], 0.0))
            own.up(nc.vector.memset(t.neg_max[:], 0.0))
            own.up(nc.vector.memset(t.Q[:], 0.0))
            own.link(dve, nc.vector.memset(t.K[:], 0.0))
            own.up(nc.vector.memset(t.ctxT[:], 0.0))
            own.wait(dve)
            own.up(nc.vector.memset(t.ctxT[D:D + 1], 1.0))
            dve.wait_ge(w_loaded, 16)
            w = W("score_w").rearrange("p (o f) -> p o f", o=1).to_broadcast((TP, chunk, D))
            for i in range(n_chunks):
                dve.wait_ge(loaded[i % 2], 16 * (i // 2 + 1))
                nc.vector.tensor_tensor(prod[:], xs[:, i % 2], w, ALU.mult).then_inc(multiplied, 1)
                dve.wait_ge(multiplied, i + 1)
                width = D
                while width > 2:
                    width //= 2
                    own.link(dve, nc.vector.tensor_tensor(prod[:, :, 0:width], prod[:, :, 0:width],
                                                          prod[:, :, width:2 * width], ALU.add))
                own.link(dve, nc.vector.tensor_tensor(t.score[:, i * chunk:(i + 1) * chunk],
                                                      prod[:, :, 0], prod[:, :, 1], ALU.add))
            own.up(nc.vector.memset(prod[:, 0, 0:1], 0.0))
            nc.vector.tensor_scalar(t.score[:], t.score[:], 1.0, None, ALU.mult).then_inc(scored, 1)
            for n, (a, e) in enumerate(groups):
                dve.wait_ge(s_turned, n + 1)
                nc.vector.tensor_copy(s_rows[0:e - a, n, :], k.bank[0:e - a, n, 0:TP]).then_inc(s_copied, 1)
            dve.wait_ge(gate_exp, 1)
            own.link(dve, nc.vector.tensor_scalar(t.gate[:], t.gate[:], 1.0, None, ALU.add))
            own.link(dve, nc.vector.reciprocal(t.gate[:], t.gate[:]))
            dve.wait_ge(const_loaded, 32)
            for par in range(2):
                for h in range(H0):
                    at = 0 if h % 2 == 0 else D
                    own.up(nc.vector.tensor_copy(t.K[at:at + D, par, h, :], F("pe")[at:at + D, :]))
            dve.wait_ge(folded, 1)
            for n in range(2):
                own.up(nc.vector.tensor_copy(t.RW[0:D + 2, n, :], k.bank[0:D + 2, 2 + n, 0:H0 * D]))

        @block.scalar
        def _(act):
            act.wait_ge(scored, 1)
            nc.scalar.activation(t.gate[:], t.score[:], ACT.Exp, scale=-1.0).then_inc(gate_exp, 1)

        @block.tensor
        def _(pe):
            pe.wait_ge(w_loaded, 16)
            for n, name in enumerate(("wposT", "wposT_swap")):
                for h in range(H0):
                    last = nc.tensor.matmul(k.bank[0:D + 2, 2 + n, h * D:(h + 1) * D], W("wqT")[:, h, :],
                                            W(name)[:, h, :], start=True, stop=True)
            last.then_inc(folded, 1)
            pe.wait_ge(const_loaded, 32)
            pe.wait_ge(scored, 1)
            for n, (a, e) in enumerate(groups):
                nc.tensor.transpose(k.bank[0:e - a, n, 0:TP], t.score[:, a:e],
                                    F("ident")[0:TP, 0:TP]).then_inc(s_turned, 1)




class SelectAttend:

    def __init__(self, k, ctx):
        nb = k.nb
        sb = lambda name, shape, dt=F32: ctx.enter_context(k.nc.sbuf_tensor(name, shape, dt))
        self.x = sb("x_tokens", [TP, 2, CI, D])
        self.score = sb("score", [TP, nb * CI])
        self.gate = sb("gate", [TP, nb * CI])
        self.s_row = sb("s_row", [TP, 2, N_IN])
        self.s_loc = sb("s_loc", [TP, CI])
        self.xg = sb("x_gated", [TP, CI, D])
        self.counted = sb("counted", [TP, N_IN], BF16)
        self.rank = sb("rank", [TP, CI])
        self.hot = sb("one_hot", [TP, CI, S])
        self.h_new = sb("h_new", [TP, NT * D])
        self.stats = sb("stats", [TP, NT, 6])
        self.mv = sb("mean_var", [TP, NT, 2])
        self.rstd = sb("rstd", [TP, NT])
        self.xn = sb("xn", [TP, NT, 128])
        self.xT = sb("xT", [96, 2, S + 1])
        self.RW = sb("RW", [96, 2, H0 * D])
        self.rot = sb("rot", [128, 4, S])
        self.Q = sb("Q", [128, 2 * H0, 2, S])
        self.K = sb("K", [128, 2, H0, S])
        self.q_tok = sb("q_tok", [TP, NT, D])
        self.v_aug = sb("v_aug", [TP, 2, NT, 128])
        self.v_next = sb("v_next", [TP, 2, NT, D])
        self.qk = sb("qk_next", [TP, NT, D])
        self.s_next = sb("s_next", [TP, NT, H0])
        self.mx = sb("mx", [TP, NT, H0])
        self.neg_max = sb("neg_max", [TP, NT, 96], BF16)
        self.maxT = sb("maxT", [96, 2, S], BF16)
        self.e_next = sb("e_next", [TP, 2, NT * H0])
        self.E = sb("E", [TP, 4, 4 * TP])
        self.cT = sb("cT", [128, S])
        self.e_v = sb("e_v", [TP, NT * H0, DH])
        self.den = sb("den", [TP, NT, H0])
        self.ctx = sb("ctx", [TP, NT, 128])
        self.ctxT = sb("ctxT", [96, S])

    def Qb(self, par):
        return self.Q[:, par * H0:(par + 1) * H0]


def select_attend(k, t, x_dram, s_dram):
    nc, nb, F, B, W, bank = k.nc, k.nb, k.F, k.B, k.W, k.bank
    sem = lambda n: k.sem("a_" + n)
    row_loaded, x_loaded, ranked, hot_ready, gathered, h_copied = map(sem, ("row_loaded", "x_loaded", "ranked", "hot", "gathered", "h_copied"))
    var_ready, rstd_ready, xn_ready, x_turned, xT_ready = map(sem, ("var", "rstd", "xn", "x_turned", "xT"))
    pv_ready, pa_ready = sem("proj_for_dve"), sem("proj_for_act")
    pv_free, pa_free = sem("proj_by_dve"), sem("proj_by_act")
    Q_rows = sem("Q_rows")
    m_ready, m_free, e_ready, e_done, pv_done = map(sem, ("m_ready", "m_free", "e_ready", "e_done", "pv_done"))
    neg_ready, neg_turned, maxT_ready, snext_ready, enext_ready = map(sem, ("neg", "neg_turned", "maxT", "snext", "enext"))
    cT_ready, ctx_turned, ctx_ready, ctxT_turned, ctxT_ready, out_ready, out_added = map(
        sem, ("cT", "c_turned", "ctx", "ctx_turned", "ctxT", "out", "out_added"))
    own_dve, own_act, own_pool, own_pe, own_sp = map(sem, ("own_dve", "own_act", "own_pool", "own_pe", "own_sp"))

    def q_unit(it):
        return ((0, 0, 0, TP * (it + 1)), (1, TP * it, TP * (it + 1), TP * (NT - it)))

    def k_unit(jt):
        return ((0, TP * jt, 0, TP * (NT - jt)), (1, 0, TP * (NT - jt), TP * (jt + 1)))

    def rows(h):
        return 96 if h % 2 == 0 else 128

    units = [(tile, h) for tile in range(NT) for h in range(H0)]
    NU = len(units)

    with nc.Block() as block:

        @block.sync
        def _(sp):
            def step(b, par):
                if alive(b, nb):
                    wait(sp, ranked, (b - 1) * CI)
                    wait(sp, x_loaded, b * 16)
                    wait(sp, row_loaded, b * 16)
                    sp.dma_start(t.s_row[:, par, :], s_row_of(b)).then_inc(row_loaded, 16)
                    sp.dma_start(t.x[:, par], x_dram[bass.ds(b, 1)].rearrange("o (c p) f -> p (o c) f", p=TP)
                                 ).then_inc(x_loaded, 16)

            def s_row_of(b):
                flat = s_dram.rearrange("(b c) p -> b (c p)", c=CI)
                return flat[bass.ds(b, 1), :].to_broadcast((TP, N_IN))

            rounds(sp, step, 3, Tally(own_sp), nb)

        @block.tensor
        def _(pe):
            def project(b, par, third):
                xT = t.xT[:, par, :]
                if third == 0:
                    pe.wait_ge(xT_ready, b + 1)
                n = [b * 6 + 2 * third, b * 5 + 2 * third]

                def fill(which, parts):
                    wait(pe, (pv_free, pa_free)[which], n[which] - (which == 0))
                    for out, lhsT, rhs in parts:
                        last = nc.tensor.matmul(out, lhsT, rhs, start=True, stop=True)
                    last.then_inc((pv_ready, pa_ready)[which], 1)
                    n[which] = n[which] + 1

                x = xT[:, 0:S]
                full = lambda bk: bank[:, bk, 0:S]
                tile = lambda it: xT[:, it * TP:(it + 1) * TP]
                after = lambda it: xT[:, it * TP + 1:(it + 1) * TP + 1]
                if third < 2:
                    cols = slice(third * 128, (third + 1) * 128)
                    fill(0, [(full(1), t.RW[:, 0, cols], x)])
                    fill(1, [(full(2), W("wck")[:, third, :], x)])
                    fill(0, [(full(0), t.RW[:, 1, cols], x)])
                    fill(1, [(full(2), W("wcq")[:, third, :], x)])
                    return
                fill(0, [(bank[0:TP, 1, it * D:(it + 1) * D], tile(it), W("wq_tok")) for it in range(NT)])
                wait(pe, maxT_ready, b)
                fill(1, [(bank[0:TP, 2, it * 128:(it + 1) * 128], tile(it), W("wv_aug")) for it in range(NT)])
                fill(0, [(bank[0:TP, 0, it * 128:(it + 1) * 128], after(it), W("wkv_next")) for it in range(NT)])

            def scores_for_exp(b, par, n):
                jt, h = units[n]
                if n == 0:
                    pe.wait_ge(maxT_ready, b + 1)
                wait(pe, e_done, b * NU + n - 1)
                out = bank[0:TP, 4 + n % 2, :]
                key = t.K[0:rows(h), par, h, jt * TP:(jt + 1) * TP]
                for part, q0, c0, cols in k_unit(jt):
                    nc.tensor.matmul(out[:, c0:c0 + cols], key, t.Qb(par)[0:rows(h), h, part, q0:q0 + cols],
                                     start=part == 0, stop=False, skip_group_check=True)
                    nc.tensor.matmul(out[:, c0:c0 + cols], B("pick_head")[:, h, :], t.maxT[:, par, q0:q0 + cols],
                                     start=False, stop=False, skip_group_check=True)
                nc.tensor.matmul(out[:, 0:TP], B("ident_b")[0:TP, 0:TP], B("m_low_k"),
                                 start=False, stop=False, skip_group_check=True)
                w = TP if jt == 0 else 2 * TP
                nc.tensor.matmul(out[:, 4 * TP - w:4 * TP], B("ident_b")[0:TP, 0:TP], B("m_up_k")[:, 2 * TP - w:],
                                 start=False, stop=True, skip_group_check=True).then_inc(e_ready, 1)

            def scores_for_max(b, par, n):
                it, h = units[n]
                if n == 0:
                    pe.wait_ge(Q_rows, (b + 1) * 2)
                    pe.wait_ge(pa_free, b * 5 + 5)
                wait(pe, m_free, b * NU + n - 1)
                out = bank[0:TP, 6 + n % 2, :]
                for part, j0, c0, cols in q_unit(it):
                    nc.tensor.matmul(out[:, c0:c0 + cols], t.Qb(par)[0:rows(h), h, part, it * TP:(it + 1) * TP],
                                     t.K[0:rows(h), par, h, j0:j0 + cols],
                                     start=part == 0, stop=False, skip_group_check=True)
                nc.tensor.matmul(out[:, it * TP:(it + 1) * TP], B("ident_b")[0:TP, 0:TP], B("m_low_q"),
                                 start=False, stop=False, skip_group_check=True)
                w = TP if it == NT - 1 else 2 * TP
                c0 = TP * (it + 1)
                nc.tensor.matmul(out[:, c0:c0 + w], B("ident_b")[0:TP, 0:TP], B("m_up_q")[:, 0:w],
                                 start=False, stop=True, skip_group_check=True).then_inc(m_ready, 1)

            def weigh_values(b, par, n):
                jt, h = units[n]
                pe.wait_ge(e_done, b * NU + n + 1)
                if n == 0:
                    wait(pe, out_added, b)
                for part, q0, c0, cols in k_unit(jt):
                    last = nc.tensor.matmul(bank[32 * h:32 * h + 32, 3, q0:q0 + cols],
                                            t.v_aug[:, par, jt, 32 * h:32 * h + 32], t.E[:, n % 4, c0:c0 + cols],
                                            start=(jt == 0 and part == 0), stop=(jt == NT - 1 and part == 1),
                                            skip_group_check=True)
                last.then_inc(pv_done, 1)

            def turn_context(b):
                pe.wait_ge(cT_ready, b + 1)
                for it in range(NT):
                    last = nc.tensor.transpose(bank[0:TP, 3, it * 128:(it + 1) * 128],
                                               t.cT[:, it * TP:(it + 1) * TP], F("ident"))
                last.then_inc(ctx_turned, 1)

            def turn_divided(b):
                pe.wait_ge(ctx_ready, b + 1)
                for it in range(NT):
                    last = nc.tensor.transpose(bank[:, 3, it * TP:(it + 1) * TP], t.ctx[:, it, :],
                                               F("ident")[0:TP, 0:TP])
                last.then_inc(ctxT_turned, 1)

            def project_out(b):
                pe.wait_ge(ctxT_ready, b + 1)
                for it in range(NT):
                    last = nc.tensor.matmul(bank[0:TP, 3, it * D:(it + 1) * D], t.ctxT[:, it * TP:(it + 1) * TP],
                                            W("wout"), start=True, stop=True)
                last.then_inc(out_ready, 1)

            def turn_max(b):
                pe.wait_ge(neg_ready, b + 1)
                pe.wait_ge(pa_free, min(5 * b + 9, 5 * nb) if isinstance(b, int) else b * 5 + 9)
                for it in range(NT):
                    last = nc.tensor.matmul(bank[0:96, 2, it * TP:(it + 1) * TP], t.neg_max[:, it, :],
                                            B("ident_b")[0:TP, 0:TP], start=True, stop=True)
                last.then_inc(neg_turned, 1)

            def gather(b):
                pe.wait_ge(hot_ready, b + 1)
                wait(pe, xT_ready, b)
                wait(pe, pv_free, b * 6)
                for it in range(NT):
                    for c in range(CI):
                        last = nc.tensor.matmul(bank[0:TP, 0, it * D:(it + 1) * D],
                                                t.hot[:, c, it * TP:(it + 1) * TP], t.xg[:, c, :],
                                                start=c == 0, stop=c == CI - 1)
                last.then_inc(gathered, 1)

            def turn_tokens(b):
                pe.wait_ge(xn_ready, b + 1)
                for it in range(NT):
                    last = nc.tensor.transpose(bank[:, 0, it * TP:(it + 1) * TP], t.xn[:, it, :],
                                               F("ident")[0:TP, 0:TP])
                last.then_inc(x_turned, 1)

            def step(r, par):
                b1, b2, b3 = r - 1, r - 2, r - 3
                for third in range(3):
                    if alive(b1, nb):
                        project(b1, 1 - par, third)
                    if alive(b3, nb):
                        (turn_context, turn_divided, project_out)[third](b3)
                    if third == 1 and alive(b2, nb):
                        turn_max(b2)
                for n in range(NU):
                    if alive(b2, nb):
                        scores_for_exp(b2, par, n)
                    if alive(b1, nb):
                        scores_for_max(b1, 1 - par, n)
                    if alive(b2, nb) and n >= 2:
                        weigh_values(b2, par, n - 2)
                    if alive(r, nb) and n == 8:
                        gather(r)
                if alive(b2, nb):
                    weigh_values(b2, par, NU - 2)
                    weigh_values(b2, par, NU - 1)
                if alive(r, nb):
                    turn_tokens(r)

            rounds(pe, step, 3, Tally(own_pe), nb)

        @block.vector
        def _(dve):
            own = Tally(own_dve)

            def projections(b, par, third):
                n = b * 6
                if third < 2:
                    wait(dve, Q_rows, b * 2 + third)
                    for i, (low, up) in enumerate((("cos_low", "cos_up"), ("sin_low", "sin_up"))):
                        dve.wait_ge(pv_ready, n + 2 * third + i + 1)
                        nc.vector.tensor_tensor(t.rot[:, i, :], bank[:, 1 - i, 0:S], F(low), ALU.mult)
                        nc.vector.tensor_tensor(t.rot[:, 2 + i, 0:S - 1], bank[:, 1 - i, 1:S], F(up),
                                                ALU.mult).then_inc(pv_free, 1)
                    return
                dve.wait_ge(pv_ready, n + 5)
                nc.vector.tensor_copy(flat3(t.q_tok[:]), bank[0:TP, 1, 0:NT * D]).then_inc(pv_free, 1)
                dve.wait_ge(pv_free, n + 5)
                dve.wait_ge(pv_ready, n + 6)
                kv = bank[0:TP, 0, 0:NT * 128].rearrange("p (a b) -> p a b", a=NT)
                nc.vector.tensor_tensor(t.qk[:], t.q_tok[:], kv[:, :, 0:D], ALU.mult)
                wait(dve, ctx_ready, b - 1)
                nc.vector.tensor_copy(t.v_next[:, par], kv[:, :, D:2 * D]).then_inc(pv_free, 1)
                dve.wait_ge(pv_free, n + 6)
                wait(dve, enext_ready, b)
                own.link(dve, nc.vector.tensor_reduce(flat3(t.s_next[:]), t.qk[:].rearrange("p a (h d) -> p (a h) d", h=H0),
                                                      AX, ALU.add))
                own.up(nc.vector.tensor_tensor(t.s_next[:], t.s_next[:], F("no_next"), ALU.add))

            def maxima(b, n):
                it, h = units[n]
                if n == 0:
                    wait(dve, neg_ready, b)
                dve.wait_ge(m_ready, b * NU + n + 1)
                nc.vector.tensor_reduce(t.mx[:, it, h:h + 1], bank[0:TP, 6 + n % 2, 0:4 * TP], AX,
                                        ALU.max).then_inc(m_free, 1)

            def negate_max(b):
                dve.wait_ge(m_free, (b + 1) * NU)
                own.link(dve, nc.vector.tensor_tensor(t.mx[:], t.mx[:], t.s_next[:], ALU.max))
                wait(dve, neg_turned, b)
                nc.vector.tensor_scalar(t.neg_max[:, :, 0:H0], t.mx[:], -1.0, None, ALU.mult).then_inc(neg_ready, 1)
                dve.wait_ge(neg_ready, b + 1)
                nc.vector.tensor_tensor(t.s_next[:], t.s_next[:], t.neg_max[:, :, 0:H0], ALU.add).then_inc(snext_ready, 1)

            def take(b, par):
                own.up(nc.vector.tensor_scalar(t.s_loc[:], t.score[:, bass.ds(b * CI, CI)], 1.0, None, ALU.mult))
                wait(dve, gathered, b)
                dve.wait_ge(x_loaded, (b + 1) * 16)
                own.up(nc.vector.tensor_tensor(t.xg[:], t.x[:, par],
                                               t.gate[:, bass.ds(b * CI, CI)].rearrange("p (c o) -> p c o", o=1)
                                               .to_broadcast((TP, CI, D)), ALU.mult))
                own.wait(dve)
                dve.wait_ge(row_loaded, (b + 1) * 16)

            def count(b, par, c):
                wait(dve, ranked, b * CI + c)
                nc.vector.scalar_tensor_tensor(t.counted[:], t.s_row[:, par, :], t.s_loc[:, c:c + 1], B("tie")[:, c, :],
                                               ALU.subtract, ALU.is_ge,
                                               accum_out=t.rank[:, c:c + 1]).then_inc(ranked, 1)

            def one_hot(b):
                wait(dve, gathered, b)
                dve.wait_ge(ranked, (b + 1) * CI)
                for c in range(CI):
                    last = nc.vector.tensor_scalar(t.hot[:, c, :], F("iota"), t.rank[:, c:c + 1], None, ALU.is_equal)
                last.then_inc(hot_ready, 1)

            def divide(b, par):
                dve.wait_ge(enext_ready, b + 1)
                e = t.e_next[:, par, :]
                wide = lambda v: v.rearrange("p (a o) -> p a o", o=1).to_broadcast((TP, NT * H0, DH))
                own.up(nc.vector.tensor_tensor(t.e_v[:], t.v_next[:, par].rearrange("p a (h d) -> p (a h) d", h=H0),
                                               wide(e), ALU.mult))
                own.wait(dve)
                dve.wait_ge(ctx_turned, b + 1)
                c = bank[0:TP, 3, 0:NT * 128].rearrange("p (a d) -> p a d", d=32)
                den = flat3(t.den[:])
                own.link(dve, nc.vector.tensor_tensor(den, c[:, :, DH], e, ALU.add))
                own.up(nc.vector.reciprocal(den, den))
                wait(dve, ctxT_turned, b)
                own.link(dve, nc.vector.tensor_tensor(t.e_v[:], c[:, :, 0:DH], t.e_v[:], ALU.add))
                for it in range(NT):
                    heads = slice(it * H0, (it + 1) * H0)
                    last = nc.vector.tensor_tensor(t.ctx[:, it, 0:D].rearrange("p (h d) -> p h d", h=H0), t.e_v[:, heads, :],
                                                   den[:, heads].rearrange("p (h o) -> p h o", o=1)
                                                   .to_broadcast((TP, H0, DH)), ALU.mult)
                last.then_inc(ctx_ready, 1)

            def add_out(b):
                dve.wait_ge(out_ready, b + 1)
                h = one(k.h, b)
                nc.vector.tensor_tensor(h, h, bank[0:TP, 3, 0:NT * D], ALU.add).then_inc(out_added, 1)

            def receive(b):
                dve.wait_ge(gathered, b + 1)
                wait(dve, xn_ready, b)
                nc.vector.tensor_copy(t.h_new[:], bank[0:TP, 0, 0:NT * D]).then_inc(h_copied, 1)
                dve.wait_ge(h_copied, b + 1)
                for it in range(NT):
                    own.up(nc.vector.bn_stats(t.stats[:, it, :], t.h_new[:, it * D:(it + 1) * D]))
                own.wait(dve)
                own.up(nc.vector.tensor_scalar(one(k.h, b), t.h_new[:], 1.0, None, ALU.mult))
                for it in range(NT):
                    last = nc.vector.bn_aggr(t.mv[:, it, :], t.stats[:, it, :])
                last.then_inc(var_ready, 1)

            def normalise(b):
                dve.wait_ge(var_ready, b + 1)
                dve.wait_ge(rstd_ready, b + 1)
                wait(dve, x_turned, b)
                for it in range(NT):
                    last = nc.vector.tensor_scalar(t.xn[:, it, 0:D], t.h_new[:, it * D:(it + 1) * D],
                                                   t.mv[:, it, 0:1], t.rstd[:, it:it + 1], ALU.subtract, ALU.mult)
                last.then_inc(xn_ready, 1)

            def step(r, par):
                b1, b2, b3 = r - 1, r - 2, r - 3
                for third in range(3):
                    if alive(b1, nb):
                        projections(b1, 1 - par, third)
                    if third == 0 and alive(b3, nb):
                        divide(b3, 1 - par)
                if alive(b3, nb):
                    add_out(b3)
                if alive(r, nb):
                    take(r, par)
                for n in range(NU):
                    if alive(b1, nb):
                        maxima(b1, n)
                    if alive(r, nb):
                        if n < CI:
                            count(r, par, n)
                        if n == CI:
                            one_hot(r)
                        if n == 8:
                            receive(r)
                        if n == 10:
                            normalise(r)
                if alive(b1, nb):
                    negate_max(b1)

            rounds(dve, step, 3, own, nb)

        @block.scalar
        def _(act):
            def projections(b, par, third):
                n = b * 5
                if third == 0:
                    wait(act, e_ready, (b - 1) * NU)
                if third < 2:
                    for i in range(2):
                        act.wait_ge(pa_ready, n + 2 * third + i + 1)
                        for h in (2 * third, 2 * third + 1):
                            at = D if h % 2 == 0 else 0
                            src = bank[at:at + 32, 2, 0:S]
                            if i == 0:
                                last = nc.scalar.copy(t.K[at:at + 32, par, h, :], src)
                            else:
                                last = nc.scalar.copy(t.Qb(par)[at:at + 32, h, :, :],
                                                      src.rearrange("p (o q) -> p o q", o=1).to_broadcast((32, 2, S)))
                        last.then_inc(pa_free, 1)
                    return
                act.wait_ge(pa_ready, n + 5)
                wait(act, pv_done, (b - 1) * NU)
                nc.scalar.copy(flat3(t.v_aug[:, par]), bank[0:TP, 2, 0:NT * 128]).then_inc(pa_free, 1)

            def exponentials(b, n):
                act.wait_ge(e_ready, b * NU + n + 1)
                wait(act, pv_done, b * NU + n - 3)
                nc.scalar.activation(t.E[:, n % 4], bank[0:TP, 4 + n % 2, 0:4 * TP], ACT.Exp,
                                     scale=float(D) ** -0.5).then_inc(e_done, 1)

            def keep_context(b):
                act.wait_ge(pv_done, (b + 1) * NU)
                wait(act, ctx_turned, b)
                nc.scalar.copy(t.cT[:], bank[:, 3, 0:S]).then_inc(cT_ready, 1)

            def keep_divided(b):
                act.wait_ge(ctxT_turned, b + 1)
                wait(act, out_ready, b)
                nc.scalar.copy(t.ctxT[0:D, :], bank[0:D, 3, 0:S]).then_inc(ctxT_ready, 1)

            def keep_max(b, par):
                act.wait_ge(neg_turned, b + 1)
                wait(act, e_ready, (b - 1) * NU)
                nc.scalar.copy(t.maxT[:, par, :], bank[0:96, 2, 0:S]).then_inc(maxT_ready, 1)

            def weigh_next(b, par):
                act.wait_ge(snext_ready, b + 1)
                wait(act, out_added, b - 1)
                nc.scalar.activation(t.e_next[:, par, :], flat3(t.s_next[:]), ACT.Exp,
                                     scale=float(D) ** -0.5).then_inc(enext_ready, 1)

            def receive(b, par):
                act.wait_ge(x_turned, b + 1)
                wait(act, pv_ready, (b - 1) * 6)
                nc.scalar.activation(t.xT[0:D, par, 0:S], bank[0:D, 0, 0:S], ACT.Identity, bias=W("beta"),
                                     scale=W("gamma")).then_inc(xT_ready, 1)

            def step(r, par):
                b1, b2, b3 = r - 1, r - 2, r - 3
                if alive(b3, nb):
                    keep_context(b3)
                for third in range(3):
                    if alive(b1, nb):
                        projections(b1, 1 - par, third)
                    if third == 0 and alive(b2, nb):
                        weigh_next(b2, par)
                    if third == 1:
                        if alive(b3, nb):
                            keep_divided(b3)
                        if alive(b2, nb):
                            keep_max(b2, par)
                if alive(b2, nb):
                    for n in range(NU):
                        exponentials(b2, n)
                if alive(r, nb):
                    receive(r, par)

            rounds(act, step, 3, Tally(own_act), nb)

        @block.gpsimd
        def _(pool):
            own = Tally(own_pool)

            def rotations(b, par):
                wait(pool, e_ready, (b - 1) * NU)
                for p in range(2):
                    pool.wait_ge(pv_free, b * 6 + 2 * p + 2)
                    for h in (2 * p, 2 * p + 1):
                        at = 0 if h % 2 == 0 else D
                        for part, cols in ((0, S), (1, S - 1)):
                            a = t.rot[at:at + D, 2 * part, 0:cols]
                            c = t.rot[at:at + D, 2 * part + 1, 0:cols]
                            last = nc.gpsimd.tensor_tensor(t.Qb(par)[at:at + D, h, part, 0:cols], a, c, ALU.add)
                    last.then_inc(Q_rows, 1)

            def normalise(b):
                pool.wait_ge(var_ready, b + 1)
                own.link(pool, nc.gpsimd.tensor_tensor(t.rstd[:], t.mv[:, :, 1], F("one_eps")[:, 0:NT], ALU.mult))
                own.link(pool, nc.gpsimd.tensor_tensor(t.rstd[:], t.rstd[:], F("eps_eps")[:, 0:NT], ALU.add))
                nc.gpsimd.tensor_tensor(t.rstd[:], t.rstd[:], k.half[:, 0:NT], ALU.pow).then_inc(rstd_ready, 1)

            def step(r, par):
                if alive(r - 1, nb):
                    rotations(r - 1, 1 - par)
                if alive(r, nb):
                    normalise(r)

            rounds(pool, step, 3, own, nb)




class Norm:

    def __init__(self, k, ctx, phase, bank=0, slots=2):
        nc = k.nc
        self.bank = k.bank[:, bank]
        sb = lambda name, shape, dt=F32: ctx.enter_context(nc.sbuf_tensor(phase + name, shape, dt))
        sem = lambda n: k.sem(phase + n)
        self.k = k
        self.carry = sb("carry", [TP, 1])
        self.h, self.stats, self.mv = sb("h_loc", [TP, NT * D]), sb("stats", [TP, NT, 6]), sb("mean_var", [TP, NT, 2])
        self.rstd, self.xn, self.xT = sb("rstd", [TP, NT]), sb("xn", [TP, NT, 128]), sb("xT", [96, slots, S])
        self.copied, self.summed, self.var, self.root = sem("copied"), sem("summed"), sem("var"), sem("root")
        self.root_own, self.applied, self.turned, self.kept = sem("root_own"), sem("applied"), sem("turned"), sem("kept")

    def clear(self, dve, own):
        nc = self.k.nc
        own.link(dve, nc.vector.memset(self.xT[:], 0.0))
        own.up(nc.vector.memset(self.xT[D:D + 1], 1.0))
        own.up(nc.vector.memset(self.xn[:, :, D:], 0.0))

    def start(self, dve, b):
        nc = self.k.nc
        wait(dve, self.applied, b)
        nc.vector.tensor_scalar(self.h[:], one(self.k.h, b), 1.0, None, ALU.mult).then_inc(self.copied, 1)
        dve.wait_ge(self.copied, b + 1)
        for it in range(NT):
            last = nc.vector.bn_stats(self.stats[:, it, :], self.h[:, it * D:(it + 1) * D])
        last.then_inc(self.summed, 1)
        dve.wait_ge(self.summed, b + 1)
        nc.vector.memset(self.carry[:], 0.0)
        for it in range(NT):
            last = nc.vector.bn_aggr(self.mv[:, it, :], self.stats[:, it, :])
        last.then_inc(self.var, 1)

    def take_root(self, pool, b):
        nc = self.k.nc
        pool.wait_ge(self.var, b + 1)
        nc.gpsimd.tensor_tensor(self.rstd[:], self.mv[:, :, 1], self.k.F("eps")[:, 0:NT], ALU.add).then_inc(self.root_own, 1)
        pool.wait_ge(self.root_own, b + 1)
        nc.gpsimd.tensor_tensor(self.rstd[:], self.rstd[:], self.k.half[:, 0:NT], ALU.pow).then_inc(self.root, 1)

    def apply(self, dve, b):
        nc = self.k.nc
        dve.wait_ge(self.var, b + 1)
        dve.wait_ge(self.root, b + 1)
        wait(dve, self.turned, b)
        for it in range(NT):
            last = nc.vector.tensor_scalar(self.xn[:, it, 0:D], self.h[:, it * D:(it + 1) * D], self.mv[:, it, 0:1],
                                           self.rstd[:, it:it + 1], ALU.subtract, ALU.mult)
        last.then_inc(self.applied, 1)

    def turn(self, pe, b):
        nc, k = self.k.nc, self.k
        pe.wait_ge(self.applied, b + 1)
        for it in range(NT):
            last = nc.tensor.transpose(self.bank[:, it * TP:(it + 1) * TP], self.xn[:, it, :],
                                       k.F("ident")[0:TP, 0:TP])
        last.then_inc(self.turned, 1)

    def keep(self, act, b, par, users):
        nc, k = self.k.nc, self.k
        act.wait_ge(self.turned, b + 1)
        for s, value in users:
            wait(act, s, value)
        nc.scalar.copy(self.xT[0:D, par, :], self.bank[0:D, 0:S]).then_inc(self.kept, 1)




def experts(k):
    nc, nb, F, B, W, bank = k.nc, k.nb, k.F, k.B, k.W, k.bank
    with ExitStack() as ctx:
        sb = lambda name, shape, dt=F32: ctx.enter_context(nc.sbuf_tensor("x_" + name, shape, dt))
        sem = lambda n: k.sem("x_" + n)
        norm = Norm(k, ctx, "xn_", slots=3)
        top, shifted, prob = sb("top", [TP, NT]), sb("shifted", [TP, NT * NE]), sb("prob", [TP, NT * NE])
        total = sb("total", [TP, NT])
        ahead, same = sb("ahead", [TP, NT, NE, NE], BF16), sb("same", [TP, NT, NE, NE], BF16)
        rank, cw, rest = sb("rank", [TP, NT * NE]), sb("cw", [TP, NT, NE]), sb("rest", [TP, NT, NE])
        parts = sb("parts", [TP, NT, 3 * NE], BF16)
        partsT, partsTf = sb("partsT", [96, 3, S], BF16), sb("partsTf", [3 * NE, 3, S])
        hid, hidw = sb("hidden", [DE, 3, S]), sb("hidden_w", [DE, 3, S])
        yT = sb("yT", [128, S])
        logits, shift_ready, exp_ready, cw_ready, cw_turned, cw_kept = map(
            sem, ("logits", "shift", "exp", "cw", "cw_turned", "cw_kept"))
        hid_ready, gelu_done, spread, weighed, down = map(sem, ("hid", "gelu", "spread", "weighed", "down"))
        y_kept, out_ready, added, own_dve = map(sem, ("y_kept", "out", "added", "own_dve"))
        own_x = [Tally(sem("own" + n)) for n in ("pe", "act", "pool")]
        cleared = sem("cleared")
        block = ctx.enter_context(nc.Block())

        @block.tensor
        def _(pe):
            pe.wait_ge(cleared, 1)

            def up(b, par, e):
                n = b * NE + e
                if e == 0:
                    pe.wait_ge(cw_kept, b + 1)
                wait(pe, gelu_done, n - 1)
                nc.tensor.matmul(bank[:, 2 + e % 2, 0:S], W("w1")[:, e, :], norm.xT[:, par, :], start=True,
                                 stop=True).then_inc(hid_ready, 1)
                wait(pe, weighed, n - 1)
                nc.tensor.matmul(bank[:, 4 + e % 2, 0:S], B("pick_expert")[:, e, :], partsT[:, par, :], start=True,
                                 stop=True).then_inc(spread, 1)

            def go_down(b, e):
                n = b * NE + e
                pe.wait_ge(weighed, n + 1)
                if e == 0:
                    wait(pe, y_kept, b)
                at = D * (e % 2)
                nc.tensor.matmul(bank[at:at + D, 6, 0:S], W("w2")[:, e, :], hidw[:, e % 2, :], start=e < 2,
                                 stop=e >= NE - 2, skip_group_check=True).then_inc(down, 1)

            def gate(b, par):
                pe.wait_ge(norm.kept, b + 1)
                wait(pe, shift_ready, b)
                for it in range(NT):
                    last = nc.tensor.matmul(bank[0:TP, 1, it * NE:(it + 1) * NE], norm.xT[:, par, it * TP:(it + 1) * TP],
                                            W("gate_w"), start=True, stop=True)
                last.then_inc(logits, 1)

            def turn_weights(b):
                pe.wait_ge(cw_ready, b + 1)
                for it in range(NT):
                    last = nc.tensor.matmul(bank[0:3 * NE, 0, it * TP:(it + 1) * TP], parts[:, it, :],
                                            B("ident_b")[0:TP, 0:TP], start=True, stop=True)
                last.then_inc(cw_turned, 1)

            def finish(b, par):
                pe.wait_ge(y_kept, b + 1)
                wait(pe, added, b)
                for it in range(NT):
                    cols = slice(it * TP, (it + 1) * TP)
                    nc.tensor.matmul(bank[0:TP, 7, it * D:(it + 1) * D], yT[:, cols], F("two_halves"), start=True,
                                     stop=False, skip_group_check=True)
                    last = nc.tensor.matmul(bank[0:TP, 7, it * D:(it + 1) * D], partsTf[:, par, cols], W("b2"),
                                            start=False, stop=True, skip_group_check=True)
                last.then_inc(out_ready, 1)

            def step(r, par):
                b1, b2, b3 = r - 1, r - 2, r - 3
                for e in range(NE):
                    if alive(b2, nb):
                        up(b2, (par - 2) % 3, e)
                        if e >= 1:
                            go_down(b2, e - 1)
                    if alive(b3, nb) and e == 1:
                        finish(b3, par)
                    if alive(r, nb):
                        if e == 2:
                            wait(pe, cw_kept, r - 1)
                            norm.turn(pe, r)
                        if e == 4:
                            gate(r, par)
                    if alive(b1, nb) and e == 7:
                        pe.wait_ge(norm.kept, min(r + 1, nb) if isinstance(r, int) else r + 1)
                        turn_weights(b1)
                if alive(b2, nb):
                    go_down(b2, NE - 1)

            rounds(pe, step, 3, own_x[0], nb, 3)

        @block.scalar
        def _(act):
            def gelu(b, e):
                n = b * NE + e
                act.wait_ge(hid_ready, n + 1)
                wait(act, weighed, n - 1)
                nc.scalar.activation(hid[:, e % 2, :], bank[:, 2 + e % 2, 0:S], ACT.Gelu).then_inc(gelu_done, 1)

            def keep_weights(b, par):
                act.wait_ge(cw_turned, b + 1)
                wait(act, spread, (b - 2) * NE)
                nc.scalar.copy(partsT[0:3 * NE, par, :], bank[0:3 * NE, 0, 0:S])
                wait(act, out_ready, b - 2)
                nc.scalar.copy(partsTf[:, par, :], bank[0:3 * NE, 0, 0:S]).then_inc(cw_kept, 1)

            def step(r, par):
                b1, b2 = r - 1, r - 2
                for e in range(NE):
                    if alive(b2, nb):
                        gelu(b2, e)
                    if alive(r, nb) and e == 2:
                        norm.keep(act, r, par, [(hid_ready, (r - 2) * NE), (logits, r - 2)])
                if alive(b1, nb):
                    keep_weights(b1, (par - 1) % 3)
                if alive(b2, nb):
                    act.wait_ge(down, b2 * NE + NE)
                    wait(act, out_ready, b2)
                    nc.scalar.copy(yT[:], bank[:, 6, 0:S]).then_inc(y_kept, 1)

            rounds(act, step, 2, own_x[1], nb, 3)

        @block.vector
        def _(dve):
            own = Tally(own_dve)
            norm.clear(dve, own)
            nc.vector.memset(partsT[:], 0.0).then_inc(cleared, 1)

            def weigh(b, e):
                n = b * NE + e
                dve.wait_ge(spread, n + 1)
                dve.wait_ge(gelu_done, n + 1)
                wait(dve, down, n - 1)
                nc.vector.tensor_tensor(hidw[:, e % 2, :], bank[:, 4 + e % 2, 0:S], hid[:, e % 2, :],
                                        ALU.mult).then_inc(weighed, 1)

            v3 = lambda a: a.rearrange("p (t e) -> p t e", t=NT)
            over_e = lambda a: a.rearrange("p (t o) -> p t o", o=1).to_broadcast((TP, NT, NE))

            def shift(b):
                dve.wait_ge(logits, b + 1)
                wait(dve, exp_ready, b)
                lg = bank[0:TP, 1, 0:NT * NE]
                own.link(dve, nc.vector.tensor_reduce(top[:], v3(lg), AX, ALU.max))
                nc.vector.tensor_tensor(v3(shifted[:]), v3(lg), over_e(top[:]), ALU.subtract).then_inc(shift_ready, 1)

            CHOOSE = 3

            def choose(b, third):
                if third == 0:
                    dve.wait_ge(exp_ready, b + 1)
                    own.link(dve, nc.vector.tensor_reduce(total[:], v3(prob[:]), AX, ALU.add))
                    own.link(dve, nc.vector.reciprocal(total[:], total[:]))
                    own.link(dve, nc.vector.tensor_tensor(v3(prob[:]), v3(prob[:]), over_e(total[:]), ALU.mult))
                    other = prob[:].rearrange("p (t o e) -> p t o e", t=NT, o=1).to_broadcast((TP, NT, NE, NE))
                    mine = prob[:].rearrange("p (t e o) -> p t e o", t=NT, o=1).to_broadcast((TP, NT, NE, NE))
                    own.up(nc.vector.tensor_tensor(same[:], other, mine, ALU.is_equal))
                    own.up(nc.vector.tensor_tensor(ahead[:], other, mine, ALU.is_gt))
                if third == 1:
                    own.wait(dve)
                    early = B("earlier").rearrange("p (o e) -> p o e", o=1).to_broadcast((TP, NT, NE * NE))
                    sf = same[:].rearrange("p t a b -> p t (a b)")
                    own.link(dve, nc.vector.tensor_tensor(sf, sf, early, ALU.mult))
                    own.link(dve, nc.vector.tensor_tensor(ahead[:], ahead[:], same[:], ALU.add))
                    own.up(nc.vector.tensor_reduce(rank[:], ahead[:].rearrange("p t a b -> p (t a) b"), AX, ALU.add))
                if third == 2:
                    own.wait(dve)
                    own.link(dve, nc.vector.scalar_tensor_tensor(cw[:].rearrange("p t e -> p (t e)"), rank[:], 2.0, prob[:],
                                                                 ALU.is_lt, ALU.mult))
                    wait(dve, cw_turned, b)
                    own.link(dve, nc.vector.tensor_copy(parts[:, :, 0:NE], cw[:]))
                    own.link(dve, nc.vector.tensor_tensor(rest[:], cw[:], parts[:, :, 0:NE], ALU.subtract))
                    own.link(dve, nc.vector.tensor_copy(parts[:, :, NE:2 * NE], rest[:]))
                    nc.vector.tensor_tensor(parts[:, :, 2 * NE:], rest[:], parts[:, :, NE:2 * NE],
                                            ALU.subtract).then_inc(cw_ready, 1)

            def step(r, par):
                b1, b2, b3 = r - 1, r - 2, r - 3
                if alive(r, nb):
                    norm.start(dve, r)
                for e in range(NE):
                    if alive(b2, nb):
                        weigh(b2, e)
                    if alive(r, nb) and e == 0:
                        norm.apply(dve, r)
                    if alive(b1, nb) and 2 <= e < 2 + CHOOSE:
                        choose(b1, e - 2)
                    if alive(r, nb) and e == 5:
                        shift(r)
                    if alive(b3, nb) and e == 3:
                        add(b3)

            def add(b):
                dve.wait_ge(out_ready, b + 1)
                h = one(k.h, b)
                nc.vector.tensor_tensor(h, h, bank[0:TP, 7, 0:NT * D], ALU.add).then_inc(added, 1)

            rounds(dve, step, 3, own, nb, 3)

        @block.gpsimd
        def _(pool):
            def step(r, par):
                if alive(r, nb):
                    norm.take_root(pool, r)
                    pool.wait_ge(shift_ready, r + 1)
                    wait(pool, cw_ready, r)
                    nc.gpsimd.tensor_tensor(prob[:], F("euler"), shifted[:], ALU.pow).then_inc(exp_ready, 1)

            rounds(pool, step, 2, own_x[2], nb)




def slices(k):
    nc, nb, F, W, bank = k.nc, k.nb, k.F, k.W, k.bank
    R = HS * DS1
    with ExitStack() as ctx:
        sb = lambda name, shape, dt=F32: ctx.enter_context(nc.sbuf_tensor("s_" + name, shape, dt))
        sem = lambda n: k.sem("s_" + n)
        norm = Norm(k, ctx, "sn_")
        WL, MB, rtemp = sb("WL", [96, HS * G]), sb("MB", [R, R]), sb("rtemp", [96, HS])
        top, shifted = sb("top", [TP, NT * HS]), sb("shifted", [TP, NT, HS * G])
        E, ET = sb("E", [TP, NT, HS * G]), sb("ET", [128, 2, PS, S])
        rsum, sumv, tin = sb("rsum", [TP, NT * HS]), sb("sum", [TP, NT * HS]), sb("tin", [TP, NT * HS, DS1])
        rnorm, tok, tokT, bothT = sb("rnorm", [128, PS]), sb("tok", [128, 128]), sb("tokT", [R, 128]), sb("bothT", [R, G])
        keys, kq, vals = sb("keys", [R, PS, G]), sb("kq", [R, 128]), sb("vals", [128, PS * DS])
        topA, shA, EA, EAT = sb("topA", [128, PS]), sb("shA", [128, PS, G]), sb("EA", [128, PS, 128]), sb("EAT", [128, PS * 128])
        sumA, OB = sb("sumA", [128, PS]), sb("OB", [128, PS, 32])
        rwide, rT, attT = sb("rwide", [TP, NT, 128]), sb("rT", [128, 2, S]), sb("attT", [128, S])
        set_up, folded, folded_kept = sem("set_up"), sem("folded"), sem("folded_kept")
        t_ready, l_ready, sh_ready = map(sem, ("t", "logits", "shifted"))
        e_done, g_ready, eT_done, tin_ready, sl_ready = map(sem, ("e", "e_turned", "eT", "tin", "slices"))
        tok_ready, tok_turned, tokT_ready, keys_ready, kqv_ready, kq_kept, s_ready = map(
            sem, ("tok", "tok_turned", "tokT", "keys", "kqv", "kq_kept", "scores"))
        shA_ready, eA_done, eA_turned, eAT_kept, o_ready, OB_ready, out_ready = map(
            sem, ("shA", "eA", "eA_turned", "eAT", "o", "OB", "out"))
        rwide_ready, r_turned, rT_kept, att_ready, res_ready, added, own_dve = map(
            sem, ("rwide", "r_turned", "rT", "att", "res", "added", "own_dve"))
        own_x = [Tally(sem("own" + n)) for n in ("pe", "act", "pool")]
        block = ctx.enter_context(nc.Block())
        tile = lambda v, par, it: v[:, par, it * TP:(it + 1) * TP]

        @block.tensor
        def _(pe):
            for h in range(HS):
                nc.tensor.matmul(bank[0:D + 1, 6, h * G:(h + 1) * G], W("w_inT")[:, h, :], W("w_slice"),
                                 start=True, stop=True)
            nc.tensor.matmul(bank[0:R, 7, 0:R], W("wq_sT"), W("wk_sT"), start=True, stop=True).then_inc(folded, 1)
            pe.wait_ge(set_up, 1)
            pe.wait_ge(folded_kept, 1)

            def logits(b, par):
                pe.wait_ge(norm.kept, b + 1)
                wait(pe, tok_ready, b)
                for it in range(NT):
                    last = nc.tensor.matmul(bank[0:TP, 1, it * D:(it + 1) * D], tile(norm.xT, par, it), W("w_in"),
                                            start=True, stop=True)
                last.then_inc(t_ready, 1)
                wait(pe, sh_ready, b * NT)
                for it in range(NT):
                    nc.tensor.matmul(bank[0:TP, 2 + it, :], tile(norm.xT, par, it), WL[:], start=True,
                                     stop=True).then_inc(l_ready, 1)

            def turn_weights(b, p):
                pe.wait_ge(e_done, b + 1)
                wait(pe, eT_done, b * PS + p - 1)
                for it in range(NT):
                    last = nc.tensor.transpose(bank[:, 6 + p % 2, it * TP:(it + 1) * TP], E[:, it, p * 128:(p + 1) * 128],
                                               F("ident")[0:TP, 0:TP])
                last.then_inc(g_ready, 1)

            def gather_slices(b):
                pe.wait_ge(tin_ready, b + 1)
                flat = tin[:].rearrange("p (t h) d -> p t (h d)", t=NT)
                for p in range(PS):
                    for it in range(NT):
                        last = nc.tensor.matmul(bank[:, 1, p * 2 * DS1:(p + 1) * 2 * DS1],
                                                E[:, it, p * 128:(p + 1) * 128],
                                                flat[:, it, p * 2 * DS1:(p + 1) * 2 * DS1],
                                                start=it == 0, stop=it == NT - 1)
                last.then_inc(sl_ready, 1)

            def turn_tokens(b):
                pe.wait_ge(tok_ready, b + 1)
                wait(pe, OB_ready, b)
                nc.tensor.transpose(bank[:, 5, 0:128], tok[:], F("ident")).then_inc(tok_turned, 1)

            def project(b):
                pe.wait_ge(tokT_ready, b + 1)
                nc.tensor.matmul(bank[0:R, 5, 0:128], MB[:], tokT[:], start=True, stop=True)
                nc.tensor.matmul(bank[:, 5, 128:128 + PS * DS], tokT[:], W("wv_s"), start=True,
                                 stop=True).then_inc(kqv_ready, 1)

            def scores(b):
                pe.wait_ge(kq_kept, b + 1)
                pe.wait_ge(keys_ready, b + 1)
                nc.tensor.matmul(bank[:, 5, 0:PS * G], kq[:], keys[:].rearrange("p a g -> p (a g)"), start=True,
                                 stop=True).then_inc(s_ready, 1)

            def turn_attention(b):
                pe.wait_ge(eA_done, b + 1)
                for p in range(PS):
                    last = nc.tensor.transpose(bank[:, 5, p * 128:(p + 1) * 128], EA[:, p, :], F("ident"))
                last.then_inc(eA_turned, 1)

            def attend(b):
                pe.wait_ge(eAT_kept, b + 1)
                for p in range(PS):
                    last = nc.tensor.matmul(bank[:, 5, p * DS:(p + 1) * DS], EAT[:, p * 128:(p + 1) * 128],
                                            vals[:, p * DS:(p + 1) * DS], start=True, stop=True)
                last.then_inc(o_ready, 1)

            def spread(b, par):
                pe.wait_ge(OB_ready, b + 1)
                for p in range(PS):
                    last = nc.tensor.matmul(bank[32 * p:32 * p + 32, 0, 0:S], OB[:, p, :], ET[:, par, p, :], start=True,
                                            stop=True, skip_group_check=True)
                last.then_inc(out_ready, 1)

            def turn_sums(b):
                pe.wait_ge(rwide_ready, b + 1)
                wait(pe, added, b - 1)
                for it in range(NT):
                    last = nc.tensor.transpose(bank[:, 0, it * TP:(it + 1) * TP], rwide[:, it, :], F("ident")[0:TP, 0:TP])
                last.then_inc(r_turned, 1)

            def project_out(b):
                pe.wait_ge(att_ready, b + 1)
                for it in range(NT):
                    out = bank[0:TP, 0, it * D:(it + 1) * D]
                    nc.tensor.matmul(out, attT[:, it * TP:(it + 1) * TP], W("w_out_s"), start=True, stop=False,
                                     skip_group_check=True)
                    last = nc.tensor.matmul(out, norm.xT[D:D + 1, 0, it * TP:(it + 1) * TP], W("b_out_s")[D:D + 1, :],
                                            start=False, stop=True, skip_group_check=True)
                last.then_inc(res_ready, 1)

            def step(r, par):
                b1, b2, b3 = r - 1, r - 2, r - 3
                one_, two, three = alive(b1, nb), alive(b2, nb), alive(b3, nb)
                if three:
                    pe.wait_ge(norm.kept, min(r, nb) if isinstance(r, int) else r)
                    pe.wait_ge(rT_kept, min(r - 1, nb) if isinstance(r, int) else r - 1)
                    spread(b3, 1 - par)
                if two:
                    turn_tokens(b2)
                if one_:
                    logits(b1, 1 - par)
                if two:
                    project(b2)
                if three:
                    project_out(b3)
                if two:
                    scores(b2)
                if one_:
                    turn_weights(b1, 0)
                    turn_weights(b1, 1)
                if two:
                    turn_attention(b2)
                if one_:
                    turn_weights(b1, 2)
                    turn_weights(b1, 3)
                if two:
                    attend(b2)
                if one_:
                    turn_sums(b1)
                    gather_slices(b1)
                if alive(r, nb):
                    wait(pe, rT_kept, r)
                    norm.turn(pe, r)

            rounds(pe, step, 3, own_x[0], nb)

        @block.scalar
        def _(act):
            def exps(b):
                act.wait_ge(sh_ready, (b + 1) * NT)
                wait(act, sl_ready, b)
                nc.scalar.activation(E[:], shifted[:], ACT.Exp).then_inc(e_done, 1)

            def keep_weights(b, par, p):
                act.wait_ge(g_ready, b * PS + p + 1)
                wait(act, out_ready, b - 1)
                nc.scalar.copy(ET[:, par, p, :], bank[:, 6 + p % 2, 0:S]).then_inc(eT_done, 1)

            def keep_projected(b):
                act.wait_ge(kqv_ready, b + 1)
                wait(act, o_ready, b)
                nc.scalar.copy(kq[:], bank[0:R, 5, 0:128])
                nc.scalar.copy(vals[:], bank[:, 5, 128:128 + PS * DS]).then_inc(kq_kept, 1)

            def attention_exps(b):
                act.wait_ge(shA_ready, b + 1)
                wait(act, OB_ready, b)
                for hh in range(2):
                    rows = slice(hh * G, (hh + 1) * G)
                    last = nc.scalar.activation(EA[rows, :, rows], shA[rows], ACT.Exp)
                last.then_inc(eA_done, 1)

            def step(r, par):
                b1, b2, b3 = r - 1, r - 2, r - 3
                one_, two, three = alive(b1, nb), alive(b2, nb), alive(b3, nb)
                if two:
                    keep_projected(b2)
                if two:
                    attention_exps(b2)
                if one_:
                    exps(b1)
                    keep_weights(b1, 1 - par, 0)
                    keep_weights(b1, 1 - par, 1)
                if two:
                    act.wait_ge(eA_turned, b2 + 1)
                    wait(act, o_ready, b2)
                    nc.scalar.copy(EAT[:], bank[:, 5, :]).then_inc(eAT_kept, 1)
                if one_:
                    keep_weights(b1, 1 - par, 2)
                    keep_weights(b1, 1 - par, 3)
                    act.wait_ge(r_turned, b1 + 1)
                    wait(act, att_ready, b1 - 1)
                    nc.scalar.copy(rT[:, 1 - par, :], bank[:, 0, 0:S]).then_inc(rT_kept, 1)
                if alive(r, nb):
                    norm.keep(act, r, par, [(l_ready, (r - 1) * NT)])

            rounds(act, step, 3, own_x[1], nb)

        @block.vector
        def _(dve):
            own = Tally(own_dve)
            norm.clear(dve, own)
            own.up(nc.vector.memset(WL[:], 0.0))
            own.up(nc.vector.memset(rwide[:], 0.0))
            own.up(nc.vector.memset(EA[:], 0.0))
            own.up(nc.vector.memset(OB[:], 0.0))
            own.up(nc.vector.memset(tok[:], 0.0))
            own.wait(dve)
            owned = tok[:, 0:R].rearrange("p (a e) -> p a e", a=PS)
            for hh in range(2):
                at = hh * DS1 + DS
                own.up(nc.vector.memset(owned[hh * G:(hh + 1) * G, :, at:at + 1], 1.0))
            own.link(dve, nc.vector.reciprocal(rtemp[:], W("temperature")))
            dve.wait_ge(folded, 1)
            own.up(nc.vector.tensor_tensor(WL[0:D + 1].rearrange("p (h g) -> p h g", h=HS),
                                           bank[0:D + 1, 6, :].rearrange("p (h g) -> p h g", h=HS),
                                           rtemp[0:D + 1].rearrange("p (h o) -> p h o", o=1)
                                           .to_broadcast((D + 1, HS, G)), ALU.mult))
            nc.vector.tensor_tensor(MB[:], bank[0:R, 7, 0:R], F("slice_block"), ALU.mult).then_inc(folded_kept, 1)
            nc.vector.memset(norm.carry[:], 0.0).then_inc(set_up, 1)

            def less_max(b, it):
                by_head = lambda v: v.rearrange("p (h g) -> p h g", h=HS)
                own_top = top[:, it * HS:(it + 1) * HS]
                dve.wait_ge(l_ready, b * NT + it + 1)
                own.link(dve, nc.vector.tensor_reduce(own_top, by_head(bank[0:TP, 2 + it, :]), AX, ALU.max))
                wait(dve, e_done, b)
                nc.vector.tensor_tensor(by_head(shifted[:, it, :]), by_head(bank[0:TP, 2 + it, :]),
                                        own_top.rearrange("p (h o) -> p h o", o=1).to_broadcast((TP, HS, G)),
                                        ALU.subtract).then_inc(sh_ready, 1)

            def divide(b):
                dve.wait_ge(e_done, b + 1)
                own.link(dve, nc.vector.tensor_reduce(sumv[:], E[:].rearrange("p t (h g) -> p (t h) g", h=HS), AX, ALU.add))
                wait(dve, rwide_ready, b)
                own.link(dve, nc.vector.reciprocal(rsum[:], sumv[:]))
                r = rsum[:].rearrange("p (a o) -> p a o", o=1)
                dve.wait_ge(t_ready, b + 1)
                wait(dve, sl_ready, b)
                nc.vector.tensor_tensor(tin[:, :, 0:DS], bank[0:TP, 1, 0:NT * D].rearrange("p (a d) -> p a d", d=DS),
                                        r.to_broadcast((TP, NT * HS, DS)), ALU.mult)
                nc.vector.tensor_copy(tin[:, :, DS:DS1], r).then_inc(tin_ready, 1)
                wait(dve, r_turned, b)
                for it in range(NT):
                    last = nc.vector.tensor_copy(
                        rwide[:, it, :].rearrange("p (q c) -> p q c", q=PS)[:, :, 0:2 * DS].rearrange("p q (h d) -> p q h d", h=2),
                        rsum[:, it * HS:(it + 1) * HS].rearrange("p (q h o) -> p q h o", q=PS, o=1)
                        .to_broadcast((TP, PS, 2, DS)))
                last.then_inc(rwide_ready, 1)

            def slice_tokens(b):
                dve.wait_ge(sl_ready, b + 1)
                wait(dve, tok_turned, b)
                sl = bank[:, 1, 0:R].rearrange("p (a e) -> p a e", a=PS)
                for hh in range(2):
                    rows = slice(hh * G, (hh + 1) * G)
                    last = nc.vector.tensor_scalar(rnorm[rows, :], sl[rows, :, hh * DS1 + DS], 1e-5, None, ALU.add)
                own.link(dve, last)
                own.link(dve, nc.vector.reciprocal(rnorm[:], rnorm[:]))
                for hh in range(2):
                    rows, cols = slice(hh * G, (hh + 1) * G), slice(hh * DS1, hh * DS1 + DS)
                    last = nc.vector.tensor_tensor(owned[rows, :, cols], sl[rows, :, cols],
                                                   rnorm[rows, :].rearrange("p (a o) -> p a o", o=1)
                                                   .to_broadcast((G, PS, DS)), ALU.mult)
                last.then_inc(tok_ready, 1)

            def turned_tokens(b):
                dve.wait_ge(tok_turned, b + 1)
                wait(dve, kqv_ready, b)
                nc.vector.tensor_copy(tokT[:], bank[0:R, 5, 0:128])
                wait(dve, s_ready, b)
                own.link(dve, nc.vector.tensor_copy(bothT[:], bank[0:R, 5, 0:G]))
                own.up(nc.vector.tensor_tensor(bothT[:], bothT[:], bank[0:R, 5, G:128], ALU.add))
                own.wait(dve)
                nc.vector.memset(norm.carry[:], 0.0).then_inc(tokT_ready, 1)
                nc.vector.tensor_tensor(keys[:], F("own_pair"), bothT[:].rearrange("p (o g) -> p o g", o=1)
                                        .to_broadcast((R, PS, G)), ALU.mult).then_inc(keys_ready, 1)

            def shift(b):
                dve.wait_ge(s_ready, b + 1)
                sc = bank[:, 5, 0:PS * G].rearrange("p (a g) -> p a g", a=PS)
                own.link(dve, nc.vector.tensor_reduce(topA[:], sc, AX, ALU.max))
                wait(dve, eA_done, b)
                nc.vector.tensor_tensor(shA[:], sc, topA[:].rearrange("p (a o) -> p a o", o=1)
                                        .to_broadcast((128, PS, G)), ALU.subtract).then_inc(shA_ready, 1)

            def attended(b):
                dve.wait_ge(eA_done, b + 1)
                own.link(dve, nc.vector.tensor_reduce(sumA[:], EA[:], AX, ALU.add))
                own.link(dve, nc.vector.reciprocal(sumA[:], sumA[:]))
                dve.wait_ge(o_ready, b + 1)
                wait(dve, out_ready, b)
                o = bank[:, 5, 0:PS * DS].rearrange("p (a d) -> p a d", a=PS)
                for hh in range(2):
                    rows = slice(hh * G, (hh + 1) * G)
                    last = nc.vector.tensor_tensor(OB[rows, :, hh * DS:(hh + 1) * DS], o[rows],
                                                   sumA[rows, :].rearrange("p (a o) -> p a o", o=1)
                                                   .to_broadcast((G, PS, DS)), ALU.mult)
                last.then_inc(OB_ready, 1)

            def out(b, par):
                dve.wait_ge(out_ready, b + 1)
                dve.wait_ge(rT_kept, b + 1)
                wait(dve, res_ready, b)
                nc.vector.tensor_tensor(attT[:], bank[:, 0, 0:S], rT[:, par, :], ALU.mult).then_inc(att_ready, 1)

            def add(b):
                dve.wait_ge(res_ready, b + 1)
                h = one(k.h, b)
                nc.vector.tensor_tensor(h, h, bank[0:TP, 0, 0:NT * D], ALU.add).then_inc(added, 1)

            def step(r, par):
                b1, b2, b3 = r - 1, r - 2, r - 3
                one_, two, three = alive(b1, nb), alive(b2, nb), alive(b3, nb)
                if two:
                    slice_tokens(b2)
                if three:
                    out(b3, 1 - par)
                if two:
                    turned_tokens(b2)
                if one_:
                    less_max(b1, 0)
                    less_max(b1, 1)
                if two:
                    shift(b2)
                if one_:
                    less_max(b1, 2)
                if three:
                    add(b3)
                if alive(r, nb):
                    norm.start(dve, r)
                if one_:
                    divide(b1)
                if alive(r, nb):
                    norm.apply(dve, r)
                if two:
                    attended(b2)

            rounds(dve, step, 3, own, nb)

        @block.gpsimd
        def _(pool):
            def step(r, par):
                if alive(r, nb):
                    norm.take_root(pool, r)

            rounds(pool, step, 3, own_x[2], nb)




def first_heads(k, res):
    nc, W, bank = k.nc, k.W, k.bank
    with ExitStack() as ctx:
        norm = Norm(k, ctx, "f_")
        ready, read, own_dve = k.sem("f_ready"), k.sem("f_read"), k.sem("f_own_dve")
        block = ctx.enter_context(nc.Block())

        @block.vector
        def _(dve):
            norm.clear(dve, Tally(own_dve))
            for b in range(HE):
                norm.start(dve, b)
                norm.apply(dve, b)
                dve.wait_ge(ready, b + 1)
                nc.vector.tensor_copy(res[:, :, b * DH2:(b + 1) * DH2],
                                      bank[0:TP, 1, 0:NT * DH2].rearrange("p (t d) -> p t d", t=NT)).then_inc(read, 1)

        @block.gpsimd
        def _(pool):
            for b in range(HE):
                norm.take_root(pool, b)

        @block.tensor
        def _(pe):
            for b in range(HE):
                norm.turn(pe, b)
                pe.wait_ge(norm.kept, b + 1)
                wait(pe, read, b)
                for it in range(NT):
                    last = nc.tensor.matmul(bank[0:TP, 1, it * DH2:(it + 1) * DH2],
                                            norm.xT[:, b % 2, it * TP:(it + 1) * TP],
                                            W("w_sx")[:, b * DH2:(b + 1) * DH2], start=True, stop=True)
                last.then_inc(ready, 1)

        @block.scalar
        def _(act):
            for b in range(HE):
                norm.keep(act, b, b % 2, [(ready, b - 1)])


def query_experts(k, res, qk_dram, out):
    nc, nb, F, B, W, bank = k.nc, k.nb, k.F, k.B, k.W, k.bank
    units = [(0, (h,), 3 * TP) for h in range(HE)] + [(1, (0, 1), 2 * TP), (1, (2, 3), 2 * TP), (2, (0, 1, 2, 3), TP)]
    UE = len(units)
    LAG = 4
    NU = EE * UE
    NP = 3
    q_parts, k_parts = (0, 0, 1, 0, 1, 2), (0, 1, 0, 2, 1, 0)
    RS = len(q_parts) * DH2
    with ExitStack() as ctx:
        sb = lambda name, shape, dt=F32: ctx.enter_context(nc.sbuf_tensor("qe_" + name, shape, dt))
        sem = lambda n: k.sem("q_" + n)
        norm = Norm(k, ctx, "qn_", 1)
        WH = sb("WH", [96, NP + 1, 128])
        parts = sb("parts", [128, 3, NP, S], BF16)
        zeros = sb("zeros", [128, S])
        rest = sb("rest", [128, NP, S])
        Q, K = sb("Q", [RS + 1, 3, QE, S], BF16), sb("K", [RS + 1, 3, HE, S], BF16)
        v_aug, nz = sb("v_aug", [TP, 3, NT, 128]), sb("nz", [128, 3, S])
        top, neg, maxT = sb("top", [TP, NT, QE]), sb("neg", [TP, NT, QE], BF16), sb("maxT", [QE, S], BF16)
        E, cT = sb("E", [TP, 4, 512]), sb("cT", [128, EE, S])
        FW = HE * VS + QE
        tok = sb("tok", [TP, NT * EE, FW])
        gsel = sb("gsel", [128, EE, FW])
        rs, gp, gl = sb("rs", [TP, NT * EE, HE]), sb("gp", [TP, NT * EE, QE]), sb("gl", [TP, NT, QE])
        gtop, gex, gsum = sb("gtop", [TP, NT * HE]), sb("gex", [TP, NT * HE, EE]), sb("gsum", [TP, NT * HE])
        wt, wc = sb("wt", [TP, NT, EE, HE]), sb("wc", [TP, NT * EE, D])
        y, sq, mean, var = sb("y", [TP, NT * HE, DH2]), sb("sq", [TP, NT * HE, DH2]), sb("mean", [TP, NT * HE]), sb("var", [TP, NT * HE])
        root = sb("root", [TP, NT * HE])
        fx, fxT = sb("fx", [TP, NT, 128]), sb("fxT", [96, S])
        r1, h1T, fo, foT = sb("r1", [D, S]), sb("h1T", [96, S]), sb("fo", [TP, NT, 128]), sb("foT", [D, S])
        fl, fs = sb("fl", [TP, NT * HE]), sb("fs", [TP, NT])
        hout = sb("hout", [TP, 3, NT * D])
        gamma, beta = sb("gamma", [TP, 2, NT * HE, DH2]), sb("beta", [TP, 2, NT * HE, DH2])
        gb = sb("gb", [TP, NT, QE])

        folded, set_up, p_ready, nz_ready, nz_done, v_kept = map(sem, ("folded", "set_up", "p", "nz", "nz_done", "v_kept"))
        hi_done, rest_ready, parts_done, parts_stored, stacked = map(sem, ("hi", "rest", "parts", "parts_stored", "stacked"))
        m_ready, m_read, neg_ready, neg_turned, maxT_kept = map(sem, ("m", "m_read", "neg", "neg_turned", "maxT"))
        max_stacked = sem("max_stacked")
        e_ready, e_done, v_done, c_kept = map(sem, ("e", "e_done", "v_done", "c_kept"))
        sel_ready, sel_read, g_ready, gex_done, sq_ready, sq_done, vs_ready, root_done = map(
            sem, ("sel", "sel_read", "g", "gex", "c", "sq", "vs", "root"))
        fx_ready, fx_turned, fxT_kept, h1_ready, r1_done, h1T_ready, h2_ready = map(
            sem, ("fx", "fx_turned", "fxT", "h1", "r1", "h1T", "h2"))
        fo_ready, fo_turned, foT_kept, fl_ready, fs_ready, fex_done, h_ready, stored = map(
            sem, ("fo", "fo_turned", "foT", "fl", "fs", "fex", "h", "stored"))
        own_dve, own_pool = sem("own_dve"), sem("own_pool")
        own_x = [Tally(sem("own" + n)) for n in ("pe", "act", "sp")]
        block = ctx.enter_context(nc.Block())
        steps = {i * (NU + LAG) // 30: i for i in range(30)}

        def step_behind(n):
            return steps.get(n)

        @block.sync
        def _(sp):
            rows_of = qk_dram.rearrange("(a d) p i s -> p d a i s", d=DH2)
            keys_of = qk_dram.rearrange("(h a d) p i s -> a p i d h s", a=2, d=DH2)

            def stack(b, par):
                wait(sp, e_ready, (b - 2) * NU)
                wait(sp, stacked, b * 32 * len(q_parts))
                sp.wait_ge(parts_done, (b + 1) * NP)
                sp.dma_start(qk_dram, parts[:]).then_inc(parts_stored, 16)
                sp.wait_ge(parts_stored, (b + 1) * 16)
                for g, (qp, kp) in enumerate(zip(q_parts, k_parts)):
                    rows = slice(g * DH2, (g + 1) * DH2)
                    sp.dma_start(Q[rows, par].rearrange("d (a i) s -> d a i s", i=2), rows_of[qp, :, :, 0:2]
                                 ).then_inc(stacked, 16)
                    sp.dma_start(K[rows, par], keys_of[0, kp, 2]).then_inc(stacked, 16)

            def step(r, par):
                b = r - 3
                if alive(r, nb):
                    stack(r, par)
                if alive(b, nb):
                    sp.wait_ge(h_ready, (b + 1) * 16)
                    wait(sp, stored, b * 16)
                    sp.dma_start(out[bass.ds(b, 1)].rearrange("o (c p) f -> p (o c) f", p=TP),
                                 hout[:, par, :].rearrange("p (c f) -> p c f", c=NT)).then_inc(stored, 16)

            rounds(sp, step, 3, own_x[2], nb, 3)
            sp.wait_ge(stored, nb * 16)

        @block.tensor
        def _(pe):
            for e in range(NP + 1):
                last = nc.tensor.matmul(bank[0:D + 1, 4, e * 128:(e + 1) * 128], W("w_sxT"),
                                        W("w_heads")[:, e, :], start=True, stop=True)
            last.then_inc(folded, 1)
            pe.wait_ge(set_up, 1)

            def project(b, i):
                x = norm.xT[:, 0, :]
                if i == 0:
                    pe.wait_ge(norm.kept, b + 1)
                elif i <= NP:
                    pe.wait_ge(rest_ready, b * NP + i)
                if i < NP:
                    nc.tensor.matmul(bank[:, 1, 0:S], WH[:, i, :], x, start=True, stop=True).then_inc(p_ready, 1)
                elif i == NP:
                    for it in range(NT):
                        last = nc.tensor.matmul(bank[0:TP, 1, it * 128:(it + 1) * 128], x[:, it * TP:(it + 1) * TP],
                                                WH[:, NP, :], start=True, stop=True)
                    last.then_inc(p_ready, 1)
                else:
                    pe.wait_ge(v_kept, b + 1)
                    nc.tensor.matmul(bank[:, 1, 0:S], W("w_sx_wide"), x, start=True, stop=True).then_inc(nz_ready, 1)

            def mask(out, heads, cols, at, name):
                out = out[:, 0:len(heads) * cols].rearrange("p (i c) -> p i c", c=cols)[:, :, at:at + TP]
                rhs = B(name).rearrange("p (o c) -> p o c", o=1).to_broadcast((TP, len(heads), TP))
                return nc.tensor.matmul(out, B("ident_b")[0:TP, 0:TP], rhs, start=False, stop=True, skip_group_check=True)

            def scores_for_max(b, par, n):
                e, u = divmod(n, UE)
                back, heads, cols = units[u]
                it = NT - 1 - back
                out = bank[0:TP, 6 + n % 2, :]
                wait(pe, m_read, b * NU + n - 1)
                for i, h in enumerate(heads):
                    nc.tensor.matmul(out[:, i * cols:(i + 1) * cols], Q[0:RS, par, h * EE + e, it * TP:(it + 1) * TP],
                                     K[0:RS, par, h, 0:cols], start=i == 0, stop=False, skip_group_check=True)
                mask(out, heads, cols, cols - TP, "m_low_q").then_inc(m_ready, 1)

            def scores_for_exp(b, par, n):
                e, u = divmod(n, UE)
                jt, heads, cols = units[u]
                out = bank[0:TP, 4 + n % 2, :]
                if n == 0:
                    pe.wait_ge(max_stacked, (b + 1) * 16)
                wait(pe, e_done, b * NU + n - 1)
                for i, h in enumerate(heads):
                    nc.tensor.matmul(out[:, i * cols:(i + 1) * cols], K[:, par, h, jt * TP:(jt + 1) * TP],
                                     Q[:, par, h * EE + e, jt * TP:S], start=i == 0, stop=False, skip_group_check=True)
                mask(out, heads, cols, 0, "m_low_k").then_inc(e_ready, 1)

            def weigh_values(b, par, n):
                e, u = divmod(n, UE)
                jt, heads, cols = units[u]
                pe.wait_ge(e_done, b * NU + n + 1)
                if u == 0:
                    wait(pe, c_kept, b * EE + e - 1)
                for i, h in enumerate(heads):
                    last = nc.tensor.matmul(bank[32 * h:32 * h + 32, 2 - 2 * (e % 2), jt * TP:S],
                                            v_aug[:, par, jt, 32 * h:32 * h + 32], E[:, n % 4, i * cols:(i + 1) * cols],
                                            start=jt == 0, stop=jt == NT - 1, skip_group_check=True)
                last.then_inc(v_done, 1)

            def turn_max(b):
                pe.wait_ge(neg_ready, b + 1)
                pe.wait_ge(nz_done, min(b + 2, nb) if isinstance(b, int) else b + 2)
                for it in range(NT):
                    last = nc.tensor.matmul(bank[0:QE, 1, it * TP:(it + 1) * TP], neg[:, it, :],
                                            B("ident_b")[0:TP, 0:TP], start=True, stop=True)
                last.then_inc(neg_turned, 1)

            def tail(b, n):
                if n < NT:
                    if n == 0:
                        pe.wait_ge(c_kept, (b + 1) * EE)
                        wait(pe, fs_ready, b)
                    wait(pe, sel_read, b * NT + n)
                    for e in range(EE):
                        last = nc.tensor.matmul(bank[0:TP, 3, e * FW:(e + 1) * FW], cT[:, e, n * TP:(n + 1) * TP],
                                                gsel[:, e, :], start=True, stop=True)
                    last.then_inc(sel_ready, 1)
                if n == 14:
                    pe.wait_ge(fx_ready, b + 1)
                    for it in range(NT):
                        last = nc.tensor.transpose(bank[:, 3, it * TP:(it + 1) * TP], fx[:, it, :], F("ident")[0:TP, 0:TP])
                    last.then_inc(fx_turned, 1)
                if n == 15:
                    pe.wait_ge(fxT_kept, b + 1)
                    nc.tensor.matmul(bank[0:D, 3, 0:S], W("fc1"), fxT[:], start=True, stop=True).then_inc(h1_ready, 1)
                if n == 17:
                    pe.wait_ge(h1T_ready, b + 1)
                    for it in range(NT):
                        last = nc.tensor.matmul(bank[0:TP, 3, it * D:(it + 1) * D], h1T[:, it * TP:(it + 1) * TP],
                                                W("fc2"), start=True, stop=True)
                    last.then_inc(h2_ready, 1)
                if n == 25:
                    pe.wait_ge(fo_ready, b + 1)
                    for it in range(NT):
                        last = nc.tensor.transpose(bank[:, 3, it * TP:(it + 1) * TP], fo[:, it, :], F("ident")[0:TP, 0:TP])
                    last.then_inc(fo_turned, 1)
                if n == 26:
                    pe.wait_ge(foT_kept, b + 1)
                    for it in range(NT):
                        last = nc.tensor.matmul(bank[0:TP, 3, it * HE:(it + 1) * HE], foT[:, it * TP:(it + 1) * TP],
                                                W("fgate"), start=True, stop=True)
                    last.then_inc(fl_ready, 1)

            def step(r, par):
                b1, b2, b3 = r - 1, r - 2, r - 3
                if alive(b1, nb):
                    pe.wait_ge(stacked, (b1 + 1) * 32 * len(q_parts))
                for n in range(NU + LAG):
                    if alive(b1, nb) and n < NU:
                        scores_for_max(b1, (par - 1) % 3, n)
                    if alive(b2, nb):
                        if n == 1:
                            turn_max(b2)
                        if n >= LAG:
                            scores_for_exp(b2, (par - 2) % 3, n - LAG)
                        if n >= LAG + 2:
                            weigh_values(b2, (par - 2) % 3, n - LAG - 2)
                    m = step_behind(n)
                    if alive(b3, nb) and m is not None:
                        tail(b3, m)
                    if alive(r, nb):
                        if m == 3:
                            wait(pe, nz_done, r)
                            wait(pe, maxT_kept, r - 1)
                            norm.turn(pe, r)
                        if m in (5, 9, 13, 17, 21):
                            project(r, m // 4 - 1)
                if alive(b2, nb):
                    weigh_values(b2, (par - 2) % 3, NU - 2)
                    weigh_values(b2, (par - 2) % 3, NU - 1)

            rounds(pe, step, 3, own_x[0], nb, 3)

        @block.scalar
        def _(act):
            def first_part(b, i):
                act.wait_ge(p_ready, b * (NP + 1) + i + 1)
                if i == 0:
                    wait(act, parts_stored, b * 16)
                nc.scalar.copy(parts[:, 0, i, :], bank[:, 1, 0:S]).then_inc(hi_done, 1)

            def keep_values(b, par):
                act.wait_ge(p_ready, (b + 1) * (NP + 1))
                wait(act, v_done, (b - 2) * NU)
                nc.scalar.copy(flat3(v_aug[:, par]), bank[0:TP, 1, 0:NT * 128]).then_inc(v_kept, 1)

            def exponentials(b, n):
                _, heads, cols = units[n % UE]
                act.wait_ge(e_ready, b * NU + n + 1)
                wait(act, v_done, b * NU + n - 3)
                used = slice(0, len(heads) * cols)
                nc.scalar.activation(E[:, n % 4, used], bank[0:TP, 4 + n % 2, used], ACT.Exp).then_inc(e_done, 1)

            def tail(b, n):
                if n < NT:
                    act.wait_ge(sel_ready, b * NT + n + 1)
                    if n == 0:
                        wait(act, sq_ready, 2 * b)
                    nc.scalar.copy(tok[:, n * EE:(n + 1) * EE, :],
                                   bank[0:TP, 3, 0:EE * FW].rearrange("p (e f) -> p e f", e=EE)).then_inc(sel_read, 1)
                if n == 4:
                    act.wait_ge(g_ready, b + 1)
                    nc.scalar.activation(flat3(gex[:]), flat3(gl[:]), ACT.Exp).then_inc(gex_done, 1)
                if n in (8, 19):
                    act.wait_ge(sq_ready, 2 * b + (n == 19) + 1)
                    nc.scalar.activation(sq[:], y[:], ACT.Square).then_inc(sq_done, 1)
                if n == 14:
                    act.wait_ge(fx_turned, b + 1)
                    wait(act, h1T_ready, b)
                    nc.scalar.copy(fxT[0:D, :], bank[0:D, 3, 0:S]).then_inc(fxT_kept, 1)
                if n == 15:
                    act.wait_ge(h1_ready, b + 1)
                    nc.scalar.activation(r1[:], bank[0:D, 3, 0:S], ACT.Relu).then_inc(r1_done, 1)
                if n == 25:
                    act.wait_ge(fo_turned, b + 1)
                    wait(act, fl_ready, b)
                    nc.scalar.copy(foT[:], bank[0:D, 3, 0:S]).then_inc(foT_kept, 1)
                if n == 27:
                    act.wait_ge(fs_ready, b + 1)
                    nc.scalar.activation(fl[:], fl[:], ACT.Exp).then_inc(fex_done, 1)

            def step(r, par):
                b1, b2, b3 = r - 1, r - 2, r - 3
                for n in range(NU + LAG):
                    if alive(b2, nb):
                        if n == 1:
                            act.wait_ge(neg_turned, b2 + 1)
                            wait(act, max_stacked, b2 * 16)
                            nc.scalar.copy(maxT[:], bank[0:QE, 1, 0:S]).then_inc(maxT_kept, 1)
                            act.wait_ge(maxT_kept, b2 + 1)
                            act.dma_start(Q[RS:RS + 1, (par - 2) % 3].rearrange("o n s -> o (n s)"), maxT[:]
                                          ).then_inc(max_stacked, 16)
                        if n >= LAG:
                            exponentials(b2, n - LAG)
                    m = step_behind(n)
                    if alive(b3, nb) and m is not None:
                        tail(b3, m)
                    if alive(r, nb):
                        if m == 3:
                            norm.keep(act, r, 0, [(nz_ready, r)])
                        if m in (5, 9, 13):
                            first_part(r, m // 4 - 1)
                        if m == 17:
                            keep_values(r, par)

            rounds(act, step, 3, own_x[1], nb, 3)

        @block.vector
        def _(dve):
            own = Tally(own_dve)
            norm.clear(dve, own)
            for v in (fx, fo, zeros):
                own.up(nc.vector.memset(v[:], 0.0))
            own.up(nc.vector.memset(K[RS:RS + 1], 1.0))
            own.up(nc.vector.memset(WH[:], 0.0))
            for v in (fxT, h1T):
                own.link(dve, nc.vector.memset(v[:], 0.0))
                own.up(nc.vector.memset(v[D:D + 1], 1.0))
            for i, (g, b_) in enumerate((("ln_g", "ln_b"), ("fnorm_g", "fnorm_b"))):
                for dst, src in ((gamma, g), (beta, b_)):
                    own.up(nc.vector.tensor_copy(dst[:, i], W(src).rearrange("p (o d) -> p o d", o=1)
                                                 .to_broadcast((TP, NT * HE, DH2))))
            own.up(nc.vector.tensor_copy(gb[:], W("gate_b2").rearrange("p (o d) -> p o d", o=1).to_broadcast((TP, NT, QE))))
            own.up(nc.vector.tensor_copy(gsel[:, :, 0:HE * VS], F("sel").rearrange("p (o d) -> p o d", o=1)
                                         .to_broadcast((128, EE, HE * VS))))
            own.up(nc.vector.tensor_copy(gsel[:, :, HE * VS:], W("gate_w2")))
            dve.wait_ge(folded, 1)
            own.up(nc.vector.tensor_scalar(flat3(WH[0:D + 1, 0:2, :]), bank[0:D + 1, 4, 0:256], float(DH2) ** 0.5, None, ALU.mult))
            own.link(dve, nc.vector.tensor_copy(flat3(WH[0:D + 1, 2:, :]), bank[0:D + 1, 4, 256:512]))
            own.link(dve, nc.vector.memset(WH[D:D + 1, NP, :].rearrange("p (n d) -> p n d", n=HE)[:, :, DH2:VS], 1.0))
            nc.vector.memset(norm.carry[:], 0.0).then_inc(set_up, 1)

            def maxima(b, n):
                e, u = divmod(n, UE)
                back, heads, cols = units[u]
                it = NT - 1 - back
                if n == 0:
                    wait(dve, neg_ready, b)
                dve.wait_ge(m_ready, b * NU + n + 1)
                src = bank[0:TP, 6 + n % 2, 0:len(heads) * cols].rearrange("p (i c) -> p i c", c=cols)
                dst = top[:, it, :].rearrange("p (h e) -> p h e", h=HE)[:, heads[0]:heads[-1] + 1, e]
                nc.vector.tensor_reduce(dst, src, AX, ALU.max).then_inc(m_read, 1)

            def negate_max(b):
                dve.wait_ge(m_read, (b + 1) * NU)
                wait(dve, neg_turned, b)
                nc.vector.tensor_scalar(neg[:], top[:], -1.0, None, ALU.mult).then_inc(neg_ready, 1)

            def normalise_start():
                own.link(dve, nc.vector.tensor_reduce(mean[:], y[:], AX, ALU.add))
                nc.vector.scalar_tensor_tensor(y[:], mean[:].rearrange("p (a o) -> p a o", o=1)
                                               .to_broadcast((TP, NT * HE, DH2)), -1.0 / DH2, y[:],
                                               ALU.mult, ALU.add).then_inc(sq_ready, 1)

            def normalise_sum(b, i):
                dve.wait_ge(sq_done, 2 * b + i + 1)
                nc.vector.tensor_reduce(var[:], sq[:], AX, ALU.add).then_inc(vs_ready, 1)

            def normalise_end(b, i, dst, done):
                dve.wait_ge(root_done, 2 * b + i + 1)
                own.link(dve, nc.vector.tensor_tensor(y[:], y[:], root[:].rearrange("p (a o) -> p a o", o=1)
                                                      .to_broadcast((TP, NT * HE, DH2)), ALU.mult))
                own.link(dve, nc.vector.tensor_tensor(y[:], y[:], gamma[:, i], ALU.mult))
                nc.vector.tensor_tensor(dst, by_tile(y[:]), by_tile(beta[:, i]), ALU.add).then_inc(done, 1)

            by_tile = lambda v: v.rearrange("p (t h) d -> p t (h d)", t=NT)

            def tail(b, par, n):
                if n == 3:
                    dve.wait_ge(sel_read, (b + 1) * NT)
                    sums = tok[:, :, 0:HE * VS].rearrange("p a (h d) -> p a h d", h=HE)[:, :, :, DH2]
                    own.link(dve, nc.vector.reciprocal(rs[:], sums))
                    own.up(nc.vector.tensor_tensor(
                        gp[:].rearrange("p a (h e) -> p a h e", h=HE),
                        tok[:, :, HE * VS:].rearrange("p a (h e) -> p a h e", h=HE),
                        rs[:].rearrange("p a (h o) -> p a h o", o=1).to_broadcast((TP, NT * EE, HE, EE)), ALU.mult))
                if n == 4:
                    own.wait(dve)
                    own.link(dve, nc.vector.tensor_reduce(gl[:], gp[:].rearrange("p (t e) f -> p t f e", t=NT), AX, ALU.add))
                    own.link(dve, nc.vector.tensor_tensor(gl[:], gl[:], gb[:], ALU.add))
                    heads = gl[:].rearrange("p t (h e) -> p (t h) e", h=HE)
                    own.link(dve, nc.vector.tensor_reduce(gtop[:], heads, AX, ALU.max))
                    nc.vector.tensor_tensor(heads, heads, gtop[:].rearrange("p (a o) -> p a o", o=1)
                                            .to_broadcast((TP, NT * HE, EE)), ALU.subtract).then_inc(g_ready, 1)
                if n == 5:
                    dve.wait_ge(gex_done, b + 1)
                    own.link(dve, nc.vector.tensor_reduce(gsum[:], gex[:], AX, ALU.add))
                    own.link(dve, nc.vector.reciprocal(gsum[:], gsum[:]))
                    own.link(dve, nc.vector.tensor_tensor(gex[:], gex[:], gsum[:].rearrange("p (a o) -> p a o", o=1)
                                                          .to_broadcast((TP, NT * HE, EE)), ALU.mult))
                    own.up(nc.vector.tensor_tensor(wt[:], gex[:].rearrange("p (t h) e -> p t e h", t=NT),
                                                          rs[:].rearrange("p (t e) h -> p t e h", t=NT), ALU.mult))
                if n == 6:
                    own.wait(dve)
                    own.up(nc.vector.tensor_tensor(
                        wc[:].rearrange("p a (h d) -> p a h d", h=HE),
                        tok[:, :, 0:HE * VS].rearrange("p a (h d) -> p a h d", h=HE)[:, :, :, 0:DH2],
                        wt[:].rearrange("p t e h -> p (t e) h").rearrange("p a (h o) -> p a h o", o=1)
                        .to_broadcast((TP, NT * EE, HE, DH2)), ALU.mult))
                if n == 7:
                    own.wait(dve)
                    own.link(dve, nc.vector.tensor_reduce(by_tile(y[:]), wc[:].rearrange("p (t e) f -> p t f e", t=NT),
                                                          AX, ALU.add))
                    own.up(nc.vector.tensor_tensor(by_tile(y[:]), by_tile(y[:]), res[:], ALU.add))
                if n == 8:
                    own.wait(dve)
                    normalise_start()
                if n == 9:
                    normalise_sum(b, 0)
                if n == 12:
                    normalise_end(b, 0, fx[:, :, 0:D], fx_ready)
                if n == 16:
                    dve.wait_ge(r1_done, b + 1)
                    wait(dve, h2_ready, b)
                    nc.vector.scalar_tensor_tensor(h1T[0:D, :], fxT[0:D, :], 0.0, r1[:], ALU.not_equal,
                                                   ALU.mult).then_inc(h1T_ready, 1)
                if n == 18:
                    dve.wait_ge(h2_ready, b + 1)
                    h2 = bank[0:TP, 3, 0:NT * D].rearrange("p (t f) -> p t f", t=NT)
                    own.link(dve, nc.vector.scalar_tensor_tensor(by_tile(y[:]), fx[:, :, 0:D], 0.0, h2, ALU.not_equal, ALU.mult))
                    own.up(nc.vector.tensor_tensor(by_tile(y[:]), by_tile(y[:]), fx[:, :, 0:D], ALU.add))
                if n == 19:
                    own.wait(dve)
                    normalise_start()
                if n == 20:
                    normalise_sum(b, 1)
                if n == 23:
                    normalise_end(b, 1, fo[:, :, 0:D], fo_ready)
                if n == 27:
                    dve.wait_ge(fl_ready, b + 1)
                    lg = bank[0:TP, 3, 0:NT * HE].rearrange("p (t h) -> p t h", t=NT)
                    own.link(dve, nc.vector.tensor_reduce(fs[:], lg, AX, ALU.max))
                    nc.vector.tensor_tensor(fl[:].rearrange("p (t h) -> p t h", t=NT), lg,
                                            fs[:].rearrange("p (t o) -> p t o", o=1).to_broadcast((TP, NT, HE)),
                                            ALU.subtract).then_inc(fs_ready, 1)
                if n == 28:
                    dve.wait_ge(fex_done, b + 1)
                    l3 = fl[:].rearrange("p (t h) -> p t h", t=NT)
                    own.link(dve, nc.vector.tensor_reduce(fs[:], l3, AX, ALU.add))
                    own.link(dve, nc.vector.reciprocal(fs[:], fs[:]))
                    own.up(nc.vector.tensor_tensor(l3, l3, fs[:].rearrange("p (t o) -> p t o", o=1)
                                                          .to_broadcast((TP, NT, HE)), ALU.mult))
                if n == 29:
                    own.wait(dve)
                    own.link(dve, nc.vector.tensor_tensor(
                        sq[:].rearrange("p (t h) d -> p t h d", t=NT), y_of(fo), fl[:].rearrange("p (t h o) -> p t h o", t=NT, o=1)
                        .to_broadcast((TP, NT, HE, DH2)), ALU.mult))
                    wait(dve, stored, (b - 1) * 16)
                    nc.vector.tensor_tensor(hout[:, par, :], sq[:].rearrange("p a d -> p (a d)"), one(k.h, b),
                                            ALU.add).then_inc(h_ready, 16)

            def y_of(v):
                return v[:, :, 0:D].rearrange("p t (h d) -> p t h d", h=HE)

            def leave_rest(b, i):
                dve.wait_ge(hi_done, b * NP + i + 1)
                wait(dve, parts_done, (b - 1) * NP + i + 1)
                nc.vector.tensor_tensor(rest[:, i, :], bank[:, 1, 0:S], parts[:, 0, i, :],
                                        ALU.subtract).then_inc(rest_ready, 1)

            def step(r, par):
                b1, b2, b3 = r - 1, r - 2, r - 3
                if alive(r, nb):
                    norm.start(dve, r)
                for n in range(NU + LAG):
                    if alive(b1, nb) and n < NU:
                        maxima(b1, n)
                    if alive(b2, nb) and n > UE and n % UE == LAG + 2:
                        keep_context(b2, (par - 2) % 3, n // UE - 1)
                    m = step_behind(n)
                    if alive(b3, nb) and m is not None:
                        tail(b3, par, m)
                    if alive(r, nb):
                        if m == 1:
                            norm.apply(dve, r)
                        if m in (6, 10, 14):
                            leave_rest(r, m // 4 - 1)
                        if m == 22:
                            dve.wait_ge(nz_ready, r + 1)
                            nc.vector.tensor_scalar(nz[:, par, :], bank[:, 1, 0:S], 0.0, None,
                                                    ALU.not_equal).then_inc(nz_done, 1)
                if alive(b2, nb):
                    keep_context(b2, (par - 2) % 3, EE - 1)
                if alive(b1, nb):
                    negate_max(b1)

            def keep_context(b, par, e):
                dve.wait_ge(v_done, b * NU + UE * (e + 1))
                wait(dve, sel_ready, b * NT)
                nc.vector.tensor_tensor(cT[:, e, :], bank[:, 2 - 2 * (e % 2), 0:S], nz[:, par, :], ALU.mult).then_inc(c_kept, 1)

            rounds(dve, step, 3, own, nb, 3)

        @block.gpsimd
        def _(pool):
            own = Tally(own_pool)

            def other_parts(b, i):
                pool.wait_ge(rest_ready, b * NP + i + 1)
                own.link(pool, nc.gpsimd.tensor_tensor(parts[:, 1, i, :], rest[:, i, :], zeros[:], ALU.add))
                nc.gpsimd.tensor_tensor(parts[:, 2, i, :], rest[:, i, :], parts[:, 1, i, :],
                                        ALU.subtract).then_inc(parts_done, 1)

            def step(r, par):
                b = r - 3
                if alive(r, nb):
                    norm.take_root(pool, r)
                    other_parts(r, 0)
                if alive(b, nb):
                    take_root(b, 0)
                if alive(r, nb):
                    other_parts(r, 1)
                    other_parts(r, 2)
                if alive(b, nb):
                    take_root(b, 1)

            def take_root(b, i):
                pool.wait_ge(vs_ready, 2 * b + i + 1)
                own.link(pool, nc.gpsimd.tensor_tensor(root[:], var[:], F("per_width"), ALU.mult))
                own.link(pool, nc.gpsimd.tensor_tensor(root[:], root[:], F("eps2"), ALU.add))
                nc.gpsimd.tensor_tensor(root[:], root[:], k.half[:], ALU.pow).then_inc(root_done, 1)

            rounds(pool, step, 3, own, nb, 3)


def flat3(ap):
    return ap.rearrange("p a b -> p (a b)")


def one(h, b):
    return h[:, bass.ds(b, 1), :].rearrange("p o f -> p (o f)")


def tower(nc, nb, x, fpack, bpack, wpack, packs, s_dram, qk_dram, out):
    with ExitStack() as ctx:
        k = Core(nc, ctx, packs, nb)
        with nc.cleanup_on_exit(), ExitStack() as c:
            t = SelectAttend(k, c)
            score_tokens(k, x, fpack, bpack, wpack, s_dram, t)
            select_attend(k, t, x, s_dram)
        with nc.cleanup_on_exit():
            experts(k)
        with nc.cleanup_on_exit():
            slices(k)
        res = k.sb("first_heads", [TP, NT, D])
        with nc.cleanup_on_exit():
            first_heads(k, res)
            query_experts(k, res, qk_dram, out)


def kernel(**inputs):
    import concourse.bacc as bacc
    from concourse.bass_utils import run_bass_kernel_spmd

    weights = {n: np.asarray(v) for n, v in inputs.items() if n != "x"}
    x = np.ascontiguousarray(inputs["x"])
    f, b = shape_constants()
    w = weight_layout(weights)
    arrays = {"x": x, "fconst_in": f.build(np.float32),
              "bconst_in": b.build(mybir.dt.np(BF16)), "weights_in": w.build(np.float32)}
    nc = bacc.Bacc("TRN2", target_bir_lowering=False, num_devices=1)
    args = [nc.dram_tensor(n, a.shape, mybir.dt.from_np(a.dtype), kind="ExternalInput").ap()
            for n, a in arrays.items()]
    nb = x.shape[0]
    out = nc.dram_tensor("out", (nb, S, D), F32, kind="ExternalOutput").ap()
    qk_dram = nc.dram_tensor("query_key_parts", (128, 3, 3, S), BF16).ap()
    s_dram = nc.dram_tensor("scores", (nb * CI, TP), F32).ap()
    tower(nc, nb, *args, (f, b, w), s_dram, qk_dram, out)
    r = run_bass_kernel_spmd(nc, [arrays], core_ids=[0])
    return r.results[0]["out"]
```
